# Optimizing a Trainium2 kernel written in Bass

```python
import numpy as np
import jax
import jax.numpy as jnp

def _softmax(x, axis=-1):
    return jax.nn.softmax(x, axis=axis)

def _gelu(x):
    return jax.nn.gelu(x, approximate=True)

def _silu(x):
    return jax.nn.silu(x)

def _sigmoid(x):
    return jax.nn.sigmoid(x)

def _layernorm(x, axis=-1, eps=1e-05):
    m = jnp.mean(x, axis=axis, keepdims=True)
    v = jnp.var(x, axis=axis, keepdims=True)
    return (x - m) / jnp.sqrt(v + eps)

def _scatter_add(tgt, idx, src, axis=0):
    return tgt.at[idx].add(src)

def _segment_sum(src, seg, n):
    return jax.ops.segment_sum(src, seg, n)
kernel_name = 'mk_prb_d2_jaxref_r8_d0c187'

def setup_inputs(seed: int=0):
    np.random.seed(seed)
    _w = jnp.asarray

    def _L0_attn_setup():
        import math
        import jax, jax.numpy as jnp
        import numpy as np
        B, T, D, H = (2, 1024, 128, 1)
        DH = D // H

        def _layernorm(x, g, b):
            m = x.mean(-1, keepdims=True)
            v = ((x - m) ** 2).mean(-1, keepdims=True)
            return (x - m) * jax.lax.rsqrt(v + 1e-05) * g + b

        def _l2norm(x):
            n = jnp.sqrt(jnp.sum(x * x, axis=-1, keepdims=True))
            return x / jnp.maximum(n, 1e-12)

        def _rope(x, times):
            half = x.shape[-1] // 2
            freqs = jnp.exp(-jnp.arange(half, dtype=x.dtype) * (math.log(10000.0) / half))
            th = times[:, None] * freqs[None, :]
            c = jnp.cos(th)[None, :, None, :]
            s = jnp.sin(th)[None, :, None, :]
            xr = x.reshape(x.shape[:-1] + (half, 2))
            x1, x2 = (xr[..., 0], xr[..., 1])
            out = jnp.stack([x1 * c - x2 * s, x1 * s + x2 * c], axis=-1)
            return out.reshape(x.shape)

        def _forward(x, Wq, Wk, Wv, gate_W, gate_b, p_W, p_b, clock_W, clock_b, out_W, out_b, ln1_g, ln1_b, ln2_g, ln2_b, mlp_W1, mlp_b1, mlp_W2, mlp_b2):
            Bc, Tc, Dc = x.shape
            residual = x
            xn = _layernorm(x, ln1_g, ln1_b)
            times = jnp.arange(Tc, dtype=x.dtype)
            q = _l2norm((xn @ Wq).reshape(Bc, Tc, H, DH))
            k = _l2norm((xn @ Wk).reshape(Bc, Tc, H, DH))
            v = (xn @ Wv).reshape(Bc, Tc, H, DH)
            clock = jax.nn.softplus(xn @ clock_W + clock_b).reshape(Bc, Tc, H, 1)
            q = _rope(q, times)
            k = _rope(k, times)
            gj = -jax.nn.softplus(xn @ gate_W + gate_b).reshape(Bc, Tc, H, DH)
            gj_cumprod = jnp.exp(jnp.clip(jnp.cumsum(gj, axis=1), -60.0, 50.0))
            q = q * gj_cumprod
            k = k / (gj_cumprod + 1e-08)
            p = (xn @ p_W + p_b).reshape(Bc, Tc, H, DH)
            p_max = jnp.max(p, axis=1, keepdims=True)
            p_exp = jnp.exp(p - p_max) * clock
            p_cum = jnp.cumsum(p_exp, axis=1)
            q = q / (p_cum + 1e-08)
            k = k * p_exp
            scale = 1.0 / math.sqrt(DH)
            scores = jnp.einsum('bqhd,bkhd->bhqk', q, k) * scale
            mask = jnp.tril(jnp.ones((Tc, Tc), dtype=bool))
            scores = jnp.where(mask[None, None], scores, jnp.finfo(scores.dtype).min)
            w = jax.nn.softmax(scores, axis=-1)
            out = jnp.einsum('bhqk,bkhd->bqhd', w, v).reshape(Bc, Tc, Dc)
            x2 = out @ out_W + out_b + residual
            h = _layernorm(x2, ln2_g, ln2_b)
            mlp = jax.nn.gelu(h @ mlp_W1 + mlp_b1, approximate=False) @ mlp_W2 + mlp_b2
            return x2 + mlp
        key = jax.random.key(seed)
        ks = jax.random.split(key, 11)
        s = 0.02
        f = lambda k, shp: jax.random.normal(k, shp, dtype=jnp.float32) * s
        return {'x': jax.random.normal(ks[0], (B, T, D), dtype=jnp.float32), 'Wq': f(ks[1], (D, D)), 'Wk': f(ks[2], (D, D)), 'Wv': f(ks[3], (D, D)), 'gate_W': f(ks[4], (D, D)), 'gate_b': jnp.zeros((D,), jnp.float32), 'p_W': f(ks[5], (D, D)), 'p_b': jnp.zeros((D,), jnp.float32), 'clock_W': f(ks[6], (D, H)), 'clock_b': jnp.zeros((H,), jnp.float32), 'out_W': f(ks[7], (D, D)), 'out_b': jnp.zeros((D,), jnp.float32), 'ln1_g': jnp.ones((D,), jnp.float32), 'ln1_b': jnp.zeros((D,), jnp.float32), 'ln2_g': jnp.ones((D,), jnp.float32), 'ln2_b': jnp.zeros((D,), jnp.float32), 'mlp_W1': f(ks[8], (D, 4 * D)), 'mlp_b1': jnp.zeros((4 * D,), jnp.float32), 'mlp_W2': f(ks[9], (4 * D, D)), 'mlp_b2': jnp.zeros((D,), jnp.float32)}
    _L0_attn_in = _L0_attn_setup()

    def _L0_ffn_setup():
        import jax, jax.numpy as jnp
        import numpy as np
        D_IN, D_HID = (128, 512)

        def _ternary(key, shape):
            return jax.random.randint(key, shape, -1, 2).astype(jnp.float32)

        def _tlin(x, w, s):
            return jnp.einsum('bsi,oi->bso', x, w) * s
        key = jax.random.key(seed)
        ks = jax.random.split(key, 12)
        inv = lambda fan: 1.0 / np.sqrt(fan).astype(np.float32)
        return {'x': jax.random.normal(ks[0], (4, 256, D_IN), dtype=jnp.float32), 'w1_w': _ternary(ks[1], (D_HID, D_IN)), 'w1_s': jax.random.uniform(ks[2], (D_HID,), dtype=jnp.float32) * inv(D_IN), 'w2_w': _ternary(ks[3], (D_HID, D_IN)), 'w2_s': jax.random.uniform(ks[4], (D_HID,), dtype=jnp.float32) * inv(D_IN), 'h1_w': _ternary(ks[5], (D_HID, D_HID)), 'h1_s': jax.random.uniform(ks[6], (D_HID,), dtype=jnp.float32) * inv(D_HID), 'h2_w': _ternary(ks[7], (D_HID, D_HID)), 'h2_s': jax.random.uniform(ks[8], (D_HID,), dtype=jnp.float32) * inv(D_HID), 'w3_w': _ternary(ks[9], (D_IN, D_HID)), 'w3_s': jax.random.uniform(ks[10], (D_IN,), dtype=jnp.float32) * inv(D_HID)}
    _L0_ffn_in = _L0_ffn_setup()

    def _L1_attn_setup():
        import jax, jax.numpy as jnp
        import numpy as np
        B, S, D, H = (4, 256, 128, 16)
        HD = D // H
        key = jax.random.key(seed)
        k0, k1, k2, k3, k4 = jax.random.split(key, 5)
        x = jax.random.normal(k0, (B, S, D), dtype=jnp.float32)
        conv_w = jax.random.normal(k1, (D, 1, 3, 3), dtype=jnp.float32) * 0.1
        pe_w = jax.random.normal(k2, (D, D), dtype=jnp.float32) * 0.02
        qkv_w = jax.random.normal(k3, (3 * D, D), dtype=jnp.float32) * 0.02
        out_w = jax.random.normal(k4, (D, D), dtype=jnp.float32) * 0.02
        return {'x': x, 'conv_w': conv_w, 'pe_w': pe_w, 'qkv_w': qkv_w, 'out_w': out_w}
    _L1_attn_in = _L1_attn_setup()

    def _L1_ffn_setup():
        import jax, jax.numpy as jnp
        import numpy as np
        B, S, D, H, F, E = (2, 128, 128, 16, 512, 8)
        HD = D // H
        EPS = 1e-06

        def _layernorm(x, g, b):
            m = jnp.mean(x, axis=-1, keepdims=True)
            v = jnp.var(x, axis=-1, keepdims=True)
            return (x - m) / jnp.sqrt(v + EPS) * g + b
        key = jax.random.key(seed)
        ks = jax.random.split(key, 10)
        sc = 0.02
        x = jax.random.normal(ks[0], (B, S, D), jnp.float32)
        Wq = jax.random.normal(ks[1], (D, D), jnp.float32) * sc
        Wk = jax.random.normal(ks[2], (D, D), jnp.float32) * sc
        Wv = jax.random.normal(ks[3], (D, D), jnp.float32) * sc
        Wo = jax.random.normal(ks[4], (D, D), jnp.float32) * sc
        bo = jnp.zeros((D,), jnp.float32)
        Wr = jax.random.normal(ks[5], (D, E), jnp.float32) * sc
        We1 = jax.random.normal(ks[6], (E, D, F), jnp.float32) * sc
        be1 = jnp.zeros((E, F), jnp.float32)
        We2 = jax.random.normal(ks[7], (E, F, D), jnp.float32) * sc
        be2 = jnp.zeros((E, D), jnp.float32)
        ln1_g = jnp.ones((D,), jnp.float32)
        ln1_b = jnp.zeros((D,), jnp.float32)
        ln2_g = jnp.ones((D,), jnp.float32)
        ln2_b = jnp.zeros((D,), jnp.float32)
        return {'x': x, 'Wq': Wq, 'Wk': Wk, 'Wv': Wv, 'Wo': Wo, 'bo': bo, 'Wr': Wr, 'We1': We1, 'be1': be1, 'We2': We2, 'be2': be2, 'ln1_g': ln1_g, 'ln1_b': ln1_b, 'ln2_g': ln2_g, 'ln2_b': ln2_b}
    _L1_ffn_in = _L1_ffn_setup()
    _d = {'L0_attn_x': _L0_attn_in['x'], 'L0_attn_Wq': _L0_attn_in['Wq'], 'L0_attn_Wk': _L0_attn_in['Wk'], 'L0_attn_Wv': _L0_attn_in['Wv'], 'L0_attn_gate_W': _L0_attn_in['gate_W'], 'L0_attn_gate_b': _L0_attn_in['gate_b'], 'L0_attn_p_W': _L0_attn_in['p_W'], 'L0_attn_p_b': _L0_attn_in['p_b'], 'L0_attn_clock_W': _L0_attn_in['clock_W'], 'L0_attn_clock_b': _L0_attn_in['clock_b'], 'L0_attn_out_W': _L0_attn_in['out_W'], 'L0_attn_out_b': _L0_attn_in['out_b'], 'L0_attn_ln1_g': _L0_attn_in['ln1_g'], 'L0_attn_ln1_b': _L0_attn_in['ln1_b'], 'L0_attn_ln2_g': _L0_attn_in['ln2_g'], 'L0_attn_ln2_b': _L0_attn_in['ln2_b'], 'L0_attn_mlp_W1': _L0_attn_in['mlp_W1'], 'L0_attn_mlp_b1': _L0_attn_in['mlp_b1'], 'L0_attn_mlp_W2': _L0_attn_in['mlp_W2'], 'L0_attn_mlp_b2': _L0_attn_in['mlp_b2'], 'L0_ffn_w1_w': _L0_ffn_in['w1_w'], 'L0_ffn_w1_s': _L0_ffn_in['w1_s'], 'L0_ffn_w2_w': _L0_ffn_in['w2_w'], 'L0_ffn_w2_s': _L0_ffn_in['w2_s'], 'L0_ffn_h1_w': _L0_ffn_in['h1_w'], 'L0_ffn_h1_s': _L0_ffn_in['h1_s'], 'L0_ffn_h2_w': _L0_ffn_in['h2_w'], 'L0_ffn_h2_s': _L0_ffn_in['h2_s'], 'L0_ffn_w3_w': _L0_ffn_in['w3_w'], 'L0_ffn_w3_s': _L0_ffn_in['w3_s'], 'L1_attn_conv_w': _L1_attn_in['conv_w'], 'L1_attn_pe_w': _L1_attn_in['pe_w'], 'L1_attn_qkv_w': _L1_attn_in['qkv_w'], 'L1_attn_out_w': _L1_attn_in['out_w'], 'L1_ffn_Wq': _L1_ffn_in['Wq'], 'L1_ffn_Wk': _L1_ffn_in['Wk'], 'L1_ffn_Wv': _L1_ffn_in['Wv'], 'L1_ffn_Wo': _L1_ffn_in['Wo'], 'L1_ffn_bo': _L1_ffn_in['bo'], 'L1_ffn_Wr': _L1_ffn_in['Wr'], 'L1_ffn_We1': _L1_ffn_in['We1'], 'L1_ffn_be1': _L1_ffn_in['be1'], 'L1_ffn_We2': _L1_ffn_in['We2'], 'L1_ffn_be2': _L1_ffn_in['be2'], 'L1_ffn_ln1_g': _L1_ffn_in['ln1_g'], 'L1_ffn_ln1_b': _L1_ffn_in['ln1_b'], 'L1_ffn_ln2_g': _L1_ffn_in['ln2_g'], 'L1_ffn_ln2_b': _L1_ffn_in['ln2_b']}
    _x0 = _d['L0_attn_x']
    _d['L0_attn_x'] = jax.random.normal(jax.random.fold_in(jax.random.key(seed), 1), (2, 1024, 128), dtype=_x0.dtype)
    del _x0
    return _d

def reference(L0_attn_x, L0_attn_Wq, L0_attn_Wk, L0_attn_Wv, L0_attn_gate_W, L0_attn_gate_b, L0_attn_p_W, L0_attn_p_b, L0_attn_clock_W, L0_attn_clock_b, L0_attn_out_W, L0_attn_out_b, L0_attn_ln1_g, L0_attn_ln1_b, L0_attn_ln2_g, L0_attn_ln2_b, L0_attn_mlp_W1, L0_attn_mlp_b1, L0_attn_mlp_W2, L0_attn_mlp_b2, L0_ffn_w1_w, L0_ffn_w1_s, L0_ffn_w2_w, L0_ffn_w2_s, L0_ffn_h1_w, L0_ffn_h1_s, L0_ffn_h2_w, L0_ffn_h2_s, L0_ffn_w3_w, L0_ffn_w3_s, L1_attn_conv_w, L1_attn_pe_w, L1_attn_qkv_w, L1_attn_out_w, L1_ffn_Wq, L1_ffn_Wk, L1_ffn_Wv, L1_ffn_Wo, L1_ffn_bo, L1_ffn_Wr, L1_ffn_We1, L1_ffn_be1, L1_ffn_We2, L1_ffn_be2, L1_ffn_ln1_g, L1_ffn_ln1_b, L1_ffn_ln2_g, L1_ffn_ln2_b):

    def _L0_attn_ref(x, Wq, Wk, Wv, gate_W, gate_b, p_W, p_b, clock_W, clock_b, out_W, out_b, ln1_g, ln1_b, ln2_g, ln2_b, mlp_W1, mlp_b1, mlp_W2, mlp_b2):
        import math
        import jax, jax.numpy as jnp
        import numpy as np
        B, T, D, H = (2, 1024, 128, 1)
        DH = D // H

        def _layernorm(x, g, b):
            m = x.mean(-1, keepdims=True)
            v = ((x - m) ** 2).mean(-1, keepdims=True)
            return (x - m) * jax.lax.rsqrt(v + 1e-05) * g + b

        def _l2norm(x):
            n = jnp.sqrt(jnp.sum(x * x, axis=-1, keepdims=True))
            return x / jnp.maximum(n, 1e-12)

        def _rope(x, times):
            half = x.shape[-1] // 2
            freqs = jnp.exp(-jnp.arange(half, dtype=x.dtype) * (math.log(10000.0) / half))
            th = times[:, None] * freqs[None, :]
            c = jnp.cos(th)[None, :, None, :]
            s = jnp.sin(th)[None, :, None, :]
            xr = x.reshape(x.shape[:-1] + (half, 2))
            x1, x2 = (xr[..., 0], xr[..., 1])
            out = jnp.stack([x1 * c - x2 * s, x1 * s + x2 * c], axis=-1)
            return out.reshape(x.shape)

        def _forward(x, Wq, Wk, Wv, gate_W, gate_b, p_W, p_b, clock_W, clock_b, out_W, out_b, ln1_g, ln1_b, ln2_g, ln2_b, mlp_W1, mlp_b1, mlp_W2, mlp_b2):
            Bc, Tc, Dc = x.shape
            residual = x
            xn = _layernorm(x, ln1_g, ln1_b)
            times = jnp.arange(Tc, dtype=x.dtype)
            q = _l2norm((xn @ Wq).reshape(Bc, Tc, H, DH))
            k = _l2norm((xn @ Wk).reshape(Bc, Tc, H, DH))
            v = (xn @ Wv).reshape(Bc, Tc, H, DH)
            clock = jax.nn.softplus(xn @ clock_W + clock_b).reshape(Bc, Tc, H, 1)
            q = _rope(q, times)
            k = _rope(k, times)
            gj = -jax.nn.softplus(xn @ gate_W + gate_b).reshape(Bc, Tc, H, DH)
            gj_cumprod = jnp.exp(jnp.clip(jnp.cumsum(gj, axis=1), -60.0, 50.0))
            q = q * gj_cumprod
            k = k / (gj_cumprod + 1e-08)
            p = (xn @ p_W + p_b).reshape(Bc, Tc, H, DH)
            p_max = jnp.max(p, axis=1, keepdims=True)
            p_exp = jnp.exp(p - p_max) * clock
            p_cum = jnp.cumsum(p_exp, axis=1)
            q = q / (p_cum + 1e-08)
            k = k * p_exp
            scale = 1.0 / math.sqrt(DH)
            scores = jnp.einsum('bqhd,bkhd->bhqk', q, k) * scale
            mask = jnp.tril(jnp.ones((Tc, Tc), dtype=bool))
            scores = jnp.where(mask[None, None], scores, jnp.finfo(scores.dtype).min)
            w = jax.nn.softmax(scores, axis=-1)
            out = jnp.einsum('bhqk,bkhd->bqhd', w, v).reshape(Bc, Tc, Dc)
            x2 = out @ out_W + out_b + residual
            h = _layernorm(x2, ln2_g, ln2_b)
            mlp = jax.nn.gelu(h @ mlp_W1 + mlp_b1, approximate=False) @ mlp_W2 + mlp_b2
            return x2 + mlp
        return _forward(x, Wq, Wk, Wv, gate_W, gate_b, p_W, p_b, clock_W, clock_b, out_W, out_b, ln1_g, ln1_b, ln2_g, ln2_b, mlp_W1, mlp_b1, mlp_W2, mlp_b2)

    def _L0_ffn_ref(x, w1_w, w1_s, w2_w, w2_s, h1_w, h1_s, h2_w, h2_s, w3_w, w3_s):
        import jax, jax.numpy as jnp
        import numpy as np
        D_IN, D_HID = (128, 512)

        def _ternary(key, shape):
            return jax.random.randint(key, shape, -1, 2).astype(jnp.float32)

        def _tlin(x, w, s):
            return jnp.einsum('bsi,oi->bso', x, w) * s
        h = jax.nn.silu(_tlin(x, w1_w, w1_s)) * _tlin(x, w2_w, w2_s)
        h = jax.nn.gelu(_tlin(h, h1_w, h1_s), approximate=False)
        h = jax.nn.gelu(_tlin(h, h2_w, h2_s), approximate=False)
        return _tlin(h, w3_w, w3_s)

    def _L1_attn_ref(x, conv_w, pe_w, qkv_w, out_w):
        import jax, jax.numpy as jnp
        import numpy as np
        B, S, D, H = (4, 256, 128, 16)
        HD = D // H
        b, s, d = x.shape
        h, hd = (H, d // H)
        xc = jnp.transpose(x, (0, 2, 1))[..., None]
        xc = jax.lax.conv_general_dilated(xc, conv_w, window_strides=(1, 1), padding=((1, 1), (1, 1)), dimension_numbers=('NCHW', 'OIHW', 'NCHW'), feature_group_count=d)
        xs = jnp.transpose(xc[..., 0], (0, 2, 1))
        xs = xs + xs @ pe_w.T
        qkv = (xs @ qkv_w.T).reshape(b, s, 3, d)
        qkv = jnp.transpose(qkv, (0, 2, 1, 3))
        q = qkv[:, 0].reshape(b, h, s, hd).astype(jnp.bfloat16)
        k = qkv[:, 1].reshape(b, h, s, hd).astype(jnp.bfloat16)
        v = qkv[:, 2].reshape(b, h, s, hd).astype(jnp.bfloat16)
        scale = jnp.sqrt(jnp.asarray(hd, dtype=jnp.bfloat16))
        scores = jnp.einsum('bhqd,bhkd->bhqk', q, k) / scale
        attn = jax.nn.softmax(scores, axis=-1)
        o = jnp.einsum('bhqk,bhkd->bhqd', attn, v)
        o = jnp.transpose(o, (0, 2, 1, 3)).reshape(b, s, d).astype(jnp.float32)
        return o @ out_w.T

    def _L1_ffn_ref(x, Wq, Wk, Wv, Wo, bo, Wr, We1, be1, We2, be2, ln1_g, ln1_b, ln2_g, ln2_b):
        import jax, jax.numpy as jnp
        import numpy as np
        B, S, D, H, F, E = (2, 128, 128, 16, 512, 8)
        HD = D // H
        EPS = 1e-06

        def _layernorm(x, g, b):
            m = jnp.mean(x, axis=-1, keepdims=True)
            v = jnp.var(x, axis=-1, keepdims=True)
            return (x - m) / jnp.sqrt(v + EPS) * g + b
        b, s, d = x.shape

        def split_heads(t):
            return t.reshape(b, s, H, HD).transpose(0, 2, 1, 3)
        q = split_heads(x @ Wq)
        k = split_heads(x @ Wk)
        v = split_heads(x @ Wv)
        scores = jnp.einsum('bhqd,bhkd->bhqk', q, k) / jnp.sqrt(jnp.float32(HD))
        attn_w = jax.nn.softmax(scores, axis=-1)
        ctx = jnp.einsum('bhqk,bhkd->bhqd', attn_w, v)
        ctx = ctx.transpose(0, 2, 1, 3).reshape(b, s, d)
        attn_out = ctx @ Wo + bo
        out1 = _layernorm(x + attn_out, ln1_g, ln1_b)
        router_probs = jax.nn.softmax(out1 @ Wr, axis=-1)
        top_g, top_i = jax.lax.top_k(router_probs, 2)
        top_g = jax.nn.softmax(top_g, axis=-1)
        acc = jnp.zeros_like(out1)
        for e in range(E):
            sel = top_i == e
            msk = jnp.any(sel, axis=-1)[..., None].astype(out1.dtype)
            h = jax.nn.gelu(out1 * msk @ We1[e] + be1[e], approximate=False)
            o = h @ We2[e] + be2[e]
            gate = jnp.sum(top_g * sel.astype(top_g.dtype), axis=-1, keepdims=True)
            acc = acc + o * gate
        return _layernorm(out1 + acc, ln2_g, ln2_b)
    x = L0_attn_x
    xn = _layernorm(x, axis=-1)
    x = x + _L0_attn_ref(xn, L0_attn_Wq, L0_attn_Wk, L0_attn_Wv, L0_attn_gate_W, L0_attn_gate_b, L0_attn_p_W, L0_attn_p_b, L0_attn_clock_W, L0_attn_clock_b, L0_attn_out_W, L0_attn_out_b, L0_attn_ln1_g, L0_attn_ln1_b, L0_attn_ln2_g, L0_attn_ln2_b, L0_attn_mlp_W1, L0_attn_mlp_b1, L0_attn_mlp_W2, L0_attn_mlp_b2) + _L0_ffn_ref(xn, L0_ffn_w1_w, L0_ffn_w1_s, L0_ffn_w2_w, L0_ffn_w2_s, L0_ffn_h1_w, L0_ffn_h1_s, L0_ffn_h2_w, L0_ffn_h2_s, L0_ffn_w3_w, L0_ffn_w3_s)
    xn = _layernorm(x, axis=-1)
    x = x + _L1_attn_ref(xn, L1_attn_conv_w, L1_attn_pe_w, L1_attn_qkv_w, L1_attn_out_w) + _L1_ffn_ref(xn, L1_ffn_Wq, L1_ffn_Wk, L1_ffn_Wv, L1_ffn_Wo, L1_ffn_bo, L1_ffn_Wr, L1_ffn_We1, L1_ffn_be1, L1_ffn_We2, L1_ffn_be2, L1_ffn_ln1_g, L1_ffn_ln1_b, L1_ffn_ln2_g, L1_ffn_ln2_b)
    return x

_drawn_inputs = setup_inputs


def setup_inputs(seed=0):
    import zlib

    import numpy as np

    out = dict(_drawn_inputs(seed))
    spreads = {'L0_attn_gate_b': (0.0, 0.1),
     'L0_attn_p_b': (0.0, 0.1),
     'L0_attn_out_b': (0.0, 0.1),
     'L0_attn_ln1_g': (1.0, 0.2),
     'L0_attn_ln1_b': (0.0, 0.1),
     'L0_attn_ln2_g': (1.0, 0.2),
     'L0_attn_ln2_b': (0.0, 0.1),
     'L0_attn_mlp_b1': (0.0, 0.1),
     'L0_attn_mlp_b2': (0.0, 0.1),
     'L1_ffn_bo': (0.0, 0.1),
     'L1_ffn_be1': (0.0, 0.1),
     'L1_ffn_be2': (0.0, 0.1),
     'L1_ffn_ln1_g': (1.0, 0.2),
     'L1_ffn_ln1_b': (0.0, 0.1),
     'L1_ffn_ln2_g': (1.0, 0.2),
     'L1_ffn_ln2_b': (0.0, 0.1)}
    factors = {}
    for name, (base, spread) in spreads.items():
        noise = np.random.default_rng([zlib.crc32(name.encode()), seed]).standard_normal(out[name].shape)
        drawn = base * np.exp(spread * noise) if base else spread * noise
        out[name] = jnp.asarray(drawn.astype(out[name].dtype))
    for name, factor in factors.items():
        out[name] = (out[name] * factor).astype(out[name].dtype)
    return out
```

```python
from contextlib import ExitStack
import math

import numpy as np
import concourse.bass as bass
from concourse import mybir

ALU = mybir.AluOpType
ACT = mybir.ActivationFunctionType
AX = mybir.AxisListType
F32 = mybir.dt.float32
BF16 = mybir.dt.bfloat16

P = 128
D = 128
BATCH, SEQ = 2, 1024
TOK = BATCH * SEQ
TILES = TOK // P
BT = 4
BLK = BT * P
BLOCKS = TOK // BLK
HID = 512
FC = HID // P
EXP = 8
HEADS, HD = 16, 8
UNITS = BATCH * HEADS // 2
KT = SEQ // P
PARTS = 3
EPS0, EPS1 = 1e-5, 1e-6
MROW = 64
SLOTS = 4
FREE = 1
CREDIT = 3
PCREDIT = 2
SCORE_BANK = (4, 5, 6, 5)
Q_PARTS = (0, 0, 0, 1, 1, 2)
K_PARTS = (0, 1, 2, 0, 1, 0)
N_PARTS = len(Q_PARTS) + len(K_PARTS) + 2
HEAD_SCALE = (1.0 / math.sqrt(HD), 1.0 / 2.828125)
NDMA = dict(x=BLOCKS, cst=1, cols=1, rows=8, w0=1, wf=1, w1=1, we1=1, we2=2)

W0 = dict(qkv=0, gate=384, p=512, clock=640, out=768, m1=896, m2=1408)
W0N = 1920
WF = dict(w1=0, w2=512, h1=1024, h2=3072, w3=5120)
WFN = 5632
W1 = dict(pe=0, qkv=128, ao=512, q=640, k=768, v=896, o=1024, r=1152)
W1N = 1160
COLS = ["gate_b", "p_b", "clock_b", "g1", "b1", "g2", "b2"]
ROWS = ["out_b", "mlp_b2", "w3_s", "bo", "l1g", "l1b", "l2g", "l2b"]
C4 = ["mb1", "s1", "s2", "t1", "t2"]
CC = {n: i for i, n in enumerate(COLS)}
for _i, _n in enumerate(C4):
    CC[_n] = len(COLS) + 4 * _i
CC["be1"] = len(COLS) + 4 * len(C4)
CC["conv"] = CC["be1"] + 4 * EXP
CN = CC["conv"] + 3
CST = dict(ident=0, mask=128, cos=256, sin=256 + KT * D, rank=256 + 2 * KT * D)
CSTN = 256 + 2 * KT * D + EXP


class Chain:

    def __init__(self, eng, sem, wait_apart):
        self.eng, self.sem, self.wait_apart, self.n, self.reg = eng, sem, wait_apart, 0, None

    def mark(self, ins):
        ins.then_inc(self.sem, 1)
        self.n += 1

    def wait(self):
        self.eng.wait_ge(self.sem, self.n if self.reg is None else self.reg + self.n)

    def __call__(self, ins):
        self.mark(ins)
        self.wait()

    def apart(self, ins):
        self.mark(ins)
        self.wait_apart(self.eng, self.sem, self.n if self.reg is None else self.reg + self.n)

    def enter(self, i, per):
        self.reg, self.start, self.per = i * per, self.n, per

    def leave(self, rounds):
        assert self.n - self.start == self.per, (self.n - self.start, self.per)
        self.reg, self.n = None, self.start + rounds * self.per


class Count:

    def __init__(self):
        self.n, self.reg = 0, None

    def seen(self):
        return self.n if self.reg is None else self.reg + self.n

    def next(self):
        self.n += 1
        return self.seen()

    def enter(self, i, per):
        self.reg, self.start, self.per = i * per, self.n, per

    def leave(self, rounds):
        assert self.n - self.start == self.per
        self.reg, self.n = None, self.start + rounds * self.per


def peak_plan(left):
    plan = {s: [] for s in range(1, KT + 1)}
    for s in range(1, KT):
        if left >= 2:
            plan[s] += [(2, 2 * s), (2, 2 * s + 1)]
        if s == 2 and left >= 1:
            plan[s].append((1, None))
    if left >= 3:
        plan[KT] += [(3, 0), (3, 1)]
    return plan


def build(nc, t, out):
    ctx = ExitStack()
    with ctx:
        def sb(name, shape, dt=F32):
            return ctx.enter_context(nc.sbuf_tensor(name, shape, dt))

        def sem(name):
            return ctx.enter_context(nc.semaphore(name))

        ps = ctx.enter_context(nc.psum_tensor("ps", [P, 8, 512], F32))
        w0 = sb("w0", [P, W0N])
        wf = sb("wf", [P, WFN])
        w1 = sb("w1", [P, W1N])
        we1 = sb("we1", [P, EXP * HID])
        we2 = sb("we2", [P, EXP * FC * D])
        cols = sb("cols", [P, CN])
        cst = sb("cst", [P, CSTN])
        rows = sb("rows", [P, len(ROWS), D])
        ident = cst[:, 0:P]
        big = sb("big", [P, 11 * TOK])
        r = [big[:, n * TOK:(n + 1) * TOK] for n in range(11)]
        x_tok, xn_tok, xn_t, v_tok, q_t, k_t, zg, zp, zc, tmp, tmp2 = r
        stage = sb("stage", [P, 2, BLK])
        stage1 = sb("stage1", [P, 2, BLK])
        stage_t = sb("stage_t", [P, 2, BLK])
        qk = sb("qk", [P, 2, 2 * BLK])
        qk1 = sb("qk1", [P, 2, 2 * BLK])
        qk2 = sb("qk2", [P, 2, 2 * BLK])
        st = sb("st", [P, BT, 6])
        mv = sb("mv", [P, BT, 2])
        sd = sb("sd", [P, BT])
        rs = sb("rs", [P, BT])
        ss = sb("ss", [P, 2 * BT])
        nrm = sb("nrm", [P, 2 * BT])
        rn = sb("rn", [P, 2 * BT])
        pm = sb("pm", [P, BATCH])
        carry = sb("carry", [P, 2])
        nm = sb("nm", [P, 4])
        sm = sb("sm", [P, 4])
        gates = sb("gates", [P, TILES, EXP])
        sil, hid0, hid1, hid2 = stage, qk, qk1, qk2
        q_s, k_s = hid0[:, 0, :], hid0[:, 1, :]
        v_s = hid1[:, 0, :]
        ao_t = hid1[:, 1, :]
        probs = hid2
        probs_t = wf[:, 0:SEQ]
        x3_tok, x3_t, y_t, v1 = r[1], r[2], r[3], r[4]
        q_parts = big[:, 5 * TOK:5 * TOK + 3 * TOK // 2].bitcast(BF16).rearrange("p (a t) -> p a t", a=PARTS)
        k_parts = big[:, 7 * TOK:7 * TOK + 3 * TOK // 2].bitcast(BF16).rearrange("p (a t) -> p a t", a=PARTS)
        q_b = r[9][:, 0:TOK // 2].bitcast(BF16)
        k_b = r[9][:, TOK // 2:TOK].bitcast(BF16)
        slot = [r[5 + n].bitcast(BF16).rearrange("p (a t) -> p a t", a=2) for n in range(SLOTS)]
        pr = [r[9 + n] for n in range(2)]
        o_in, den = r[2][:, 0:SEQ], r[2][:, SEQ:TOK]
        ctx_t = r[3][:, 0:SEQ]
        o_st = [r[3][:, SEQ + n * 512:SEQ + (n + 1) * 512] for n in range(2)]
        va = [wf[:, n * 512:(n + 1) * 512] for n in range(4)]
        v2 = wf[:, 2048:2048 + TOK // 2].bitcast(BF16)
        neg_m = sb("neg_m", [P, 2, 16])
        m_rest = sb("m_rest", [P, 2, 16])
        m_split = sb("m_split", [P, 2, PARTS, 16], BF16)
        m_t = sb("m_t", [PARTS * 16, 2, P], BF16)
        ident_b = sb("ident_b", [P, P], BF16)
        o1_t = r[4]
        g_t = r[2][0:EXP, :]
        xs = qk1[:, 0, :].rearrange("p (h c t) -> p h c t", h=8, c=2)
        gb = sb("gb", [P, 2, BT * EXP])
        be2 = sb("be2", [EXP, D])
        one_col = sb("one_col", [P, 1])
        eps0, eps1 = (sb(f"eps{n}", [P, 1])[:, :] for n in range(2))
        tk = wf[:, 3072:3072 + 12 * TILES * EXP].rearrange("p (k m) -> p k m", k=12)
        qs_dram = nc.dram_tensor("qs_dram", (6, BATCH, P, SEQ), BF16, kind="Internal").ap()
        ks_dram = nc.dram_tensor("ks_dram", (6, BATCH, P, SEQ), BF16, kind="Internal").ap()
        qb_dram = nc.dram_tensor("qb_dram", (P, TOK), BF16, kind="Internal").ap()
        kb_dram = nc.dram_tensor("kb_dram", (P, TOK), BF16, kind="Internal").ap()
        o_dram = [nc.dram_tensor(f"o_dram{n}", (UNITS, P, 512), F32, kind="Internal").ap() for n in range(2)]

        landed = {n: sem("in_" + n) for n in ("x", "w0", "wf", "w1", "we1", "we2", "cols", "cst", "rows")}
        dve_seq, act_seq, pool_seq = (sem(n + "_seq") for n in ("dve", "act", "pool"))
        stored = sem("stored")
        S = {n: sem(n) for n in (
            "consts var_ready sd_ready xn_ready n1_ready xn_t_psum n1_t_psum n1_t_kept xn_t_kept qkv_ready gp_ready "
            "clock_ready nrm_ready qk_scaled rope_ready rope_t_psum zg_kept zp_kept zc_kept q_kept k_kept v_kept "
            "z_ready sil_done glu_done h1_ready h1_done h2_ready h2_done y_ready y_done pm_ready logs_ready "
            "decay_ready decay_exp factors_done "
            "batch_staged s_ready peak_ready exp_done p_ready p_t_psum p_t_kept av_ready av_kept x2_ready x2_kept "
            "m_var m_sd m_n m_t_psum m_t_kept m1_ready m1_done m2_ready m2_kept "
            "l_var l_sd l_n l_t_psum l_t_kept lq_ready hi_kept parts_kept lv_ready lv_kept conv_done pe_ready "
            "xs_kept bq_ready bq_kept bv_ready bv_kept o_var o_sd o_n o_psum o_sum o_t_psum o_t_kept route_ready "
            "route_exp route_exp2 route_sum gates_ready gt_psum gt_kept up_ready up_done down_ready down_kept f_var f_sd "
            "ctx_ready wo_ready wo_kept").split()}
        att = [{n: sem(f"{n}{a}") for n in (
            "peak_scores_ready peak_bank_free scores_ready probs_done av_steps out_kept m_split_ready "
            "va_ready rows_zeroed slots_ready out_back").split()} for a in range(2)]
        for a in range(2):
            att[a]["out_stored"] = [sem(f"out_stored{a}_{n}") for n in range(2)]
            att[a]["qk_loaded"] = [sem(f"qk_loaded{a}_{n}") for n in range(SLOTS)]
            att[a]["m_loaded"] = [sem(f"m_loaded{a}_{n}") for n in range(SLOTS)]
        parts_stored = sem("parts_stored")
        free_at_start = [S[n] for n in (
            "k_kept q_kept qk_scaled zg_kept zp_kept zc_kept y_done glu_done h1_done h2_done h1_ready h2_ready y_ready "
            "exp_done p_t_kept p_t_psum av_ready av_kept x2_kept m_t_kept m1_done m2_kept m2_ready l_t_kept parts_kept "
            "lv_kept xs_kept bq_kept bv_kept bv_ready up_done down_kept down_ready").split()]
        for A in att:
            free_at_start += [A["out_kept"], *A["out_stored"]]

        block = ctx.enter_context(nc.Block())

        def wait_apart(eng, semaphore, value):
            if not isinstance(value, int):
                eng.compute_val(value)
                eng.wait_ge(S["consts"], 1)
            eng.wait_ge(semaphore, value)

        def flat(a):
            return a[:, :, :].rearrange("p a b -> p (a b)")

        def tiled(a):
            return a.rearrange("p (j d) -> p j d", d=D)

        def rep(name):
            return rows[:, ROWS.index(name), :].unsqueeze(1).to_broadcast([P, BT, D])

        def values(a, c):
            return va[c % 2] if a == 0 else va[2 + c % 2].bitcast(BF16)[:, 0:512]

        def probabilities(a, s):
            return pr[s % 2] if a == 0 else pr[s % 2].bitcast(BF16)[:, 0:4 * 512]

        def one_of(ap, n):
            return ap[n] if isinstance(n, int) else ap[bass.ds(n, 1)].squeeze(0)

        def blk(i, s):
            return bass.ds(i * (2 * BLK) + s * BLK, BLK)

        def tile_cols(i, s, j):
            return bass.ds(i * (2 * BLK) + (s * BT + j) * P, P)

        def col(name, n=0):
            return cols[:, CC[name] + n:CC[name] + n + 1]

        def row(name):
            return rows[:, ROWS.index(name), :]

        @block.vector
        def _(dve):
            link = Chain(dve, dve_seq, wait_apart)
            v = nc.vector

            def stats(src, ready):
                for j in range(BT):
                    ins = v.bn_stats(st[:, j, :], src(j))
                link.apart(ins)
                for j in range(BT):
                    ins = v.bn_aggr(mv[:, j, :], st[:, j, :])
                ins.then_inc(S[ready], 1)

            def normalise(src, dst, sd_ready, n, done):
                dve.wait_ge(S[sd_ready], n)
                link(v.reciprocal(rs[:, :], sd[:, :]))
                for j in range(BT):
                    ins = v.tensor_scalar(dst(j), src(j), mv[:, j, 0:1], rs[:, j:j + 1], ALU.subtract, ALU.mult)
                if done is None:
                    link(ins)
                else:
                    ins.then_inc(S[done], 1)

            for n in ("x", "cst", "cols", "rows"):
                dve.wait_ge(landed[n], 16 * NDMA[n])
            with dve.Fori(0, BATCH) as i:
                link.enter(i, 2 * 8)
                for s in range(2):
                    n = 2 * i + s
                    stats(lambda j: x_tok[:, tile_cols(i, s, j)], "var_ready")
                    dst = lambda j: stage[:, s, j * P:(j + 1) * P]
                    normalise(lambda j: x_tok[:, tile_cols(i, s, j)], dst, "sd_ready", 2 * n + 1, "xn_ready")
                    dve.wait_ge(S["xn_ready"], n + 1)
                    link.mark(v.tensor_copy(xn_tok[:, blk(i, s)], stage[:, s, :]))
                    stats(dst, "var_ready")
                    normalise(dst, lambda j: stage1[:, s, j * P:(j + 1) * P], "sd_ready", 2 * n + 2, "n1_ready")
                    dve.wait_ge(S["nrm_ready"], n + 1)
                    link(v.tensor_scalar(nrm[:, :], nrm[:, :], 1e-12, None, ALU.max))
                    link(v.reciprocal(rn[:, :], nrm[:, :]))
                    for j in range(BT):
                        for h in range(2):
                            ins = v.tensor_scalar(qk[:, s, (2 * j + h) * D:(2 * j + h + 1) * D],
                                                  ps[:, 2 + j, h * D:(h + 1) * D],
                                                  rn[:, 2 * j + h:2 * j + h + 1], None, ALU.mult)
                    ins.then_inc(S["qk_scaled"], 1)
                    dve.wait_ge(S["qk_scaled"], FREE + n + 1)
                    src = qk[:, s, :].rearrange("p (j h d) -> p j h d", j=BT, h=2)
                    pairs = qk[:, s, :].rearrange("p (j h f e) -> p j h f e", j=BT, h=2, e=2)
                    turned = qk2[:, s, :].rearrange("p (j h f e) -> p j h f e", j=BT, h=2, e=2)
                    a = qk1[:, s, :].rearrange("p (j h d) -> p j h d", j=BT, h=2)
                    cos = cst[:, CST["cos"] + s * BLK:CST["cos"] + (s + 1) * BLK].rearrange("p (j d) -> p j d", j=BT)
                    sin = cst[:, CST["sin"] + s * BLK:CST["sin"] + (s + 1) * BLK].rearrange(
                        "p (j f e) -> p j f e", j=BT, e=2)
                    for h in range(2):
                        v.tensor_tensor(a[:, :, h, :], src[:, :, h, :], cos, ALU.mult)
                        v.tensor_tensor(turned[:, :, h, :, 0], pairs[:, :, h, :, 1], sin[:, :, :, 0], ALU.mult)
                        ins = v.tensor_tensor(turned[:, :, h, :, 1], pairs[:, :, h, :, 0], sin[:, :, :, 1], ALU.mult)
                    link(ins)
                    v.tensor_tensor(qk1[:, s, :], qk1[:, s, :], qk2[:, s, :], ALU.add).then_inc(S["rope_ready"], 1)
                link.leave(BATCH)

            half = SEQ // 2
            with dve.Fori(0, BATCH) as i:
                link.enter(i, 29)
                for s in range(2):
                    n = 2 * i + s
                    at = blk(i, s)
                    if s == 0:
                        dve.wait_ge(S["zp_kept"], FREE + BLOCKS)
                        v.tensor_reduce(pm[:, 0:1], zp[:, bass.ds(i * SEQ, SEQ)], AX.X, ALU.max,
                                        negate=True).then_inc(S["pm_ready"], 1)
                    for fc in range(FC):
                        dve.wait_ge(S["sil_done"], 4 * n + fc + 1)
                        if fc == 0:
                            dve.wait_ge(S["h1_ready"], FREE + 4 * n)
                        v.scalar_tensor_tensor(out=flat(hid0)[:, fc * BLK:(fc + 1) * BLK], in0=ps[:, 2 + fc % 2, :],
                                               scalar=col("s2", fc), in1=sil[:, fc % 2, :], op0=ALU.mult,
                                               op1=ALU.mult).then_inc(S["glu_done"], 1)
                    dve.wait_ge(S["logs_ready"], n + 1)
                    link(v.scalar_tensor_tensor(out=zg[:, at], in0=zg[:, at], scalar=0.0, in1=tmp[:, at],
                                                op0=ALU.max, op1=ALU.add))
                    link(v.scalar_tensor_tensor(out=zc[:, at], in0=zc[:, at], scalar=0.0, in1=tmp2[:, at],
                                                op0=ALU.max, op1=ALU.add))
                    link(v.tensor_tensor(zp[:, at], zp[:, at], zc[:, at], ALU.mult))
                    ones = one_col[:, 0:1].to_broadcast([P, BLK])
                    link(v.tensor_tensor_scan(tmp[:, at], ones, zg[:, at], carry[:, 0:1] if s else 0.0,
                                              ALU.mult, ALU.add))
                    link(v.tensor_tensor_scan(tmp2[:, at], ones, zp[:, at], carry[:, 1:2] if s else 0.0,
                                              ALU.mult, ALU.add))
                    if s == 0:
                        last = bass.ds(i * SEQ + half - 1, 1)
                        v.tensor_copy(carry[:, 0:1], tmp[:, last])
                        link(v.tensor_copy(carry[:, 1:2], tmp2[:, last]))
                    link(v.tensor_scalar(tmp[:, at], tmp[:, at], -1.0, -60.0, ALU.mult, ALU.max))
                    v.tensor_scalar(tmp[:, at], tmp[:, at], 50.0, None, ALU.min).then_inc(S["decay_ready"], 1)
                    link.apart(v.tensor_scalar(tmp2[:, at], tmp2[:, at], 1e-8, None, ALU.add))
                    link(v.reciprocal(tmp2[:, at], tmp2[:, at]))
                    dve.wait_ge(S["decay_exp"], n + 1)
                    link(v.tensor_tensor(tmp2[:, at], zg[:, at], tmp2[:, at], ALU.mult))
                    link.apart(v.tensor_scalar(tmp[:, at], zg[:, at], 1e-8, None, ALU.add))
                    link(v.reciprocal(tmp[:, at], tmp[:, at]))
                    link(v.tensor_tensor(tmp[:, at], zp[:, at], tmp[:, at], ALU.mult))
                    v.tensor_tensor(q_t[:, at], q_t[:, at], tmp2[:, at], ALU.mult)
                    link(v.tensor_tensor(k_t[:, at], k_t[:, at], tmp[:, at], ALU.mult))
                    dve.wait_ge(S["y_ready"], FREE + n + 1)
                    v.tensor_tensor(tiled(stage1[:, s, :]), tiled(ps[:, 0, :]), rep("w3_s"),
                                    ALU.mult).then_inc(S["y_done"], 1)
                    dve.wait_ge(S["y_done"], FREE + n + 1)
                    link(v.tensor_tensor(x_tok[:, at], x_tok[:, at], stage1[:, s, :], ALU.add))
                link.leave(BATCH)

            scale = 1.0 / math.sqrt(D)
            with dve.Fori(0, BATCH) as i:
                link.enter(i, 2 * KT + 2)
                all_of = bass.ds(i * SEQ, SEQ)
                v.tensor_copy(q_s, q_t[:, all_of])
                v.tensor_copy(k_s, k_t[:, all_of])
                v.tensor_copy(v_s, v_tok[:, all_of]).then_inc(S["batch_staged"], 1)

                def peak(qt):
                    dve.wait_ge(S["s_ready"], KT * i + qt + 1)
                    pair = ps[:, 2 * (qt % 2):2 * (qt % 2) + 2, :].rearrange("p a b -> p (a b)")
                    link(v.tensor_reduce(nm[:, qt % 2:qt % 2 + 1], pair[:, 0:(qt + 1) * P], AX.X, ALU.max,
                                         negate=True))
                    v.tensor_scalar(nm[:, 2 + qt % 2:3 + qt % 2], nm[:, qt % 2:qt % 2 + 1], scale, None,
                                    ALU.mult).then_inc(S["peak_ready"], 1)

                def divide(qt):
                    dve.wait_ge(S["exp_done"], FREE + KT * i + qt + 1)
                    link(v.reciprocal(sm[:, 2 + qt % 2:3 + qt % 2], sm[:, qt % 2:qt % 2 + 1]))
                    p = probs[:, qt % 2, 0:(qt + 1) * P]
                    v.tensor_scalar(p, p, sm[:, 2 + qt % 2:3 + qt % 2], None, ALU.mult).then_inc(S["p_ready"], 1)

                def keep(qt):
                    dve.wait_ge(S["av_ready"], FREE + KT * i + qt + 1)
                    v.tensor_copy(ao_t[:, qt * P:(qt + 1) * P], ps[:, 6, 0:P]).then_inc(S["av_kept"], 1)

                peak(0)
                for qt in range(KT):
                    if qt + 1 < KT:
                        peak(qt + 1)
                    divide(qt)
                    if qt:
                        keep(qt - 1)
                keep(KT - 1)
                for s in range(2):
                    at = blk(i, s)
                    dve.wait_ge(S["x2_ready"], 2 * i + s + 1)
                    v.tensor_tensor(xn_tok[:, at], xn_tok[:, at], ps[:, 7, :], ALU.add).then_inc(S["x2_kept"], 1)
                    dve.wait_ge(S["x2_kept"], FREE + 2 * i + s + 1)
                    link(v.tensor_tensor(tiled(xn_tok[:, at]), tiled(xn_tok[:, at]), rep("out_b"), ALU.add))
                link.leave(BATCH)

            with dve.Fori(0, BATCH) as i:
                link.enter(i, 8)
                for s in range(2):
                    n, at = 2 * i + s, blk(i, s)
                    src = lambda j: xn_tok[:, tile_cols(i, s, j)]
                    stats(src, "m_var")
                    normalise(src, lambda j: stage[:, s, j * P:(j + 1) * P], "m_sd", n + 1, "m_n")
                    dve.wait_ge(S["m2_ready"], FREE + n + 1)
                    v.tensor_tensor(x_tok[:, at], x_tok[:, at], ps[:, 5, :], ALU.add).then_inc(S["m2_kept"], 1)
                    dve.wait_ge(S["m2_kept"], FREE + n + 1)
                    link(v.tensor_tensor(x_tok[:, at], x_tok[:, at], xn_tok[:, at], ALU.add))
                    link(v.tensor_tensor(tiled(x_tok[:, at]), tiled(x_tok[:, at]), rep("mlp_b2"), ALU.add))
                link.leave(BATCH)

            with dve.Fori(0, BATCH) as i:
                link.enter(i, 18)
                for s in range(2):
                    n, at = 2 * i + s, blk(i, s)
                    src = lambda j: x_tok[:, tile_cols(i, s, j)]
                    stats(src, "l_var")
                    normalise(src, lambda j: stage[:, s, j * P:(j + 1) * P], "l_sd", n + 1, "l_n")
                    dve.wait_ge(S["l_n"], n + 1)
                    link.mark(v.tensor_copy(x3_tok[:, at], stage[:, s, :]))
                    for m, parts in enumerate((q_parts, k_parts)):
                        rest = stage1[:, m, :]
                        dve.wait_ge(S["hi_kept"], 2 * n + m + 1)
                        link(v.tensor_tensor(rest, ps[:, 1 + m, :], parts[:, 0, at], ALU.subtract))
                        link(v.tensor_copy(parts[:, 1, at], rest))
                        link(v.tensor_tensor(rest, rest, parts[:, 1, at], ALU.subtract))
                        v.tensor_copy(parts[:, 2, at], rest).then_inc(S["parts_kept"], 1)
                        dve.wait_ge(S["parts_kept"], FREE + 2 * n + m + 1)
                link.leave(BATCH)
            dve.wait_ge(S["l_t_kept"], FREE + BLOCKS)
            for b in range(BATCH):
                x3, y3 = (a[:, b * SEQ:(b + 1) * SEQ] for a in (x3_t, y_t))
                link(v.tensor_scalar(y3, x3, col("conv", 1), None, ALU.mult))
                link(v.scalar_tensor_tensor(out=y3[:, 1:SEQ], in0=x3[:, 0:SEQ - 1], scalar=col("conv", 0),
                                            in1=y3[:, 1:SEQ], op0=ALU.mult, op1=ALU.add))
                v.scalar_tensor_tensor(out=y3[:, 0:SEQ - 1], in0=x3[:, 1:SEQ], scalar=col("conv", 2),
                                       in1=y3[:, 0:SEQ - 1], op0=ALU.mult, op1=ALU.add).then_inc(S["conv_done"], 1)
                dve.wait_ge(S["conv_done"], b + 1)
            with dve.Fori(0, BATCH) as i:
                for s in range(2):
                    n, at = 2 * i + s, blk(i, s)
                    dve.wait_ge(S["pe_ready"], n + 1)
                    dve.wait_ge(S["bv_ready"], FREE + 2 * n)
                    for c in range(2):
                        ins = v.tensor_tensor(xs[:, :, c, :], ps[:, 4, :].rearrange("p (h t) -> p h t", h=8),
                                              y_t[:, at].rearrange("p (h t) -> p h t", h=8), ALU.add)
                    ins.then_inc(S["xs_kept"], 1)
                    for g in range(2):
                        dve.wait_ge(S["bv_ready"], FREE + 2 * n + g + 1)
                        for c in range(2):
                            rng = slice(64 * c, 64 * c + 64)
                            vals = ps[rng, 7 * (1 - g), :].rearrange("p (a c j) -> p a c j", c=2, j=HD)[:, :, c, :]
                            dst = v2[rng, bass.ds(i * 1024 + s * 512 + g * 256, 256)]
                            ins = v.tensor_copy(dst.rearrange("p (a j) -> p a j", j=HD), vals)
                        ins.then_inc(S["bv_kept"], 1)

            def attention(a):
                A = att[a]
                items = Count()

                def peaks(c, k):
                    b = 2 * (items.n % 2)
                    dve.wait_ge(A["peak_scores_ready"], items.next())
                    pair = ps[:, b:b + 2, :].rearrange("p a b -> p (a b)")
                    v.tensor_reduce(neg_m[:, c % 2, k:k + 1], pair, AX.X, ALU.max,
                                    negate=True).then_inc(A["peak_bank_free"], 1)
                    if k == 15:
                        dve.wait_ge(A["peak_bank_free"], items.seen() + PCREDIT)
                        rest, parts = m_rest[:, c % 2, :], m_split[:, c % 2]
                        link(v.tensor_copy(parts[:, 0, :], neg_m[:, c % 2, :]))
                        link(v.tensor_tensor(rest, neg_m[:, c % 2, :], parts[:, 0, :], ALU.subtract))
                        link(v.tensor_copy(parts[:, 1, :], rest))
                        link(v.tensor_tensor(rest, rest, parts[:, 1, :], ALU.subtract))
                        v.tensor_copy(parts[:, 2, :], rest).then_inc(A["m_split_ready"], 1)

                def turned(c):
                    b = 2 * (items.n % 2)
                    dve.wait_ge(A["peak_scores_ready"], items.next())
                    v.tensor_copy(m_t[:, c % 2, :], ps[0:PARTS * 16, b, 0:P // 2].bitcast(BF16)).then_inc(
                        A["peak_bank_free"], 1)

                def unit(c, left):
                    plan = peak_plan(left)
                    for s in range(1, KT + 1):
                        for ahead, k in plan[s]:
                            if k is None:
                                turned(c + ahead)
                            else:
                                peaks(c + ahead, k)

                for k in range(16):
                    peaks(0, k)
                turned(0)
                for k in range(16):
                    peaks(1, k)
                peaks(2, 0)
                peaks(2, 1)
                with dve.Fori(0, UNITS // SLOTS - 1) as i:
                    items.enter(i, 17 * SLOTS)
                    link.enter(i, 4 * SLOTS)
                    for c in range(SLOTS):
                        unit(c, 3)
                    link.leave(UNITS // SLOTS - 1)
                    items.leave(UNITS // SLOTS - 1)
                for c in range(SLOTS):
                    unit(c, 3 - c)

            def heads_out(a, b):
                dve.wait_ge(att[a]["out_back"], 64 * (b + 1))
                dve.wait_ge(S["wo_ready"], 2 * (BATCH * a + b))
                link(v.reciprocal(den, den))
                if a == 0:
                    v.tensor_tensor(ctx_t, o_in, den, ALU.mult).then_inc(S["ctx_ready"], 1)
                else:
                    order = lambda x: x.rearrange("p (c t) -> p c t", c=HEADS)
                    v.tensor_tensor(ctx_t.rearrange("p (t c) -> p c t", c=HEADS), order(o_in), order(den),
                                    ALU.mult).then_inc(S["ctx_ready"], 1)

            attention(0)

            for b in range(BATCH):
                heads_out(0, b)
                for s in range(2):
                    n = 2 * b + s
                    at = slice(n * BLK, (n + 1) * BLK)
                    src = lambda j: x3_tok[:, n * BLK + j * P:n * BLK + (j + 1) * P]
                    dve.wait_ge(S["wo_ready"], n + 1)
                    v.tensor_tensor(x3_tok[:, at], x3_tok[:, at], ps[:, n % 2, :], ALU.add).then_inc(S["wo_kept"], 1)
                    dve.wait_ge(S["wo_kept"], n + 1)
                    link(v.tensor_tensor(tiled(x3_tok[:, at]), tiled(x3_tok[:, at]), rep("bo"), ALU.add))
                    stats(src, "o_var")
                    normalise(src, lambda j: stage1[:, s, j * P:(j + 1) * P], "o_sd", n + 1, None)
                    link(v.tensor_tensor(tiled(stage1[:, s, :]), tiled(stage1[:, s, :]), rep("l1g"), ALU.mult))
                    v.tensor_tensor(tiled(stage[:, s, :]), tiled(stage1[:, s, :]), rep("l1b"),
                                    ALU.add).then_inc(S["o_n"], 1)
                    dve.wait_ge(S["o_n"], n + 1)
                    link(v.tensor_copy(x3_tok[:, at], stage[:, s, :]))
            n_e = TILES * EXP
            T = lambda k: tk[:, k, :].rearrange("p (a e) -> p a e", e=EXP)
            one = lambda k: tk[:, k, 0:TILES]
            wide = lambda k: one(k).unsqueeze(2).to_broadcast([P, TILES, EXP])
            rank = cst[:, CST["rank"]:CST["rank"] + EXP].unsqueeze(1).to_broadcast([P, TILES, EXP])
            dve.wait_ge(S["route_ready"], BLOCKS)
            link(v.tensor_copy(tk[:, 0, :], ps[:, 4, 0:n_e]))
            link(v.tensor_reduce(one(1), T(0), AX.X, ALU.max))
            v.tensor_tensor(T(0), T(0), wide(1), ALU.subtract).then_inc(S["route_sum"], 1)
            dve.wait_ge(S["route_exp"], 1)
            link(v.tensor_reduce(one(1), T(2), AX.X, ALU.add))
            link(v.reciprocal(one(1), one(1)))
            link(v.tensor_tensor(T(2), T(2), wide(1), ALU.mult))
            for best, chosen in ((3, 4), (5, 6)):
                link(v.tensor_reduce(one(best), T(2), AX.X, ALU.max))
                link(v.tensor_tensor(T(7), T(2), wide(best), ALU.is_equal))
                link(v.tensor_tensor(T(7), T(7), rank, ALU.mult))
                link(v.tensor_reduce(one(8), T(7), AX.X, ALU.max))
                link(v.tensor_tensor(T(chosen), T(7), wide(8), ALU.is_equal))
                link(v.scalar_tensor_tensor(out=T(2), in0=T(chosen), scalar=-2.0, in1=T(2), op0=ALU.mult,
                                            op1=ALU.add))
            v.tensor_tensor(one(9), one(5), one(3), ALU.subtract).then_inc(S["route_sum"], 1)
            dve.wait_ge(S["route_exp"], 2)
            link(v.tensor_scalar(one(11), one(10), 1.0, None, ALU.add))
            link(v.reciprocal(one(11), one(11)))
            link(v.tensor_tensor(one(10), one(10), one(11), ALU.mult))
            link(v.tensor_tensor(T(4), T(4), wide(11), ALU.mult))
            link(v.tensor_tensor(T(6), T(6), wide(10), ALU.mult))
            v.tensor_tensor(gates[:, :, :], T(4), T(6), ALU.add).then_inc(S["gates_ready"], 1)
            for n in range(BLOCKS):
                at = slice(n * BLK, (n + 1) * BLK)
                dve.wait_ge(S["gt_psum"], n + 1)
                v.tensor_copy(g_t[:, at], ps[0:EXP, n % 2, :]).then_inc(S["gt_kept"], 1)
            for n in range(BLOCKS):
                at = slice(n * BLK, (n + 1) * BLK)
                dve.wait_ge(S["gt_psum"], BLOCKS + n + 1)
                v.tensor_tensor(x3_tok[:, at], x3_tok[:, at], ps[:, 2 + n % 2, :], ALU.add).then_inc(S["gt_kept"], 1)

            dve.wait_ge(S["gt_kept"], 2 * BLOCKS)
            dve.wait_ge(S["gates_ready"], 1)
            with dve.Fori(0, BATCH) as i:
                link.enter(i, 2 * 7)
                for s in range(2):
                    n, at = 2 * i + s, blk(i, s)
                    acc = stage1[:, s, :]
                    v.tensor_copy(acc, x3_tok[:, at])
                    link(v.tensor_copy(gb[:, s, :], gates[:, :, :].rearrange("p a e -> p (a e)")[
                        :, bass.ds(i * (2 * BT * EXP) + s * BT * EXP, BT * EXP)]))
                    for e in range(EXP):
                        dve.wait_ge(S["down_ready"], FREE + EXP * n + e + 1)
                        for j in range(BT):
                            a = acc[:, j * P:(j + 1) * P]
                            ins = v.scalar_tensor_tensor(out=a, in0=ps[:, 4 + e % 2, j * P:(j + 1) * P],
                                                         scalar=gb[:, s, j * EXP + e:j * EXP + e + 1], in1=a,
                                                         op0=ALU.mult, op1=ALU.add)
                        ins.then_inc(S["down_kept"], 1)
                        dve.wait_ge(S["down_kept"], FREE + EXP * n + e + 1)
                    own = lambda j: acc[:, j * P:(j + 1) * P]
                    stats(own, "f_var")
                    dve.wait_ge(S["f_sd"], n + 1)
                    link(v.reciprocal(rs[:, :], sd[:, :]))
                    for j in range(BT):
                        ins = v.tensor_scalar(own(j), own(j), mv[:, j, 0:1], rs[:, j:j + 1], ALU.subtract, ALU.mult)
                    link(ins)
                    link(v.tensor_tensor(tiled(acc), tiled(acc), rep("l2g"), ALU.mult))
                    link(v.tensor_tensor(tiled(acc), tiled(acc), rep("l2b"), ALU.add))
                    link(v.tensor_tensor(x_tok[:, at], x_tok[:, at], acc, ALU.add))
                link.leave(BATCH)

            attention(1)
            for b in range(BATCH):
                heads_out(1, b)
                for s in range(2):
                    n = 2 * BATCH + 2 * b + s
                    at = slice((2 * b + s) * BLK, (2 * b + s + 1) * BLK)
                    dve.wait_ge(S["wo_ready"], n + 1)
                    v.tensor_tensor(x_tok[:, at], x_tok[:, at], ps[:, n % 2, :], ALU.add).then_inc(S["wo_kept"], 1)

        @block.tensor
        def _(pe):
            mm = nc.tensor.matmul

            def turn(bank, src, width=BT):
                for j in range(width):
                    ins = nc.tensor.transpose(ps[:, bank, j * P:(j + 1) * P], src(j), ident)
                return ins

            for n in ("cst", "w0"):
                pe.wait_ge(landed[n], 16 * NDMA[n])
            with pe.Fori(0, BATCH) as i:
                for s in range(2):
                    n = 2 * i + s
                    pe.wait_ge(S["xn_ready"], n + 1)
                    pe.wait_ge(S["k_kept"], FREE + n)
                    turn(0, lambda j: stage[:, s, j * P:(j + 1) * P]).then_inc(S["xn_t_psum"], 1)
                    pe.wait_ge(S["n1_ready"], n + 1)
                    pe.wait_ge(S["q_kept"], FREE + n)
                    turn(1, lambda j: stage1[:, s, j * P:(j + 1) * P]).then_inc(S["n1_t_psum"], 1)
                    pe.wait_ge(S["n1_t_kept"], n + 1)
                    pe.wait_ge(S["qk_scaled"], FREE + n)
                    xt = stage_t[:, s, :]
                    for j in range(BT):
                        ins = mm(ps[:, 2 + j, 0:3 * D], xt[:, j * P:(j + 1) * P], w0[:, 0:3 * D], start=True, stop=True)
                    ins.then_inc(S["qkv_ready"], 1)
                    pe.wait_ge(S["zg_kept"], FREE + n)
                    mm(ps[:, 6, :], w0[:, W0["gate"]:W0["gate"] + P], xt, start=True, stop=True)
                    pe.wait_ge(S["zp_kept"], FREE + n)
                    mm(ps[:, 7, :], w0[:, W0["p"]:W0["p"] + P], xt, start=True, stop=True).then_inc(S["gp_ready"], 1)
                    pe.wait_ge(S["xn_t_kept"], n + 1)
                    mm(ps[:, 0, :], w0[:, W0["clock"]:W0["clock"] + P], xt, start=True, stop=True).then_inc(
                        S["clock_ready"], 1)
                    pe.wait_ge(S["rope_ready"], n + 1)
                    pe.wait_ge(S["zc_kept"], FREE + n + 1)
                    turn(1, lambda j: qk1[:, s, 2 * j * D:(2 * j + 1) * D])
                    turn(0, lambda j: qk1[:, s, (2 * j + 1) * D:(2 * j + 2) * D]).then_inc(S["rope_t_psum"], 1)

            pe.wait_ge(landed["wf"], 16 * NDMA["wf"])
            for n in ("k_kept", "q_kept", "qk_scaled", "zg_kept", "zp_kept"):
                pe.wait_ge(S[n], FREE + BLOCKS)
            pe.wait_ge(S["xn_t_kept"], BLOCKS)
            h0, h1, h2 = flat(hid0), flat(hid1), flat(hid2)
            with pe.Fori(0, BATCH) as i:
                for s in range(2):
                    n = 2 * i + s
                    pe.wait_ge(S["y_done"], FREE + n)
                    for fc in range(FC):
                        pe.wait_ge(S["glu_done"], FREE + 4 * n + (fc - 1 if fc >= 2 else 0))
                        for b, w in ((0, "w1"), (2, "w2")):
                            ins = mm(ps[:, b + fc % 2, :], wf[:, WF[w] + fc * P:WF[w] + (fc + 1) * P], xn_t[:, blk(i, s)],
                                     start=True, stop=True)
                        ins.then_inc(S["z_ready"], 1)
                    for layer, (w, src, ready, done, before) in enumerate((
                            ("h1", h0, "h1_ready", "h1_done", "glu_done"), ("h2", h1, "h2_ready", "h2_done", "h1_done"))):
                        pe.wait_ge(S[before], FREE + 4 * n + 4)
                        for oc in range(FC):
                            pe.wait_ge(S[done], FREE + 4 * n + (oc - 1 if oc >= 2 else 0))
                            for fc in range(FC):
                                at = WF[w] + fc * HID + oc * P
                                ins = mm(ps[:, 4 + 2 * layer + oc % 2, :], wf[:, at:at + P], src[:, fc * BLK:(fc + 1) * BLK],
                                         start=fc == 0, stop=fc == FC - 1)
                            ins.then_inc(S[ready], 1)
                    pe.wait_ge(S["h2_done"], FREE + 4 * n + 4)
                    for j in range(BT):
                        for fc in range(FC):
                            ins = mm(ps[:, 0, j * P:(j + 1) * P], h2[:, fc * BLK + j * P:fc * BLK + (j + 1) * P],
                                     wf[:, WF["w3"] + fc * D:WF["w3"] + (fc + 1) * D], start=fc == 0, stop=fc == FC - 1)
                    ins.then_inc(S["y_ready"], 1)

            pe.wait_ge(S["y_done"], FREE + BLOCKS)
            for n in ("h1_done", "h2_done"):
                pe.wait_ge(S[n], FREE + FC * BLOCKS)
            with pe.Fori(0, BATCH) as i:
                pe.wait_ge(S["batch_staged"], i + 1)

                def scores(qt):
                    pe.wait_ge(S["exp_done"], FREE + KT * i + (qt - 1 if qt >= 2 else 0))
                    width = (qt + 1) * P
                    b, q = 2 * (qt % 2), q_s[:, qt * P:(qt + 1) * P]
                    for c in range((width + 511) // 512):
                        w = min(512, width - 512 * c)
                        mm(ps[:, b + c, 0:w], q, k_s[:, 512 * c:512 * c + w], start=True, stop=c != qt // 4)
                    m = (qt % 4) * P
                    mm(ps[:, b + qt // 4, m:m + P], ident, cst[:, CST["mask"]:CST["mask"] + P], start=False,
                       stop=True).then_inc(S["s_ready"], 1)

                scores(0)
                for qt in range(KT):
                    if qt + 1 < KT:
                        scores(qt + 1)
                    pe.wait_ge(S["p_ready"], KT * i + qt + 1)
                    pe.wait_ge(S["p_t_kept"], FREE + KT * i + qt)
                    for kt in range(qt + 1):
                        ins = nc.tensor.transpose(ps[:, 4 + kt // 4, (kt % 4) * P:(kt % 4 + 1) * P],
                                                  probs[:, qt % 2, kt * P:(kt + 1) * P], ident)
                    ins.then_inc(S["p_t_psum"], 1)
                    pe.wait_ge(S["p_t_kept"], FREE + KT * i + qt + 1)
                    pe.wait_ge(S["av_kept"], FREE + KT * i + qt)
                    for kt in range(qt + 1):
                        ins = mm(ps[:, 6, 0:P], v_s[:, kt * P:(kt + 1) * P], probs_t[:, kt * P:(kt + 1) * P],
                                 start=kt == 0, stop=kt == qt)
                    ins.then_inc(S["av_ready"], 1)
                pe.wait_ge(S["av_kept"], FREE + KT * i + KT)
                for s in range(2):
                    pe.wait_ge(S["x2_kept"], FREE + 2 * i + s)
                    for j in range(BT):
                        t0 = (s * BT + j) * P
                        ins = mm(ps[:, 7, j * P:(j + 1) * P], ao_t[:, t0:t0 + P], w0[:, W0["out"]:W0["out"] + D],
                                 start=True, stop=True)
                    ins.then_inc(S["x2_ready"], 1)

            pe.wait_ge(S["exp_done"], FREE + KT * BATCH)
            pe.wait_ge(S["p_t_kept"], FREE + KT * BATCH)
            with pe.Fori(0, BATCH) as i:
                for s in range(2):
                    n = 2 * i + s
                    pe.wait_ge(S["m_n"], n + 1)
                    pe.wait_ge(S["m_t_kept"], FREE + n)
                    turn(0, lambda j: stage[:, s, j * P:(j + 1) * P]).then_inc(S["m_t_psum"], 1)
                    pe.wait_ge(S["m_t_kept"], FREE + n + 1)
                    pe.wait_ge(S["m1_done"], FREE + 4 * n)
                    for fc in range(FC):
                        at = W0["m1"] + fc * P
                        mm(ps[:, 1 + fc, :], w0[:, at:at + P], stage_t[:, s, :], start=True, stop=True).then_inc(
                            S["m1_ready"], 1)
                    pe.wait_ge(S["m1_done"], FREE + 4 * n + 4)
                    pe.wait_ge(S["m2_kept"], FREE + n)
                    for j in range(BT):
                        for fc in range(FC):
                            at = W0["m2"] + fc * D
                            ins = mm(ps[:, 5, j * P:(j + 1) * P], h0[:, fc * BLK + j * P:fc * BLK + (j + 1) * P],
                                     w0[:, at:at + D], start=fc == 0, stop=fc == FC - 1)
                    ins.then_inc(S["m2_ready"], 1)

            pe.wait_ge(landed["w1"], 16 * NDMA["w1"])
            pe.wait_ge(S["m_t_kept"], FREE + BLOCKS)
            pe.wait_ge(S["m1_done"], FREE + FC * BLOCKS)
            wcol = lambda name, n=P: w1[:, W1[name]:W1[name] + n]
            with pe.Fori(0, BATCH) as i:
                for s in range(2):
                    n = 2 * i + s
                    pe.wait_ge(S["l_n"], n + 1)
                    pe.wait_ge(S["l_t_kept"], FREE + n)
                    turn(0, lambda j: stage[:, s, j * P:(j + 1) * P]).then_inc(S["l_t_psum"], 1)
                    pe.wait_ge(S["l_t_kept"], FREE + n + 1)
                    for m, w in enumerate(("q", "k")):
                        pe.wait_ge(S["parts_kept"], FREE + 2 * n)
                        mm(ps[:, 1 + m, :], wcol(w), stage_t[:, s, :], start=True, stop=True).then_inc(S["lq_ready"], 1)
                    pe.wait_ge(S["lv_kept"], FREE + n)
                    for j in range(BT):
                        ins = mm(ps[:, 3, j * P:(j + 1) * P], stage_t[:, s, j * P:(j + 1) * P], wcol("v"),
                                 start=True, stop=True)
                    ins.then_inc(S["lv_ready"], 1)
            pe.wait_ge(S["conv_done"], BATCH)
            pe.wait_ge(S["l_t_kept"], FREE + BLOCKS)
            with pe.Fori(0, BATCH) as i:
                for s in range(2):
                    n = 2 * i + s
                    pe.wait_ge(S["xs_kept"], FREE + n)
                    mm(ps[:, 4, :], wcol("pe"), y_t[:, blk(i, s)], start=True, stop=True).then_inc(S["pe_ready"], 1)
                    pe.wait_ge(S["xs_kept"], FREE + n + 1)
                    for m in range(2):
                        pe.wait_ge(S["bq_kept"], FREE + 2 * n)
                        at = W1["qkv"] + m * P
                        mm(ps[:, 5 + m, :].rearrange("p (h t) -> p h t", h=8), w1[:, at:at + P], xs[:, :, 0, :],
                           start=True, stop=True).then_inc(S["bq_ready"], 1)
                    for g in range(2):
                        pe.wait_ge(S["bv_kept"], FREE + 2 * n)
                        at = W1["qkv"] + 2 * P
                        for h in range(4):
                            ins = mm(ps[:, 7 * (1 - g), h * D:(h + 1) * D], xs[:, 4 * g + h, :, :].rearrange(
                                "p c t -> p (c t)"), w1[:, at:at + P], start=True, stop=True)
                        ins.then_inc(S["bv_ready"], 1)

            def attention(a):
                A = att[a]
                items = Count()

                def peaks(i, c, k):
                    sl = slot[c % SLOTS]
                    if k == 0:
                        use = i + c // SLOTS
                        pe.wait_ge(A["qk_loaded"][c % SLOTS], 64 * (use + 1))
                        pe.wait_ge(A["rows_zeroed"], SLOTS * i + c + 1)
                    b = 2 * (items.n % 2)
                    pe.wait_ge(A["peak_bank_free"], items.next())
                    h, qt = k // KT, k % KT
                    for f in range(2):
                        at = h * SEQ + f * 512
                        ins = mm(ps[:, b + f, :], sl[:, 0, h * SEQ + qt * P:h * SEQ + (qt + 1) * P],
                                 sl[:, 1, at:at + 512], start=True, stop=True)
                    ins.then_inc(A["peak_scores_ready"], 1)

                def turn_maxima(i, c):
                    b = 2 * (items.n % 2)
                    wait_apart(pe, A["m_split_ready"], SLOTS * i + c + 1)
                    wait_apart(pe, A["peak_bank_free"], items.next())
                    nc.tensor.transpose(ps[0:PARTS * 16, b, 0:P // 2].bitcast(BF16),
                                        m_split[:, c % 2].rearrange("p a k -> p (a k)"), ident_b[:, :]).then_inc(
                        A["peak_scores_ready"], 1)

                def scores(i, c, s, tiles):
                    sl = slot[c % SLOTS]
                    if s == 0 and 0 in tiles:
                        pe.wait_ge(A["m_loaded"][c % SLOTS], 16 * (i + c // SLOTS + 1))
                    for q in tiles:
                        tile = 32 * c + 4 * s + q
                        pe.wait_ge(A["probs_done"], 32 * SLOTS * i + tile + 1 - (2 if q % 2 else 4) + CREDIT)
                        h, half = q // 2, q % 2
                        mm(ps[:, SCORE_BANK[q], :], sl[:, 1, h * SEQ + s * P:h * SEQ + (s + 1) * P],
                           sl[:, 0, h * SEQ + half * 512:h * SEQ + (half + 1) * 512],
                           start=True, stop=True).then_inc(A["scores_ready"], 1)

                def sums(i, c, s):
                    if s == 0:
                        pe.wait_ge(A["va_ready"], SLOTS * i + c + 1)
                        pe.wait_ge(A["out_kept"], FREE + SLOTS * i + c)
                    pe.wait_ge(A["probs_done"], 32 * SLOTS * i + 32 * c + 4 * s + 4 + CREDIT)
                    vals = values(a, c)
                    for q in range(4):
                        h = q // 2
                        ins = mm(ps[32 * q:32 * q + 32, 7, :], vals[:, (h * KT + s) * 32:(h * KT + s + 1) * 32],
                                 probabilities(a, s)[:, q * 512:(q + 1) * 512], start=s == 0, stop=s == KT - 1)
                    ins.then_inc(A["av_steps"], 1)

                def unit(i, c, left):
                    plan = peak_plan(left)
                    for s in range(1, KT + 1):
                        def step(tiles):
                            if s < KT:
                                scores(i, c, s, tiles)
                            elif left:
                                scores(i, c + 1, 0, tiles)

                        def for_maxima(items_):
                            for ahead, k in items_:
                                if k is None:
                                    turn_maxima(i, c + ahead)
                                else:
                                    peaks(i, c + ahead, k)

                        step((0, 1))
                        for_maxima(plan[s][:1])
                        step((2,))
                        if a == 0:
                            for_maxima(plan[s][1:])
                            step((3,))
                            sums(i, c, s - 1)
                        else:
                            sums(i, c, s - 1)
                            step((3,))
                            for_maxima(plan[s][1:])

                for k in range(16):
                    peaks(0, 0, k)
                turn_maxima(0, 0)
                for k in range(16):
                    peaks(0, 1, k)
                peaks(0, 2, 0)
                peaks(0, 2, 1)
                scores(0, 0, 0, range(4))
                with pe.Fori(0, UNITS // SLOTS - 1) as i:
                    items.enter(i, 17 * SLOTS)
                    for c in range(SLOTS):
                        unit(i, c, 3)
                    items.leave(UNITS // SLOTS - 1)
                for c in range(SLOTS):
                    unit(UNITS // SLOTS - 1, c, 3 - c)

            def project(a, b, w):
                pe.wait_ge(S["ctx_ready"], BATCH * a + b + 1)
                for s in range(2):
                    n = 2 * (BATCH * a + b) + s
                    if n >= 2:
                        pe.wait_ge(S["wo_kept"], n - 1)
                    for j in range(BT):
                        t0 = (s * BT + j) * P
                        ins = mm(ps[:, n % 2, j * P:(j + 1) * P], ctx_t[:, t0:t0 + P], wcol(w), start=True, stop=True)
                    ins.then_inc(S["wo_ready"], 1)

            pe.wait_ge(S["parts_kept"], FREE + 2 * BLOCKS)
            pe.wait_ge(S["lv_kept"], FREE + BLOCKS)
            pe.wait_ge(S["bq_kept"], FREE + 2 * BLOCKS)
            pe.wait_ge(S["bv_kept"], FREE + 2 * BLOCKS)
            attention(0)

            for b in range(BATCH):
                project(0, b, "o")
                for s in range(2):
                    n = 2 * b + s
                    pe.wait_ge(S["o_n"], n + 1)
                    if n:
                        pe.wait_ge(S["o_t_kept"], n)
                    turn(2, lambda j: stage[:, s, j * P:(j + 1) * P]).then_inc(S["o_t_psum"], 1)
                    pe.wait_ge(S["o_t_kept"], n + 1)
                    for j in range(BT):
                        at = (n * BT + j) * EXP
                        ins = mm(ps[:, 4, at:at + EXP], stage_t[:, s, j * P:(j + 1) * P], wcol("r", EXP),
                                 start=True, stop=True)
                    ins.then_inc(S["route_ready"], 1)
            pe.wait_ge(S["gates_ready"], 1)
            pe.wait_ge(S["wo_kept"], 2 * BATCH)
            for n in range(BLOCKS):
                if n >= 2:
                    pe.wait_ge(S["gt_kept"], n - 1)
                for j in range(BT):
                    ins = nc.tensor.transpose(ps[0:EXP, n % 2, j * P:(j + 1) * P], gates[:, n * BT + j, :], ident)
                ins.then_inc(S["gt_psum"], 1)
            for n in range(BLOCKS):
                pe.wait_ge(S["gt_kept"], BLOCKS + (n - 1 if n >= 2 else 0))
                for j in range(BT):
                    t0 = (n * BT + j) * P
                    ins = mm(ps[:, 2 + n % 2, j * P:(j + 1) * P], g_t[:, t0:t0 + P], be2[:, :], start=True, stop=True)
                ins.then_inc(S["gt_psum"], 1)

            for n in ("we1", "we2"):
                pe.wait_ge(landed[n], 16 * NDMA[n])
            pe.wait_ge(S["gt_kept"], 2 * BLOCKS)
            pe.wait_ge(S["o_t_kept"], BLOCKS)
            with pe.Fori(0, BATCH) as i:
                for s in range(2):
                    n = 2 * i + s

                    def up(e):
                        for fc in range(FC):
                            pe.wait_ge(S["up_done"], FREE + 4 * EXP * n + (4 * e - 3 + fc if e else 0))
                            at = (e * FC + fc) * P
                            mm(ps[:, fc, :], we1[:, at:at + P], o1_t[:, blk(i, s)], start=True, stop=True).then_inc(
                                S["up_ready"], 1)

                    def down(e):
                        pe.wait_ge(S["up_done"], FREE + 4 * (EXP * n + e + 1))
                        pe.wait_ge(S["down_kept"], FREE + EXP * n + (e - 1 if e >= 2 else 0))
                        h = flat((hid0, hid1)[e % 2])
                        for j in range(BT):
                            for fc in range(FC):
                                at = (e * FC + fc) * D
                                ins = mm(ps[:, 4 + e % 2, j * P:(j + 1) * P], h[:, fc * BLK + j * P:fc * BLK + (j + 1) * P],
                                         we2[:, at:at + D], start=fc == 0, stop=fc == FC - 1)
                        ins.then_inc(S["down_ready"], 1)

                    up(0)
                    for e in range(EXP):
                        if e + 1 < EXP:
                            up(e + 1)
                        down(e)

            pe.wait_ge(S["up_done"], FREE + 4 * EXP * BLOCKS)
            pe.wait_ge(S["down_kept"], FREE + EXP * BLOCKS)
            attention(1)
            for b in range(BATCH):
                project(1, b, "ao")

        @block.scalar
        def _(act):
            link = Chain(act, act_seq, wait_apart)
            fn = nc.scalar.activation

            def root(ready, n, eps, done):
                act.wait_ge(S[ready], n)
                fn(sd[:, :], mv[:, :, 1], ACT.Sqrt, bias=eps).then_inc(S[done], 1)

            act.wait_ge(landed["cols"], 16 * NDMA["cols"])
            act.wait_ge(S["consts"], 4)
            with act.Fori(0, BATCH) as i:
                link.enter(i, 4)
                for s in range(2):
                    n, at = 2 * i + s, blk(i, s)
                    root("var_ready", 2 * n + 1, eps0, "sd_ready")
                    root("var_ready", 2 * n + 2, eps0, "sd_ready")
                    act.wait_ge(S["xn_t_psum"], n + 1)
                    fn(xn_t[:, at], ps[:, 0, :], ACT.Copy).then_inc(S["xn_t_kept"], 1)
                    act.wait_ge(S["n1_t_psum"], n + 1)
                    fn(stage_t[:, s, :], ps[:, 1, :], ACT.Identity, scale=col("g1"), bias=col("b1")).then_inc(
                        S["n1_t_kept"], 1)
                    act.wait_ge(S["qkv_ready"], n + 1)
                    for j in range(BT):
                        for h in range(2):
                            m = 2 * j + h
                            ins = fn(qk2[:, s, m * D:(m + 1) * D], ps[:, 2 + j, h * D:(h + 1) * D], ACT.Square,
                                     accum_out=ss[:, m:m + 1])
                    link(ins)
                    link.mark(fn(tiled(v_tok[:, at]), ps[:, 2:2 + BT, 2 * D:3 * D], ACT.Copy))
                    fn(nrm[:, :], ss[:, :], ACT.Sqrt).then_inc(S["nrm_ready"], 1)
                    act.wait_ge(S["gp_ready"], n + 1)
                    fn(zg[:, at], ps[:, 6, :], ACT.Identity, bias=col("gate_b")).then_inc(S["zg_kept"], 1)
                    fn(zp[:, at], ps[:, 7, :], ACT.Identity, bias=col("p_b")).then_inc(S["zp_kept"], 1)
                    act.wait_ge(S["clock_ready"], n + 1)
                    fn(zc[:, at], ps[:, 0, :], ACT.Identity, bias=col("clock_b")).then_inc(S["zc_kept"], 1)
                    act.wait_ge(S["rope_t_psum"], n + 1)
                    fn(q_t[:, at], ps[:, 1, :], ACT.Copy).then_inc(S["q_kept"], 1)
                    fn(k_t[:, at], ps[:, 0, :], ACT.Copy).then_inc(S["k_kept"], 1)
                link.leave(BATCH)

            for n in ("zg_kept", "zp_kept", "zc_kept"):
                act.wait_ge(S[n], FREE + BLOCKS)
            with act.Fori(0, BATCH) as i:
                link.enter(i, 4)
                for s in range(2):
                    n, at = 2 * i + s, blk(i, s)
                    for fc in range(FC):
                        act.wait_ge(S["z_ready"], 4 * n + fc + 1)
                        act.wait_ge(S["glu_done"], FREE + 4 * n + (fc - 1 if fc >= 2 else 0))
                        fn(sil[:, fc % 2, :], ps[:, fc % 2, :], ACT.Silu, scale=col("s1", fc)).then_inc(S["sil_done"], 1)
                    act.wait_ge(S["pm_ready"], i + 1)
                    fn(tmp[:, at], zg[:, at], ACT.Abs)
                    link.apart(fn(tmp2[:, at], zc[:, at], ACT.Abs))
                    fn(tmp[:, at], tmp[:, at], ACT.Exp, scale=-1.0)
                    fn(tmp2[:, at], tmp2[:, at], ACT.Exp, scale=-1.0)
                    link.apart(fn(zp[:, at], zp[:, at], ACT.Exp, bias=pm[:, 0:1]))
                    fn(tmp[:, at], tmp[:, at], ACT.Ln, bias=1.0)
                    fn(tmp2[:, at], tmp2[:, at], ACT.Ln, bias=1.0).then_inc(S["logs_ready"], 1)
                    for layer, (ready, done, free, dst, scales) in enumerate((
                            ("h1_ready", "h1_done", "h2_ready", hid1, "t1"), ("h2_ready", "h2_done", "y_ready", hid2, "t2"))):
                        act.wait_ge(S[free], FREE + (1 if layer else 4) * n)
                        for oc in range(FC):
                            act.wait_ge(S[ready], FREE + 4 * n + oc + 1)
                            fn(flat(dst)[:, oc * BLK:(oc + 1) * BLK], ps[:, 4 + 2 * layer + oc % 2, :], ACT.Gelu,
                               scale=col(scales, oc)).then_inc(S[done], 1)
                        if layer == 0:
                            wait_apart(act, S["decay_ready"], n + 1)
                            fn(zg[:, at], tmp[:, at], ACT.Exp).then_inc(S["decay_exp"], 1)
                link.leave(BATCH)

            with act.Fori(0, BATCH) as i:
                def exps(qt):
                    act.wait_ge(S["peak_ready"], KT * i + qt + 1)
                    act.wait_ge(S["p_t_psum"], FREE + KT * i + (qt - 1 if qt >= 2 else 0))
                    pair = ps[:, 2 * (qt % 2):2 * (qt % 2) + 2, :].rearrange("p a b -> p (a b)")
                    fn(probs[:, qt % 2, 0:(qt + 1) * P], pair[:, 0:(qt + 1) * P], ACT.Exp, scale=1.0 / math.sqrt(D),
                       bias=nm[:, 2 + qt % 2:3 + qt % 2], accum_out=sm[:, qt % 2:qt % 2 + 1]).then_inc(S["exp_done"], 1)

                exps(0)
                for qt in range(KT):
                    if qt + 1 < KT:
                        exps(qt + 1)
                    act.wait_ge(S["p_t_psum"], FREE + KT * i + qt + 1)
                    act.wait_ge(S["av_ready"], FREE + KT * i + qt)
                    fn(probs_t[:, 0:(qt + 1) * P], ps[:, 4:6, :].rearrange("p a b -> p (a b)")[:, 0:(qt + 1) * P],
                       ACT.Copy).then_inc(S["p_t_kept"], 1)

            with act.Fori(0, BATCH) as i:
                for s in range(2):
                    n = 2 * i + s
                    root("m_var", n + 1, eps0, "m_sd")
                    act.wait_ge(S["m_t_psum"], n + 1)
                    fn(stage_t[:, s, :], ps[:, 0, :], ACT.Identity, scale=col("g2"), bias=col("b2")).then_inc(
                        S["m_t_kept"], 1)
                    act.wait_ge(S["m2_ready"], FREE + n)
                    for fc in range(FC):
                        act.wait_ge(S["m1_ready"], 4 * n + fc + 1)
                        fn(flat(hid0)[:, fc * BLK:(fc + 1) * BLK], ps[:, 1 + fc, :], ACT.Gelu,
                           bias=col("mb1", fc)).then_inc(S["m1_done"], 1)

            with act.Fori(0, BATCH) as i:
                for s in range(2):
                    n, at = 2 * i + s, blk(i, s)
                    root("l_var", n + 1, eps0, "l_sd")
                    act.wait_ge(S["l_t_psum"], n + 1)
                    fn(x3_t[:, at], ps[:, 0, :], ACT.Copy)
                    fn(stage_t[:, s, :], ps[:, 0, :], ACT.Copy).then_inc(S["l_t_kept"], 1)
                    for m, parts in enumerate((q_parts, k_parts)):
                        act.wait_ge(S["lq_ready"], 2 * n + m + 1)
                        fn(parts[:, 0, at], ps[:, 1 + m, :], ACT.Copy).then_inc(S["hi_kept"], 1)
                    act.wait_ge(S["lv_ready"], n + 1)
                    for j in range(BT):
                        dst = v1[:, bass.ds(i * SEQ, SEQ)].rearrange("p (u h k j) -> p u h k j", u=8, h=2, k=KT)
                        ins = fn(dst[:, :, :, 4 * s + j, :], ps[:, 3, j * P:(j + 1) * P].rearrange(
                            "p (u h j) -> p u h j", u=8, h=2), ACT.Copy)
                    ins.then_inc(S["lv_kept"], 1)
            with act.Fori(0, BATCH) as i:
                for s in range(2):
                    n, at = 2 * i + s, blk(i, s)
                    for m, dst in enumerate((q_b, k_b)):
                        act.wait_ge(S["bq_ready"], 2 * n + m + 1)
                        fn(dst[:, at], ps[:, 5 + m, :], ACT.Copy).then_inc(S["bq_kept"], 1)

            def attention(a):
                A = att[a]

                def exps(i, c, s):
                    act.wait_ge(A["av_steps"], SLOTS * KT * i + KT * c + s - 1 + PCREDIT)
                    for q in range(4):
                        act.wait_ge(A["scores_ready"], 32 * SLOTS * i + 32 * c + 4 * s + q + 1)
                        fn(probabilities(a, s)[:, q * 512:(q + 1) * 512], ps[:, SCORE_BANK[q], :], ACT.Exp,
                           scale=HEAD_SCALE[a]).then_inc(A["probs_done"], 1)

                def keep(i, c):
                    act.wait_ge(A["av_steps"], SLOTS * KT * i + KT * (c + 1) + PCREDIT)
                    act.wait_ge(A["out_stored"][c % 2], FREE + 16 * (SLOTS // 2 * i + c // 2))
                    fn(o_st[c % 2], ps[:, 7, :], ACT.Copy).then_inc(A["out_kept"], 1)

                def unit(i, c, left):
                    for s in range(1, KT):
                        exps(i, c, s)
                    if left:
                        exps(i, c + 1, 0)
                    keep(i, c)

                exps(0, 0, 0)
                with act.Fori(0, UNITS // SLOTS - 1) as i:
                    for c in range(SLOTS):
                        unit(i, c, 3)
                for c in range(SLOTS):
                    unit(UNITS // SLOTS - 1, c, 3 - c)

            act.wait_ge(parts_stored, 16 * N_PARTS)
            attention(0)

            for n in range(BLOCKS):
                s = n % 2
                root("o_var", n + 1, eps1, "o_sd")
                act.wait_ge(S["o_t_psum"], n + 1)
                fn(o1_t[:, n * BLK:(n + 1) * BLK], ps[:, 2, :], ACT.Copy)
                fn(stage_t[:, s, :], ps[:, 2, :], ACT.Copy).then_inc(S["o_t_kept"], 1)
            act.wait_ge(S["route_sum"], 1)
            fn(tk[:, 2, :], tk[:, 0, :], ACT.Exp).then_inc(S["route_exp"], 1)
            act.wait_ge(S["route_sum"], 2)
            fn(tk[:, 10, 0:TILES], tk[:, 9, 0:TILES], ACT.Exp).then_inc(S["route_exp"], 1)

            with act.Fori(0, BATCH) as i:
                for s in range(2):
                    n = 2 * i + s
                    for e in range(EXP):
                        act.wait_ge(S["down_ready"], FREE + EXP * n + (e - 1 if e >= 2 else 0))
                        for fc in range(FC):
                            act.wait_ge(S["up_ready"], 4 * EXP * n + 4 * e + fc + 1)
                            fn(flat((hid0, hid1)[e % 2])[:, fc * BLK:(fc + 1) * BLK], ps[:, fc, :], ACT.Gelu,
                               bias=col("be1", e * FC + fc)).then_inc(S["up_done"], 1)
                    root("f_var", n + 1, eps1, "f_sd")

            attention(1)

        @block.gpsimd
        def _(pool):
            g = nc.gpsimd
            for semaphore in free_at_start:
                pool.sem_inc(semaphore, FREE)
            g.memset(eps0, EPS0).then_inc(S["consts"], 1)
            g.memset(eps1, EPS1).then_inc(S["consts"], 1)
            g.memset(one_col[:, :], 1.0).then_inc(S["consts"], 1)
            pool.wait_ge(landed["cst"], 16 * NDMA["cst"])
            g.tensor_copy(ident_b[:, :], ident).then_inc(S["consts"], 1)

            def attention(a):
                A = att[a]
                pool.sem_inc(A["probs_done"], CREDIT)
                pool.sem_inc(A["peak_bank_free"], PCREDIT)
                pool.sem_inc(A["av_steps"], PCREDIT)
                for n in range(SLOTS):
                    g.memset(r[5 + n], 0.0).then_inc(pool_seq, 1)
                pool.wait_ge(pool_seq, (SLOTS + 2) * a + SLOTS)
                for n in range(SLOTS):
                    g.memset(slot[n][MROW:MROW + PARTS, 1, :], 1.0).then_inc(A["slots_ready"], 1)
                pool.wait_ge(A["slots_ready"], SLOTS)
                for n in range(2):
                    g.memset(values(a, n), 1.0).then_inc(pool_seq, 1)
                pool.wait_ge(pool_seq, (SLOTS + 2) * a + SLOTS + 2)

                def values_of(i, c):
                    src = v1 if a == 0 else v2
                    g.tensor_copy(values(a, c).rearrange("p (m w) -> p m w", w=32)[:, :, 0:HD],
                                  src[:, bass.ds(i * (SLOTS * P) + c * P, P)].rearrange("p (m j) -> p m j", j=HD)).then_inc(
                        A["va_ready"], 1)

                def unit(i, c, left):
                    if left:
                        pool.wait_ge(A["rows_zeroed"], SLOTS * i + c + SLOTS if left > 3 else UNITS)
                        pool.wait_ge(A["av_steps"], SLOTS * KT * i + KT * c + PCREDIT)
                        values_of(i, c + 1)
                    if left > 3:
                        pool.wait_ge(A["va_ready"], SLOTS * i + c + 2)
                        wait_apart(pool, A["av_steps"], SLOTS * KT * i + KT * (c + 1) + PCREDIT)
                        g.memset(slot[c][MROW:MROW + PARTS, 0, :], 0.0).then_inc(A["rows_zeroed"], 1)

                pool.sem_inc(A["rows_zeroed"], SLOTS)
                values_of(0, 0)
                with pool.Fori(0, UNITS // SLOTS - 1) as i:
                    for c in range(SLOTS):
                        unit(i, c, 4)
                for c in range(SLOTS):
                    unit(UNITS // SLOTS - 1, c, 3 - c)

            pool.wait_ge(parts_stored, 16 * N_PARTS)
            pool.wait_ge(S["bv_kept"], FREE + 2 * BLOCKS)
            attention(0)
            pool.wait_ge(S["ctx_ready"], 1)
            attention(1)

        @block.sync
        def _(sp):
            def load(name, dst, src):
                sp.dma_start(dst, src).then_inc(landed[name], 16)

            xv = t["L0_attn_x"].rearrange("b (n p) d -> p (b n) d", p=P)
            xt3 = x_tok.rearrange("p (n d) -> p n d", d=D)
            for n in range(BLOCKS):
                load("x", xt3[:, n * BT:(n + 1) * BT, :], xv[:, n * BT:(n + 1) * BT, :])
            load("cst", cst[:, :], t["consts"])
            load("cols", cols[:, :], t["cols"])
            for m, name in enumerate(("L0_attn_out_b", "L0_attn_mlp_b2", "L0_ffn_w3_s", "L1_ffn_bo", "L1_ffn_ln1_g",
                                      "L1_ffn_ln1_b", "L1_ffn_ln2_g", "L1_ffn_ln2_b")):
                load("rows", rows[:, m, :], t[name].partition_broadcast(P))
            load("w0", w0[:, :], t["w0"])
            load("wf", wf[:, :], t["wf"])
            load("w1", w1[:, :], t["w1"])
            load("we1", we1[:, :].rearrange("p (e f) -> p e f", e=EXP), t["L1_ffn_We1"].rearrange("e d f -> d e f"))
            load("we2", we2[:, :].rearrange("p (e c d) -> p e c d", e=EXP, c=FC),
                 t["L1_ffn_We2"].rearrange("e (c p) d -> p e c d", p=P))
            load("we2", be2[:, :], t["L1_ffn_be2"])

            sp.wait_ge(S["parts_kept"], FREE + 2 * BLOCKS)
            for dram, parts, order in ((qs_dram, q_parts, Q_PARTS), (ks_dram, k_parts, K_PARTS)):
                for m, part in enumerate(order):
                    sp.dma_start(dram[m].rearrange("b p t -> p b t"),
                                 parts[:, part, :].rearrange("p (b t) -> p b t", b=BATCH)).then_inc(parts_stored, 16)
            sp.wait_ge(S["bq_kept"], FREE + 2 * BLOCKS)
            sp.dma_start(qb_dram, q_b).then_inc(parts_stored, 16)
            sp.dma_start(kb_dram, k_b).then_inc(parts_stored, 16)

            def attention(a):
                A = att[a]
                if a == 0:
                    heads = [d.rearrange("m b (u h j) t -> (b u) h m j t", u=8, h=2) for d in (qs_dram, ks_dram)]
                    n_rows = len(Q_PARTS) * HD
                else:
                    heads = [d.rearrange("(c j) (u h t) -> u h j c t", c=HEADS, h=2, t=64) for d in (qb_dram, kb_dram)]
                    n_rows = HD

                def fetch(i, c):
                    for m in range(2):
                        for h in range(2):
                            sp.dma_start(slot[c % SLOTS][0:n_rows, m, h * SEQ:(h + 1) * SEQ],
                                         one_of(heads[m], i * SLOTS + c)[h]).then_inc(A["qk_loaded"][c % SLOTS], 16)

                items = Count()

                def maxima(c):
                    sp.wait_ge(A["peak_bank_free"], items.seen() + PCREDIT)
                    sp.dma_start(slot[c % SLOTS][MROW:MROW + PARTS, 0, :].rearrange("p (k q) -> p k q", q=P),
                                 m_t[:, c % 2, :]).then_inc(A["m_loaded"][c % SLOTS], 16)

                def unit(i, c, left):
                    for s in range(1, KT + 1):
                        for ahead, k in peak_plan(min(left, 3))[s]:
                            items.next()
                            if k is None:
                                maxima(c + ahead)
                    sp.wait_ge(A["av_steps"], SLOTS * KT * i + KT * (c + 1) + PCREDIT)
                    if left > 3:
                        fetch(i, c + SLOTS)
                    sp.wait_ge(A["out_kept"], FREE + SLOTS * i + c + 1)
                    sp.dma_start(one_of(o_dram[a], i * SLOTS + c), o_st[c % 2]).then_inc(A["out_stored"][c % 2], 16)

                sp.wait_ge(A["slots_ready"], SLOTS)
                for c in range(SLOTS):
                    fetch(0, c)
                for k in range(17):
                    items.next()
                maxima(0)
                for k in range(18):
                    items.next()
                with sp.Fori(0, UNITS // SLOTS - 1) as i:
                    items.enter(i, 17 * SLOTS)
                    for c in range(SLOTS):
                        unit(i, c, 4)
                    items.leave(UNITS // SLOTS - 1)
                for c in range(SLOTS):
                    unit(UNITS // SLOTS - 1, c, 3 - c)
                for n in range(2):
                    sp.wait_ge(A["out_stored"][n], FREE + 16 * UNITS // 2)
                for b in range(BATCH):
                    if b:
                        sp.wait_ge(S["ctx_ready"], BATCH * a + b)
                    src = o_dram[a][b * 8:(b + 1) * 8].rearrange("u (h q m) t -> u h m q t", h=2, q=2)
                    for q in range(2):
                        at = slice(512 * q, 512 * (q + 1))
                        sp.dma_start(o_in[:, at], src[:, :, 0:HD, q]).then_inc(A["out_back"], 16)
                        sp.dma_start(den[:, at], src[:, :, HD:2 * HD, q]).then_inc(A["out_back"], 16)

            sp.wait_ge(parts_stored, 16 * N_PARTS)
            attention(0)
            attention(1)
            ov = out.rearrange("b (n p) d -> p (b n) d", p=P)
            for n in range(BLOCKS):
                sp.wait_ge(S["wo_kept"], 2 * BATCH + n + 1)
                sp.dma_start(ov[:, n * BT:(n + 1) * BT, :], xt3[:, n * BT:(n + 1) * BT, :]).then_inc(stored, 16)
            sp.wait_ge(stored, 16 * BLOCKS)


def laid_out(x):
    n = lambda k: np.asarray(x[k])
    chunks = lambda w: w.reshape(-1, P, w.shape[1]).transpose(1, 0, 2).reshape(P, -1)
    vec = lambda v: v.reshape(-1, P).T
    clock = np.repeat(n("L0_attn_clock_W"), P, axis=1)
    w0 = [n("L0_attn_Wq"), n("L0_attn_Wk"), n("L0_attn_Wv"), n("L0_attn_gate_W"), n("L0_attn_p_W"), clock,
          n("L0_attn_out_W"), n("L0_attn_mlp_W1"), chunks(n("L0_attn_mlp_W2"))]
    wf = [n("L0_ffn_w1_w").T, n("L0_ffn_w2_w").T, chunks(n("L0_ffn_h1_w").T), chunks(n("L0_ffn_h2_w").T),
          chunks(n("L0_ffn_w3_w").T)]
    w1 = [n("L1_attn_pe_w").T, n("L1_attn_qkv_w").T, n("L1_attn_out_w").T, n("L1_ffn_Wq"), n("L1_ffn_Wk"),
          n("L1_ffn_Wv"), n("L1_ffn_Wo"), n("L1_ffn_Wr")]
    cols = [vec(n("L0_attn_gate_b")), vec(n("L0_attn_p_b")), np.repeat(n("L0_attn_clock_b"), P)[:, None]]
    cols += [vec(n("L0_attn_" + k)) for k in ("ln1_g", "ln1_b", "ln2_g", "ln2_b", "mlp_b1")]
    cols += [vec(n("L0_ffn_" + k)) for k in ("w1_s", "w2_s", "h1_s", "h2_s")]
    cols += [vec(n("L1_ffn_be1")), n("L1_attn_conv_w")[:, 0, :, 1]]
    return {"w0": np.concatenate(w0, 1), "wf": np.concatenate(wf, 1), "w1": np.concatenate(w1, 1),
            "cols": np.concatenate(cols, 1)}


def constants():
    half = D // 2
    freqs = np.exp(-np.arange(half, dtype=np.float32) * np.float32(math.log(10000.0) / half)).astype(np.float32)
    th = np.arange(SEQ, dtype=np.float32)[:, None] * freqs[None, :]
    c = np.repeat(np.cos(th.astype(np.float64)), 2, axis=1)
    s = np.stack([-np.sin(th.astype(np.float64)), np.sin(th.astype(np.float64))], -1).reshape(SEQ, D)
    tiles = lambda a: a.reshape(KT, P, D).transpose(1, 0, 2).reshape(P, KT * D)
    above = np.triu(np.ones((P, P)), 1) * -3e38
    rank = np.broadcast_to(np.arange(EXP, 0, -1), (P, EXP))
    return np.concatenate([np.eye(P), above, tiles(c), tiles(s), rank], 1).astype(np.float32)


_PLAIN = ["L0_attn_x", "L0_attn_out_b", "L0_attn_mlp_b2", "L0_ffn_w3_s", "L1_ffn_bo", "L1_ffn_ln1_g", "L1_ffn_ln1_b",
          "L1_ffn_ln2_g", "L1_ffn_ln2_b", "L1_ffn_We1", "L1_ffn_We2", "L1_ffn_be2"]


def kernel(**inputs):
    import concourse.bacc as bacc
    from concourse.bass_utils import run_bass_kernel_spmd

    arrays = {k: np.ascontiguousarray(inputs[k]) for k in _PLAIN}
    arrays |= {k: np.ascontiguousarray(a) for k, a in laid_out(inputs).items()}
    arrays["consts"] = constants()
    nc = bacc.Bacc("TRN2", target_bir_lowering=False, num_devices=1)
    t = {k: nc.dram_tensor("in_" + k, a.shape, mybir.dt.from_np(a.dtype), kind="ExternalInput").ap()
         for k, a in arrays.items()}
    out = nc.dram_tensor("out", (BATCH, SEQ, D), F32, kind="ExternalOutput").ap()
    build(nc, t, out)
    r = run_bass_kernel_spmd(nc, [{"in_" + k: a for k, a in arrays.items()}], core_ids=[0])
    return r.results[0]["out"]
```

```python
from contextlib import ExitStack
import math

import numpy as np
import concourse.bass as bass
from concourse import mybir

ALU = mybir.AluOpType
ACT = mybir.ActivationFunctionType
AX = mybir.AxisListType
F32 = mybir.dt.float32
BF16 = mybir.dt.bfloat16

P = 128
D = 128
BATCH, SEQ = 2, 1024
TOK = BATCH * SEQ
TILES = TOK // P
BT = 4
BLK = BT * P
BLOCKS = TOK // BLK
HID = 512
FC = HID // P
EXP = 8
HEADS, HD = 16, 8
UNITS = BATCH * HEADS // 2
KT = SEQ // P
PARTS = 3
EPS0, EPS1 = 1e-5, 1e-6
MROW = 64
SLOTS = 4
MLP_GROUPS = ((("z", 0), ("z", 1)), (("z", 2), ("z", 3)), (("h1", 0), ("h1", 1)), (("h1", 2), ("h1", 3)),
              (("h2", 0), ("h2", 1)), (("h2", 2), ("h2", 3)), (("y", 0), ("y", 1)), ())
EARLY_PAIRS = ((0, 2), (6,))
FREE = 1
CREDIT = 3
PCREDIT = 2
SCORE_BANK = (4, 5, 6, 5)
Q_PARTS = (0, 0, 0, 1, 1, 2)
K_PARTS = (0, 1, 2, 0, 1, 0)
Q_RUNS = ((0, 3, 0), (3, 2, 1), (5, 1, 2))
K_RUNS = ((0, 3, 0), (3, 2, 0), (5, 1, 0))
HEAD_SCALE = (1.0 / math.sqrt(HD), 1.0 / 2.828125)
NDMA = dict(x=BLOCKS, cst=1, cols=1, rows=8, w0=1, wf=1, w1=1, we1=1, we2=2)

W0 = dict(qkv=0, gate=384, p=512, clock=640, out=768, m1=896, m2=1408)
W0N = 1920
WF = dict(w1=0, w2=512, h1=1024, h2=3072, w3=5120)
WFN = 5632
W1 = dict(pe=0, qkv=128, ao=512, q=640, k=768, v=896, o=1024, r=1152)
W1N = 1160
COLS = ["gate_b", "p_b", "clock_b", "g1", "b1", "g2", "b2"]
ROWS = ["out_b", "mlp_b2", "w3_s", "bo", "l1g", "l1b", "l2g", "l2b"]
C4 = ["mb1", "s1", "s2", "t1", "t2"]
CC = {n: i for i, n in enumerate(COLS)}
for _i, _n in enumerate(C4):
    CC[_n] = len(COLS) + 4 * _i
CC["be1"] = len(COLS) + 4 * len(C4)
CC["conv"] = CC["be1"] + 4 * EXP
CN = CC["conv"] + 3
CST = dict(ident=0, mask=128, cos=256, sin=256 + KT * D, rank=256 + 2 * KT * D)
CSTN = 256 + 2 * KT * D + EXP


class Chain:

    def __init__(self, eng, sem, wait_apart):
        self.eng, self.sem, self.wait_apart, self.n, self.reg = eng, sem, wait_apart, 0, None

    def mark(self, ins):
        ins.then_inc(self.sem, 1)
        self.n += 1

    def wait(self):
        self.eng.wait_ge(self.sem, self.n if self.reg is None else self.reg + self.n)

    def __call__(self, ins):
        self.mark(ins)
        self.wait()

    def apart(self, ins):
        self.mark(ins)
        self.wait_apart(self.eng, self.sem, self.n if self.reg is None else self.reg + self.n)

    def enter(self, i, per):
        self.reg, self.start, self.per = i * per, self.n, per

    def leave(self, rounds):
        assert self.n - self.start == self.per, (self.n - self.start, self.per)
        self.reg, self.n = None, self.start + rounds * self.per


class Count:

    def __init__(self):
        self.n, self.reg = 0, None

    def seen(self):
        return self.n if self.reg is None else self.reg + self.n

    def next(self):
        self.n += 1
        return self.seen()

    def enter(self, i, per):
        self.reg, self.start, self.per = i * per, self.n, per

    def leave(self, rounds):
        assert self.n - self.start == self.per
        self.reg, self.n = None, self.start + rounds * self.per


def peak_plan(left):
    plan = {s: [] for s in range(1, KT + 1)}
    for s in range(1, KT):
        if left >= 2:
            plan[s] += [(2, 2 * s), (2, 2 * s + 1)]
        if s == 2 and left >= 1:
            plan[s].append((1, None))
    if left >= 3:
        plan[KT] += [(3, 0), (3, 1)]
    return plan


def build(nc, t, out):
    ctx = ExitStack()
    with ctx:
        def sb(name, shape, dt=F32):
            return ctx.enter_context(nc.sbuf_tensor(name, shape, dt))

        def sem(name):
            return ctx.enter_context(nc.semaphore(name))

        ps = ctx.enter_context(nc.psum_tensor("ps", [P, 8, 512], F32))
        w0 = sb("w0", [P, W0N])
        wf = sb("wf", [P, WFN])
        w1 = sb("w1", [P, W1N])
        we1 = sb("we1", [P, EXP * HID])
        we2 = sb("we2", [P, EXP * FC * D])
        cols = sb("cols", [P, CN])
        cst = sb("cst", [P, CSTN])
        rows = sb("rows", [P, len(ROWS), D])
        ident = cst[:, 0:P]
        big = sb("big", [P, 11 * TOK])
        r = [big[:, n * TOK:(n + 1) * TOK] for n in range(11)]
        x_tok, xn_tok, xn_t, v_tok, q_t, k_t, zg, zp, zc, tmp, tmp2 = r
        stage = sb("stage", [P, 2, BLK])
        stage1 = sb("stage1", [P, 2, BLK])
        stage_t = sb("stage_t", [P, 2, BLK])
        qk = sb("qk", [P, 2, 2 * BLK])
        qk1 = sb("qk1", [P, 2, 2 * BLK])
        qk2 = sb("qk2", [P, 2, 2 * BLK])
        st = sb("st", [P, 2, BT, 6])
        mv = sb("mv", [P, 2, BT, 2])
        sd = sb("sd", [P, 2, BT])
        rs = sb("rs", [P, 2, BT])
        ss = sb("ss", [P, 2, 2 * BT])
        nrm = sb("nrm", [P, 2, 2 * BT])
        rn = sb("rn", [P, 2, 2 * BT])
        pm = sb("pm", [P, BATCH])
        nm = sb("nm", [P, 4])
        sm = sb("sm", [P, 4])
        gates = sb("gates", [P, TILES, EXP])
        sil, hid0, hid1, hid2 = stage, qk, qk1, qk2
        q_s, k_s = r[6][:, 0:SEQ], r[6][:, SEQ:TOK]
        v_s, ao_t = r[7][:, 0:SEQ], r[7][:, SEQ:TOK]
        probs = r[8].rearrange("p (a t) -> p a t", a=2)
        probs_t = r[9][:, 0:SEQ]
        x3_tok, x3_t, y_t, v1 = r[1], r[2], r[3], r[4]
        q_parts = big[:, 8 * TOK:8 * TOK + 3 * TOK // 2].bitcast(BF16).rearrange("p (a t) -> p a t", a=PARTS)
        k_parts = big[:, 8 * TOK + 3 * TOK // 2:11 * TOK].bitcast(BF16).rearrange("p (a t) -> p a t", a=PARTS)
        q_b, k_b = (qk2[:, n, :].bitcast(BF16) for n in range(2))
        slots = big[:, 5 * TOK:(5 + SLOTS) * TOK].bitcast(BF16)
        slot = [r[5 + n].bitcast(BF16).rearrange("p (a t) -> p a t", a=2) for n in range(SLOTS)]
        pr = [r[9 + n] for n in range(2)]
        o_in, den = r[2][:, 0:SEQ], r[2][:, SEQ:TOK]
        ctx_t = r[3][:, 0:SEQ]
        o_st = [r[3][:, SEQ + n * 512:SEQ + (n + 1) * 512] for n in range(2)]
        va = [wf[:, n * 512:(n + 1) * 512] for n in range(4)]
        v2 = wf[:, 2048:2048 + TOK // 2].bitcast(BF16)
        neg_m = sb("neg_m", [P, 2, 16])
        m_rest = sb("m_rest", [P, 2, 16])
        m_split = sb("m_split", [P, 2, PARTS, 16], BF16)
        m_t = sb("m_t", [PARTS * 16, 2, P], BF16)
        ident_b = sb("ident_b", [P, P], BF16)
        o1_t = r[4]
        g_t = r[2][0:EXP, :]
        xs = qk1[:, 0, :].rearrange("p (h c t) -> p h c t", h=8, c=2)
        gb = sb("gb", [P, 2, BT * EXP])
        be2 = sb("be2", [EXP, D])
        one_col = sb("one_col", [P, 1])
        eps0, eps1 = (sb(f"eps{n}", [P, 1])[:, :] for n in range(2))
        tk = wf[:, 3072:3072 + 12 * TILES * EXP].rearrange("p (k m) -> p k m", k=12)
        qs_dram = nc.dram_tensor("qs_dram", (6, BATCH, P, SEQ), BF16, kind="Internal").ap()
        ks_dram = nc.dram_tensor("ks_dram", (6, BATCH, P, SEQ), BF16, kind="Internal").ap()
        qb_dram = nc.dram_tensor("qb_dram", (P, TOK), BF16, kind="Internal").ap()
        kb_dram = nc.dram_tensor("kb_dram", (P, TOK), BF16, kind="Internal").ap()
        o_dram = [nc.dram_tensor(f"o_dram{n}", (UNITS, P, 512), F32, kind="Internal").ap() for n in range(2)]

        landed = {n: sem("in_" + n) for n in ("x", "w0", "wf", "w1", "we1", "we2", "cols", "cst", "rows")}
        dve_seq, act_seq, pool_seq = (sem(n + "_seq") for n in ("dve", "act", "pool"))
        stored = sem("stored")
        S = {n: sem(n) for n in (
            "consts var_ready sd_ready xn_ready n1_ready xn_t_psum n1_t_psum n1_t_kept xn_t_kept qkv_ready gp_ready "
            "clock_ready nrm_ready qk_scaled rope_ready rope_t_psum zg_kept zp_kept zc_kept q_kept k_kept v_kept "
            "z_ready sil_done glu_done h1_ready h1_done h2_ready h2_done y_ready y_done pm_ready logs_ready "
            "p_exp decay_ready decay_exp "
            "batch_staged s_ready peak_ready exp_done p_ready p_t_psum p_t_kept av_ready av_kept x2_ready x2_kept "
            "m_var m_sd m_n m_t_psum m_t_kept m1_ready m1_done m2_ready m2_kept "
            "l_var l_sd l_n l_t_psum l_t_kept lq_ready hi_kept parts_kept lv_ready lv_kept conv_done pe_ready "
            "xs_kept bq_ready bq_kept bv_ready bv_kept o_var o_sd o_n o_psum o_sum o_t_psum o_t_kept route_ready "
            "route_exp route_exp2 route_sum gates_ready gt_psum gt_kept up_ready up_done down_ready down_kept f_var f_sd "
            "ctx_ready wo_ready wo_kept").split()}
        att = [{n: sem(f"{n}{a}") for n in (
            "peak_scores_ready peak_bank_free scores_ready probs_done av_steps out_kept m_split_ready "
            "va_ready rows_zeroed slots_ready out_back early_scores_ready early_bank_free").split()} for a in range(2)]
        for a in range(2):
            att[a]["out_stored"] = [sem(f"out_stored{a}_{n}") for n in range(2)]
            att[a]["qk_loaded"] = [sem(f"qk_loaded{a}_{n}") for n in range(SLOTS)]
            att[a]["m_loaded"] = [sem(f"m_loaded{a}_{n}") for n in range(SLOTS)]
        parts_stored, b_stored = sem("parts_stored"), sem("b_stored")
        PARTS_STORES = BLOCKS * (len(Q_RUNS) + len(K_RUNS))
        free_at_start = [S[n] for n in (
            "k_kept q_kept qk_scaled zg_kept zp_kept zc_kept y_done glu_done h1_done h2_done h1_ready h2_ready y_ready "
            "exp_done p_t_kept p_t_psum av_ready av_kept x2_kept m_t_kept m1_done m2_kept m2_ready l_t_kept parts_kept "
            "lv_kept xs_kept bq_kept bv_kept bv_ready up_done down_kept down_ready").split()]
        for A in att:
            free_at_start += [A["out_kept"], *A["out_stored"]]

        block = ctx.enter_context(nc.Block())

        def wait_apart(eng, semaphore, value):
            if not isinstance(value, int):
                eng.compute_val(value)
                eng.wait_ge(S["consts"], 1)
            eng.wait_ge(semaphore, value)

        def flat(a):
            return a[:, :, :].rearrange("p a b -> p (a b)")

        def tiled(a):
            return a.rearrange("p (j d) -> p j d", d=D)

        def rep(name):
            return rows[:, ROWS.index(name), :].unsqueeze(1).to_broadcast([P, BT, D])

        def values(a, c):
            return va[c % 2] if a == 0 else va[2 + c % 2].bitcast(BF16)[:, 0:512]

        def probabilities(a, s):
            return pr[s % 2] if a == 0 else pr[s % 2].bitcast(BF16)[:, 0:4 * 512]

        def one_of(ap, n):
            return ap[n] if isinstance(n, int) else ap[bass.ds(n, 1)].squeeze(0)

        def blk(i, s):
            return bass.ds(i * (2 * BLK) + s * BLK, BLK)

        def tile_cols(i, s, j):
            return bass.ds(i * (2 * BLK) + (s * BT + j) * P, P)

        def col(name, n=0):
            return cols[:, CC[name] + n:CC[name] + n + 1]

        def row(name):
            return rows[:, ROWS.index(name), :]

        @block.vector
        def _(dve):
            link = Chain(dve, dve_seq, wait_apart)
            v = nc.vector

            def stats(s, src, ready):
                for j in range(BT):
                    ins = v.bn_stats(st[:, s, j, :], src(j))
                link.apart(ins)
                for j in range(BT):
                    ins = v.bn_aggr(mv[:, s, j, :], st[:, s, j, :])
                ins.then_inc(S[ready], 1)

            def normalise(s, src, dst, sd_ready, n, done):
                dve.wait_ge(S[sd_ready], n)
                link(v.reciprocal(rs[:, s, :], sd[:, s, :]))
                for j in range(BT):
                    ins = v.tensor_scalar(dst(j), src(j), mv[:, s, j, 0:1], rs[:, s, j:j + 1], ALU.subtract, ALU.mult)
                if done is None:
                    link(ins)
                else:
                    ins.then_inc(S[done], 1)

            for n in ("x", "cst", "cols", "rows"):
                dve.wait_ge(landed[n], 16 * NDMA[n])
            with dve.Fori(0, BATCH) as i:
                link.enter(i, 2 * 8)
                two = range(2)
                x_of = [lambda j, s=s: x_tok[:, tile_cols(i, s, j)] for s in two]
                xn_of = [lambda j, s=s: stage[:, s, j * P:(j + 1) * P] for s in two]
                n1_of = [lambda j, s=s: stage1[:, s, j * P:(j + 1) * P] for s in two]
                for s in two:
                    stats(s, x_of[s], "var_ready")
                for s in two:
                    normalise(s, x_of[s], xn_of[s], "sd_ready", 4 * i + s + 1, "xn_ready")
                for s in two:
                    dve.wait_ge(S["xn_ready"], 2 * i + s + 1)
                    stats(s, xn_of[s], "var_ready")
                for s in two:
                    normalise(s, xn_of[s], n1_of[s], "sd_ready", 4 * i + 2 + s + 1, "n1_ready")
                for s in two:
                    link.mark(v.tensor_copy(xn_tok[:, blk(i, s)], stage[:, s, :]))
                for s in two:
                    n = 2 * i + s
                    dve.wait_ge(S["nrm_ready"], n + 1)
                    link(v.tensor_scalar(nrm[:, s, :], nrm[:, s, :], 1e-12, None, ALU.max))
                    link(v.reciprocal(rn[:, s, :], nrm[:, s, :]))
                    for j in range(BT):
                        for h in range(2):
                            ins = v.tensor_scalar(qk[:, s, (2 * j + h) * D:(2 * j + h + 1) * D],
                                                  ps[:, 2 + j, h * D:(h + 1) * D],
                                                  rn[:, s, 2 * j + h:2 * j + h + 1], None, ALU.mult)
                    ins.then_inc(S["qk_scaled"], 1)
                    dve.wait_ge(S["qk_scaled"], FREE + n + 1)
                    src = qk[:, s, :].rearrange("p (j h d) -> p j h d", j=BT, h=2)
                    pairs = qk[:, s, :].rearrange("p (j h f e) -> p j h f e", j=BT, h=2, e=2)
                    turned = qk2[:, s, :].rearrange("p (j h f e) -> p j h f e", j=BT, h=2, e=2)
                    a = qk1[:, s, :].rearrange("p (j h d) -> p j h d", j=BT, h=2)
                    cos = cst[:, CST["cos"] + s * BLK:CST["cos"] + (s + 1) * BLK].rearrange("p (j d) -> p j d", j=BT)
                    sin = cst[:, CST["sin"] + s * BLK:CST["sin"] + (s + 1) * BLK].rearrange(
                        "p (j f e) -> p j f e", j=BT, e=2)
                    for h in range(2):
                        v.tensor_tensor(a[:, :, h, :], src[:, :, h, :], cos, ALU.mult)
                        v.tensor_tensor(turned[:, :, h, :, 0], pairs[:, :, h, :, 1], sin[:, :, :, 0], ALU.mult)
                        ins = v.tensor_tensor(turned[:, :, h, :, 1], pairs[:, :, h, :, 0], sin[:, :, :, 1], ALU.mult)
                    link(ins)
                    v.tensor_tensor(qk1[:, s, :], qk1[:, s, :], qk2[:, s, :], ALU.add).then_inc(S["rope_ready"], 1)
                link.leave(BATCH)

            def glu(n, fc, bank):
                dve.wait_ge(S["sil_done"], 4 * n + fc + 1)
                if fc == 0:
                    dve.wait_ge(S["h1_ready"], FREE + 4 * n)
                v.scalar_tensor_tensor(out=flat(hid0)[:, fc * BLK:(fc + 1) * BLK], in0=ps[:, bank, :],
                                       scalar=col("s2", fc), in1=sil[:, fc % 2, :], op0=ALU.mult,
                                       op1=ALU.mult).then_inc(S["glu_done"], 1)

            def add_mlp(n, at, bank):
                dve.wait_ge(S["y_ready"], FREE + n + 1)
                v.tensor_tensor(tiled(stage1[:, 0, :]), tiled(ps[:, bank, :]), rep("w3_s"),
                                ALU.mult).then_inc(S["y_done"], 1)
                dve.wait_ge(S["y_done"], FREE + n + 1)
                link(v.tensor_tensor(x_tok[:, at], x_tok[:, at], stage1[:, 0, :], ALU.add))

            dve.wait_ge(S["zp_kept"], FREE + BLOCKS)
            with dve.Fori(0, BATCH) as i:
                link.enter(i, 14)
                at = bass.ds(i * SEQ, SEQ)
                v.tensor_reduce(pm[:, 0:1], zp[:, at], AX.X, ALU.max, negate=True).then_inc(S["pm_ready"], 1)
                glu(i, 0, 2)
                glu(i, 1, 3)
                dve.wait_ge(S["logs_ready"], BATCH)
                link(v.scalar_tensor_tensor(out=zg[:, at], in0=zg[:, at], scalar=0.0, in1=tmp[:, at],
                                            op0=ALU.max, op1=ALU.add))
                ones = one_col[:, 0:1].to_broadcast([P, SEQ])
                link(v.tensor_tensor_scan(tmp[:, at], ones, zg[:, at], 0.0, ALU.mult, ALU.add))
                glu(i, 2, 2)
                glu(i, 3, 3)
                link(v.tensor_scalar(tmp[:, at], tmp[:, at], -1.0, -60.0, ALU.mult, ALU.max))
                v.tensor_scalar(tmp[:, at], tmp[:, at], 50.0, None, ALU.min).then_inc(S["decay_ready"], 1)
                link(v.scalar_tensor_tensor(out=zc[:, at], in0=zc[:, at], scalar=0.0, in1=tmp2[:, at],
                                            op0=ALU.max, op1=ALU.add))
                dve.wait_ge(S["p_exp"], i + 1)
                link(v.tensor_tensor(zp[:, at], zp[:, at], zc[:, at], ALU.mult))
                link(v.tensor_tensor_scan(tmp2[:, at], ones, zp[:, at], 0.0, ALU.mult, ALU.add))
                link.apart(v.tensor_scalar(tmp2[:, at], tmp2[:, at], 1e-8, None, ALU.add))
                link(v.reciprocal(tmp2[:, at], tmp2[:, at]))
                dve.wait_ge(S["decay_exp"], i + 1)
                link(v.tensor_tensor(tmp2[:, at], zg[:, at], tmp2[:, at], ALU.mult))
                link.apart(v.tensor_scalar(tmp[:, at], zg[:, at], 1e-8, None, ALU.add))
                link(v.reciprocal(tmp[:, at], tmp[:, at]))
                link(v.tensor_tensor(tmp[:, at], zp[:, at], tmp[:, at], ALU.mult))
                v.tensor_tensor(q_t[:, at], q_t[:, at], tmp2[:, at], ALU.mult)
                link(v.tensor_tensor(k_t[:, at], k_t[:, at], tmp[:, at], ALU.mult))
                add_mlp(i, bass.ds(i * BLK, BLK), 4)
                link.leave(BATCH)

            scale = 1.0 / math.sqrt(D)
            with dve.Fori(0, BATCH) as i:
                link.enter(i, 2 * KT + 3)
                all_of = bass.ds(i * SEQ, SEQ)
                v.tensor_copy(q_s, q_t[:, all_of])
                v.tensor_copy(k_s, k_t[:, all_of])
                v.tensor_copy(v_s, v_tok[:, all_of]).then_inc(S["batch_staged"], 1)

                def peak(qt):
                    dve.wait_ge(S["s_ready"], KT * i + qt + 1)
                    pair = ps[:, 0:2, :].rearrange("p a b -> p (a b)")
                    link(v.tensor_reduce(nm[:, qt % 2:qt % 2 + 1], pair[:, 0:(qt + 1) * P], AX.X, ALU.max,
                                         negate=True))
                    v.tensor_scalar(nm[:, 2 + qt % 2:3 + qt % 2], nm[:, qt % 2:qt % 2 + 1], scale, None,
                                    ALU.mult).then_inc(S["peak_ready"], 1)

                def divide(qt):
                    dve.wait_ge(S["exp_done"], FREE + KT * i + qt + 1)
                    link(v.reciprocal(sm[:, 2 + qt % 2:3 + qt % 2], sm[:, qt % 2:qt % 2 + 1]))
                    p = probs[:, qt % 2, 0:(qt + 1) * P]
                    v.tensor_scalar(p, p, sm[:, 2 + qt % 2:3 + qt % 2], None, ALU.mult).then_inc(S["p_ready"], 1)

                def keep(qt):
                    dve.wait_ge(S["av_ready"], FREE + KT * i + qt + 1)
                    v.tensor_copy(ao_t[:, qt * P:(qt + 1) * P],
                                  ps[:, (4, 7)[qt % 2], 0:P]).then_inc(S["av_kept"], 1)

                peak(0)
                for qt in range(KT):
                    divide(qt)
                    if qt + 1 < KT:
                        peak(qt + 1)
                    if qt:
                        keep(qt - 1)
                    for group in MLP_GROUPS[qt]:
                        if group[0] == "z":
                            glu(2 + i, group[1], 6)
                    if qt == KT - 1:
                        add_mlp(2 + i, bass.ds((2 + i) * BLK, BLK), 6)
                keep(KT - 1)
                for s in range(2):
                    at = blk(i, s)
                    dve.wait_ge(S["x2_ready"], 2 * i + s + 1)
                    v.tensor_tensor(xn_tok[:, at], xn_tok[:, at], ps[:, 2 + s, :], ALU.add).then_inc(S["x2_kept"], 1)
                    dve.wait_ge(S["x2_kept"], FREE + 2 * i + s + 1)
                    link(v.tensor_tensor(tiled(xn_tok[:, at]), tiled(xn_tok[:, at]), rep("out_b"), ALU.add))
                link.leave(BATCH)

            with dve.Fori(0, BATCH) as i:
                link.enter(i, 8)
                x2_of = [lambda j, s=s: xn_tok[:, tile_cols(i, s, j)] for s in range(2)]
                for s in range(2):
                    stats(s, x2_of[s], "m_var")
                for s in range(2):
                    normalise(s, x2_of[s], lambda j: stage[:, s, j * P:(j + 1) * P], "m_sd", 2 * i + s + 1, "m_n")
                for s in range(2):
                    n, at = 2 * i + s, blk(i, s)
                    dve.wait_ge(S["m2_ready"], FREE + n + 1)
                    v.tensor_tensor(x_tok[:, at], x_tok[:, at], ps[:, 5 + s, :], ALU.add).then_inc(S["m2_kept"], 1)
                    dve.wait_ge(S["m2_kept"], FREE + n + 1)
                    link(v.tensor_tensor(x_tok[:, at], x_tok[:, at], xn_tok[:, at], ALU.add))
                    link(v.tensor_tensor(tiled(x_tok[:, at]), tiled(x_tok[:, at]), rep("mlp_b2"), ALU.add))
                link.leave(BATCH)

            with dve.Fori(0, BATCH) as i:
                link.enter(i, 20)
                xl_of = [lambda j, s=s: x_tok[:, tile_cols(i, s, j)] for s in range(2)]
                for s in range(2):
                    stats(s, xl_of[s], "l_var")
                for s in range(2):
                    normalise(s, xl_of[s], lambda j: stage[:, s, j * P:(j + 1) * P], "l_sd", 2 * i + s + 1, "l_n")
                for s in range(2):
                    n, at = 2 * i + s, blk(i, s)
                    dve.wait_ge(S["l_n"], n + 1)
                    link.mark(v.tensor_copy(x3_tok[:, at], stage[:, s, :]))
                for s in range(2):
                    n, at = 2 * i + s, blk(i, s)
                    for m, parts in enumerate((q_parts, k_parts)):
                        rest = stage1[:, m, :]
                        dve.wait_ge(S["hi_kept"], 2 * n + m + 1)
                        link(v.tensor_tensor(rest, ps[:, 1 + 2 * s + m, :], parts[:, 0, at], ALU.subtract))
                        link(v.tensor_copy(parts[:, 1, at], rest))
                        link(v.tensor_tensor(rest, rest, parts[:, 1, at], ALU.subtract))
                        v.tensor_copy(parts[:, 2, at], rest).then_inc(S["parts_kept"], 1)
                        dve.wait_ge(S["parts_kept"], FREE + 2 * n + m + 1)
                dve.wait_ge(S["l_t_kept"], FREE + 2 * i + 2)
                x3 = lambda a, b: x3_t[:, bass.ds(i * SEQ + a, b - a)]
                y3 = lambda a, b: y_t[:, bass.ds(i * SEQ + a, b - a)]
                link(v.tensor_scalar(y3(0, SEQ), x3(0, SEQ), col("conv", 1), None, ALU.mult))
                link(v.scalar_tensor_tensor(out=y3(1, SEQ), in0=x3(0, SEQ - 1), scalar=col("conv", 0),
                                            in1=y3(1, SEQ), op0=ALU.mult, op1=ALU.add))
                v.scalar_tensor_tensor(out=y3(0, SEQ - 1), in0=x3(1, SEQ), scalar=col("conv", 2),
                                       in1=y3(0, SEQ - 1), op0=ALU.mult, op1=ALU.add).then_inc(S["conv_done"], 1)
                link.leave(BATCH)

            def split_maxima(a, neg, rest, part):
                link(v.tensor_copy(part(0), neg))
                link(v.tensor_tensor(rest, neg, part(0), ALU.subtract))
                link(v.tensor_copy(part(1), rest))
                link(v.tensor_tensor(rest, rest, part(1), ALU.subtract))
                v.tensor_copy(part(2), rest).then_inc(att[a]["m_split_ready"], 1)

            def early_maxima(a, i, s, k):
                A, b = att[a], EARLY_PAIRS[a][k % len(EARLY_PAIRS[a])]
                dve.wait_ge(A["early_scores_ready"], 2 * KT * i + KT * s + k + 1)
                pair = ps[:, b:b + 2, :].rearrange("p a b -> p (a b)")
                maxima = neg_m[:, :, :].rearrange("p c k -> p (c k)")
                v.tensor_reduce(maxima[:, bass.ds(i * 16 + s * KT + k, 1)], pair, AX.X, ALU.max,
                                negate=True).then_inc(A["early_bank_free"], 1)
                if s and k == KT - 1:
                    dve.wait_ge(A["early_bank_free"], len(EARLY_PAIRS[a]) + 2 * KT * (i + 1))
                    parts = m_split[:, :, :, :].rearrange("p c a k -> p (c a k)")
                    split_maxima(a, maxima[:, bass.ds(i * 16, 16)], m_rest[:, 0, :],
                                 lambda n: parts[:, bass.ds(i * (16 * PARTS) + n * 16, 16)])

            def attention(a):
                A = att[a]
                items = Count()

                def peaks(c, k):
                    b = 2 * (items.n % 2)
                    dve.wait_ge(A["peak_scores_ready"], items.next())
                    pair = ps[:, b:b + 2, :].rearrange("p a b -> p (a b)")
                    v.tensor_reduce(neg_m[:, c % 2, k:k + 1], pair, AX.X, ALU.max,
                                    negate=True).then_inc(A["peak_bank_free"], 1)
                    if k == 15:
                        dve.wait_ge(A["peak_bank_free"], items.seen() + PCREDIT)
                        split_maxima(a, neg_m[:, c % 2, :], m_rest[:, c % 2, :], lambda n: m_split[:, c % 2, n, :])

                def turned(c):
                    b = 2 * (items.n % 2)
                    dve.wait_ge(A["peak_scores_ready"], items.next())
                    v.tensor_copy(m_t[:, c % 2, :], ps[0:PARTS * 16, b, 0:P // 2].bitcast(BF16)).then_inc(
                        A["peak_bank_free"], 1)

                def unit(c, left):
                    plan = peak_plan(left)
                    for s in range(1, KT + 1):
                        for ahead, k in plan[s]:
                            if k is None:
                                turned(c + ahead)
                            else:
                                peaks(c + ahead, k)

                turned(0)
                peaks(2, 0)
                peaks(2, 1)
                with dve.Fori(0, UNITS // SLOTS - 1) as i:
                    items.enter(i, 17 * SLOTS)
                    link.enter(i, 4 * SLOTS)
                    for c in range(SLOTS):
                        unit(c, 3)
                    link.leave(UNITS // SLOTS - 1)
                    items.leave(UNITS // SLOTS - 1)
                for c in range(SLOTS):
                    unit(c, 3 - c)

            def heads_out(a, b):
                dve.wait_ge(att[a]["out_back"], 64 * (b + 1))
                dve.wait_ge(S["wo_ready"], 2 * (BATCH * a + b))
                link(v.reciprocal(den, den))
                if a == 0:
                    v.tensor_tensor(ctx_t, o_in, den, ALU.mult).then_inc(S["ctx_ready"], 1)
                else:
                    order = lambda x: x.rearrange("p (c t) -> p c t", c=HEADS)
                    v.tensor_tensor(ctx_t.rearrange("p (t c) -> p c t", c=HEADS), order(o_in), order(den),
                                    ALU.mult).then_inc(S["ctx_ready"], 1)

            with dve.Fori(0, BATCH) as i:
                link.enter(i, 4)
                for s in range(2):
                    n, at = 2 * i + s, blk(i, s)
                    dve.wait_ge(S["pe_ready"], n + 1)
                    dve.wait_ge(S["conv_done"], BATCH)
                    dve.wait_ge(S["bv_ready"], FREE + 2 * n)
                    for c in range(2):
                        ins = v.tensor_tensor(xs[:, :, c, :], ps[:, 4, :].rearrange("p (h t) -> p h t", h=8),
                                              y_t[:, at].rearrange("p (h t) -> p h t", h=8), ALU.add)
                    ins.then_inc(S["xs_kept"], 1)
                    for k in range(KT):
                        early_maxima(0, i, s, k)
                link.leave(BATCH)

            attention(0)

            for b in range(BATCH):
                heads_out(0, b)
                for s in range(2):
                    n = 2 * b + s
                    at = slice(n * BLK, (n + 1) * BLK)
                    src = lambda j: x3_tok[:, n * BLK + j * P:n * BLK + (j + 1) * P]
                    dve.wait_ge(S["wo_ready"], n + 1)
                    v.tensor_tensor(x3_tok[:, at], x3_tok[:, at], ps[:, n % 2, :], ALU.add).then_inc(S["wo_kept"], 1)
                    dve.wait_ge(S["wo_kept"], n + 1)
                    link(v.tensor_tensor(tiled(x3_tok[:, at]), tiled(x3_tok[:, at]), rep("bo"), ALU.add))
                    stats(s, src, "o_var")
                    normalise(s, src, lambda j: stage1[:, s, j * P:(j + 1) * P], "o_sd", n + 1, None)
                    link(v.tensor_tensor(tiled(stage1[:, s, :]), tiled(stage1[:, s, :]), rep("l1g"), ALU.mult))
                    v.tensor_tensor(tiled(stage[:, s, :]), tiled(stage1[:, s, :]), rep("l1b"),
                                    ALU.add).then_inc(S["o_n"], 1)
                    dve.wait_ge(S["o_n"], n + 1)
                    link(v.tensor_copy(x3_tok[:, at], stage[:, s, :]))
            n_e = TILES * EXP
            T = lambda k: tk[:, k, :].rearrange("p (a e) -> p a e", e=EXP)
            one = lambda k: tk[:, k, 0:TILES]
            wide = lambda k: one(k).unsqueeze(2).to_broadcast([P, TILES, EXP])
            rank = cst[:, CST["rank"]:CST["rank"] + EXP].unsqueeze(1).to_broadcast([P, TILES, EXP])
            dve.wait_ge(S["route_ready"], BLOCKS)
            link(v.tensor_copy(tk[:, 0, :], ps[:, 4, 0:n_e]))
            link(v.tensor_reduce(one(1), T(0), AX.X, ALU.max))
            v.tensor_tensor(T(0), T(0), wide(1), ALU.subtract).then_inc(S["route_sum"], 1)
            dve.wait_ge(S["route_exp"], 1)
            link(v.tensor_reduce(one(1), T(2), AX.X, ALU.add))
            link(v.reciprocal(one(1), one(1)))
            link(v.tensor_tensor(T(2), T(2), wide(1), ALU.mult))
            for best, chosen in ((3, 4), (5, 6)):
                link(v.tensor_reduce(one(best), T(2), AX.X, ALU.max))
                link(v.tensor_tensor(T(7), T(2), wide(best), ALU.is_equal))
                link(v.tensor_tensor(T(7), T(7), rank, ALU.mult))
                link(v.tensor_reduce(one(8), T(7), AX.X, ALU.max))
                link(v.tensor_tensor(T(chosen), T(7), wide(8), ALU.is_equal))
                link(v.scalar_tensor_tensor(out=T(2), in0=T(chosen), scalar=-2.0, in1=T(2), op0=ALU.mult,
                                            op1=ALU.add))
            v.tensor_tensor(one(9), one(5), one(3), ALU.subtract).then_inc(S["route_sum"], 1)
            dve.wait_ge(S["route_exp"], 2)
            link(v.tensor_scalar(one(11), one(10), 1.0, None, ALU.add))
            link(v.reciprocal(one(11), one(11)))
            link(v.tensor_tensor(one(10), one(10), one(11), ALU.mult))
            link(v.tensor_tensor(T(4), T(4), wide(11), ALU.mult))
            link(v.tensor_tensor(T(6), T(6), wide(10), ALU.mult))
            v.tensor_tensor(gates[:, :, :], T(4), T(6), ALU.add).then_inc(S["gates_ready"], 1)
            for n in range(BLOCKS):
                at = slice(n * BLK, (n + 1) * BLK)
                dve.wait_ge(S["gt_psum"], n + 1)
                v.tensor_copy(g_t[:, at], ps[0:EXP, n % 2, :]).then_inc(S["gt_kept"], 1)
            for n in range(BLOCKS):
                at = slice(n * BLK, (n + 1) * BLK)
                dve.wait_ge(S["gt_psum"], BLOCKS + n + 1)
                v.tensor_tensor(x3_tok[:, at], x3_tok[:, at], ps[:, 2 + n % 2, :], ALU.add).then_inc(S["gt_kept"], 1)

            dve.wait_ge(S["gt_kept"], 2 * BLOCKS)
            dve.wait_ge(S["gates_ready"], 1)
            with dve.Fori(0, BATCH) as i:
                link.enter(i, 2 * 7 + 4)
                for s in range(2):
                    n, at = 2 * i + s, blk(i, s)
                    acc = stage1[:, s, :]
                    v.tensor_copy(acc, x3_tok[:, at])
                    link(v.tensor_copy(gb[:, s, :], gates[:, :, :].rearrange("p a e -> p (a e)")[
                        :, bass.ds(i * (2 * BT * EXP) + s * BT * EXP, BT * EXP)]))
                    for e in range(EXP):
                        early_maxima(1, i, s, e)
                        dve.wait_ge(S["down_ready"], FREE + EXP * n + e + 1)
                        for j in range(BT):
                            a = acc[:, j * P:(j + 1) * P]
                            ins = v.scalar_tensor_tensor(out=a, in0=ps[:, 4 + e % 2, j * P:(j + 1) * P],
                                                         scalar=gb[:, s, j * EXP + e:j * EXP + e + 1], in1=a,
                                                         op0=ALU.mult, op1=ALU.add)
                        ins.then_inc(S["down_kept"], 1)
                        dve.wait_ge(S["down_kept"], FREE + EXP * n + e + 1)
                    own = lambda j: acc[:, j * P:(j + 1) * P]
                    stats(s, own, "f_var")
                    normalise(s, own, own, "f_sd", n + 1, None)
                    link(v.tensor_tensor(tiled(acc), tiled(acc), rep("l2g"), ALU.mult))
                    link(v.tensor_tensor(tiled(acc), tiled(acc), rep("l2b"), ALU.add))
                    link(v.tensor_tensor(x_tok[:, at], x_tok[:, at], acc, ALU.add))
                link.leave(BATCH)

            attention(1)
            for b in range(BATCH):
                heads_out(1, b)
                for s in range(2):
                    n = 2 * BATCH + 2 * b + s
                    at = slice((2 * b + s) * BLK, (2 * b + s + 1) * BLK)
                    dve.wait_ge(S["wo_ready"], n + 1)
                    v.tensor_tensor(x_tok[:, at], x_tok[:, at], ps[:, n % 2, :], ALU.add).then_inc(S["wo_kept"], 1)

        @block.tensor
        def _(pe):
            mm = nc.tensor.matmul

            def turn(bank, src, width=BT):
                for j in range(width):
                    ins = nc.tensor.transpose(ps[:, bank, j * P:(j + 1) * P], src(j), ident)
                return ins

            for n in ("cst", "w0"):
                pe.wait_ge(landed[n], 16 * NDMA[n])
            with pe.Fori(0, BATCH) as i:
                n = 2 * i
                for s, (bank, kept) in enumerate(((0, "k_kept"), (1, "q_kept"))):
                    pe.wait_ge(S["xn_ready"], n + s + 1)
                    pe.wait_ge(S[kept], FREE + n)
                    turn(bank, lambda j: stage[:, s, j * P:(j + 1) * P]).then_inc(S["xn_t_psum"], 1)
                for s, (bank, kept) in enumerate(((6, "k_kept"), (7, "q_kept"))):
                    pe.wait_ge(S["n1_ready"], n + s + 1)
                    pe.wait_ge(S[kept], FREE + n)
                    turn(bank, lambda j: stage1[:, s, j * P:(j + 1) * P]).then_inc(S["n1_t_psum"], 1)
                for s in range(2):
                    pe.wait_ge(S["n1_t_kept"], n + s + 1)
                    pe.wait_ge(S["qk_scaled"], FREE + n + s)
                    xt = stage_t[:, s, :]
                    for j in range(BT):
                        ins = mm(ps[:, 2 + j, 0:3 * D], xt[:, j * P:(j + 1) * P], w0[:, 0:3 * D], start=True, stop=True)
                    ins.then_inc(S["qkv_ready"], 1)
                    if s == 0:
                        pe.wait_ge(S["xn_t_kept"], n + 2)
                    else:
                        pe.wait_ge(S["zg_kept"], FREE + n + 1)
                    mm(ps[:, 0, :], w0[:, W0["gate"]:W0["gate"] + P], xt, start=True, stop=True)
                    mm(ps[:, 6 + s, :], w0[:, W0["p"]:W0["p"] + P], xt, start=True, stop=True).then_inc(S["gp_ready"], 1)
                    if s == 1:
                        pe.wait_ge(S["zp_kept"], FREE + n + 1)
                    mm(ps[:, (1, 6)[s], :], w0[:, W0["clock"]:W0["clock"] + P], xt, start=True, stop=True).then_inc(
                        S["clock_ready"], 1)
                for s in range(2):
                    pe.wait_ge(S["rope_ready"], n + s + 1)
                    pe.wait_ge(S["zc_kept"], FREE + n + s + 1)
                    pe.wait_ge(S["zg_kept"], FREE + n + 2)
                    pe.wait_ge(S["zp_kept"], FREE + n + s + 1)
                    turn((1, 7)[s], lambda j: qk1[:, s, 2 * j * D:(2 * j + 1) * D])
                    turn((0, 6)[s], lambda j: qk1[:, s, (2 * j + 1) * D:(2 * j + 2) * D]).then_inc(S["rope_t_psum"], 1)

            pe.wait_ge(landed["wf"], 16 * NDMA["wf"])
            for n in ("k_kept", "q_kept", "qk_scaled", "zg_kept", "zp_kept"):
                pe.wait_ge(S[n], FREE + BLOCKS)
            pe.wait_ge(S["xn_t_kept"], BLOCKS)
            h0, h1, h2 = flat(hid0), flat(hid1), flat(hid2)

            def z(n, at, fc, banks):
                for b, w in zip(banks, ("w1", "w2")):
                    ins = mm(ps[:, b, :], wf[:, WF[w] + fc * P:WF[w] + (fc + 1) * P], xn_t[:, at], start=True, stop=True)
                ins.then_inc(S["z_ready"], 1)

            def hidden(w, src, oc, bank, ready):
                for fc in range(FC):
                    at = WF[w] + fc * HID + oc * P
                    ins = mm(ps[:, bank, :], wf[:, at:at + P], src[:, fc * BLK:(fc + 1) * BLK],
                             start=fc == 0, stop=fc == FC - 1)
                ins.then_inc(S[ready], 1)

            def last(j, bank):
                for fc in range(FC):
                    ins = mm(ps[:, bank, j * P:(j + 1) * P], h2[:, fc * BLK + j * P:fc * BLK + (j + 1) * P],
                             wf[:, WF["w3"] + fc * D:WF["w3"] + (fc + 1) * D], start=fc == 0, stop=fc == FC - 1)
                return ins

            with pe.Fori(0, BATCH) as i:
                for fc in range(FC):
                    pe.wait_ge(S["glu_done"], FREE + 4 * i + (fc - 1 if fc >= 2 else 0))
                    z(i, bass.ds(i * BLK, BLK), fc, (fc % 2, 2 + fc % 2))
                pe.wait_ge(S["glu_done"], FREE + 4 * i + 4)
                pe.wait_ge(S["y_done"], FREE + i)
                for oc in range(FC):
                    pe.wait_ge(S["h1_done"], FREE + 4 * i + (oc - 1 if oc >= 2 else 0))
                    hidden("h1", h0, oc, 4 + oc % 2, "h1_ready")
                pe.wait_ge(S["h1_done"], FREE + 4 * i + 4)
                for oc in range(FC):
                    pe.wait_ge(S["h2_done"], FREE + 4 * i + (oc - 1 if oc >= 2 else 0))
                    hidden("h2", h1, oc, 6 + oc % 2, "h2_ready")
                pe.wait_ge(S["h2_done"], FREE + 4 * i + 4)
                for j in range(BT):
                    ins = last(j, 4)
                ins.then_inc(S["y_ready"], 1)

            pe.wait_ge(S["y_done"], FREE + 2)
            with pe.Fori(0, BATCH) as i:
                n = 2 + i

                def mlp_group(kind, k):
                    if kind == "z":
                        if k == 0:
                            pe.wait_ge(S["y_done"], FREE + n)
                        pe.wait_ge(S["glu_done"], FREE + 4 * n + k)
                        z(n, bass.ds((2 + i) * BLK, BLK), k, (5, 6))
                    elif kind == "h1":
                        pe.wait_ge(S["glu_done"], FREE + 4 * n + 4)
                        if k >= 2:
                            pe.wait_ge(S["h1_done"], FREE + 4 * n + k - 1)
                        hidden("h1", h0, k, 5 + k % 2, "h1_ready")
                    elif kind == "h2":
                        pe.wait_ge(S["h1_done"], FREE + 4 * n + 4)
                        if k >= 2:
                            pe.wait_ge(S["h2_done"], FREE + 4 * n + k - 1)
                        hidden("h2", h1, k, 5 + k % 2, "h2_ready")
                    else:
                        pe.wait_ge(S["h2_done"], FREE + 4 * n + 4)
                        last(2 * k, 6)
                        ins = last(2 * k + 1, 6)
                        if k == 1:
                            ins.then_inc(S["y_ready"], 1)

                pe.wait_ge(S["batch_staged"], i + 1)

                def scores(qt):
                    pe.wait_ge(S["exp_done"], FREE + KT * i + qt)
                    width = (qt + 1) * P
                    q = q_s[:, qt * P:(qt + 1) * P]
                    for c in range((width + 511) // 512):
                        w = min(512, width - 512 * c)
                        mm(ps[:, c, 0:w], q, k_s[:, 512 * c:512 * c + w], start=True, stop=c != qt // 4)
                    m = (qt % 4) * P
                    mm(ps[:, qt // 4, m:m + P], ident, cst[:, CST["mask"]:CST["mask"] + P], start=False,
                       stop=True).then_inc(S["s_ready"], 1)

                scores(0)
                for qt in range(KT):
                    if qt + 1 < KT:
                        scores(qt + 1)
                    groups = MLP_GROUPS[qt]
                    if groups:
                        mlp_group(*groups[0])
                    pe.wait_ge(S["p_ready"], KT * i + qt + 1)
                    pe.wait_ge(S["p_t_kept"], FREE + KT * i + qt)
                    if qt == 0:
                        pe.wait_ge(S["x2_kept"], FREE + 2 * i)
                    for kt in range(qt + 1):
                        ins = nc.tensor.transpose(ps[:, 2 + kt // 4, (kt % 4) * P:(kt % 4 + 1) * P],
                                                  probs[:, qt % 2, kt * P:(kt + 1) * P], ident)
                    ins.then_inc(S["p_t_psum"], 1)
                    if groups:
                        mlp_group(*groups[1])
                    pe.wait_ge(S["p_t_kept"], FREE + KT * i + qt + 1)
                    if qt >= 2:
                        pe.wait_ge(S["av_kept"], FREE + KT * i + qt - 1)
                    for kt in range(qt + 1):
                        ins = mm(ps[:, (4, 7)[qt % 2], 0:P], v_s[:, kt * P:(kt + 1) * P],
                                 probs_t[:, kt * P:(kt + 1) * P], start=kt == 0, stop=kt == qt)
                    ins.then_inc(S["av_ready"], 1)
                pe.wait_ge(S["av_kept"], FREE + KT * i + KT)
                for s in range(2):
                    for j in range(BT):
                        t0 = (s * BT + j) * P
                        ins = mm(ps[:, 2 + s, j * P:(j + 1) * P], ao_t[:, t0:t0 + P], w0[:, W0["out"]:W0["out"] + D],
                                 start=True, stop=True)
                    ins.then_inc(S["x2_ready"], 1)

            pe.wait_ge(S["y_done"], FREE + BLOCKS)
            pe.wait_ge(S["exp_done"], FREE + KT * BATCH)
            pe.wait_ge(S["p_t_kept"], FREE + KT * BATCH)
            with pe.Fori(0, BATCH) as i:
                for s, bank in enumerate((0, 7)):
                    n = 2 * i + s
                    pe.wait_ge(S["m_n"], n + 1)
                    pe.wait_ge(S["m_t_kept"], FREE + 2 * i)
                    turn(bank, lambda j: stage[:, s, j * P:(j + 1) * P]).then_inc(S["m_t_psum"], 1)
                for s in range(2):
                    n = 2 * i + s
                    pe.wait_ge(S["m_t_kept"], FREE + n + 1)
                    for fc in range(FC):
                        if s:
                            pe.wait_ge(S["m1_done"], FREE + 8 * i + fc + 1)
                        at = W0["m1"] + fc * P
                        mm(ps[:, 1 + fc, :], w0[:, at:at + P], stage_t[:, s, :], start=True, stop=True).then_inc(
                            S["m1_ready"], 1)
                for s in range(2):
                    n = 2 * i + s
                    pe.wait_ge(S["m1_done"], FREE + 4 * n + 4)
                    pe.wait_ge(S["m2_kept"], FREE + 2 * i)
                    for j in range(BT):
                        for fc in range(FC):
                            at = W0["m2"] + fc * D
                            ins = mm(ps[:, 5 + s, j * P:(j + 1) * P],
                                     (h0, h1)[s][:, fc * BLK + j * P:fc * BLK + (j + 1) * P],
                                     w0[:, at:at + D], start=fc == 0, stop=fc == FC - 1)
                    ins.then_inc(S["m2_ready"], 1)

            pe.wait_ge(landed["w1"], 16 * NDMA["w1"])
            pe.wait_ge(S["m_t_kept"], FREE + BLOCKS)
            pe.wait_ge(S["m1_done"], FREE + FC * BLOCKS)
            wcol = lambda name, n=P: w1[:, W1[name]:W1[name] + n]
            with pe.Fori(0, BATCH) as i:
                for s, bank in enumerate((0, 7)):
                    pe.wait_ge(S["l_n"], 2 * i + s + 1)
                    pe.wait_ge(S["l_t_kept"], FREE + 2 * i)
                    turn(bank, lambda j: stage[:, s, j * P:(j + 1) * P]).then_inc(S["l_t_psum"], 1)
                for s in range(2):
                    n = 2 * i + s
                    pe.wait_ge(S["l_t_kept"], FREE + n + 1)
                    pe.wait_ge(S["parts_kept"], FREE + 4 * i)
                    for m, w in enumerate(("q", "k")):
                        mm(ps[:, 1 + 2 * s + m, :], wcol(w), stage_t[:, s, :], start=True, stop=True).then_inc(
                            S["lq_ready"], 1)
                    pe.wait_ge(S["lv_kept"], FREE + 2 * i)
                    for j in range(BT):
                        ins = mm(ps[:, 5 + s, j * P:(j + 1) * P], stage_t[:, s, j * P:(j + 1) * P], wcol("v"),
                                 start=True, stop=True)
                    ins.then_inc(S["lv_ready"], 1)
            pe.wait_ge(S["conv_done"], BATCH)
            pe.wait_ge(S["l_t_kept"], FREE + BLOCKS)
            pe.wait_ge(S["parts_kept"], FREE + 2 * BLOCKS)
            pe.wait_ge(S["lv_kept"], FREE + BLOCKS)

            def early_peaks(a, i, s, k):
                b = EARLY_PAIRS[a][k % len(EARLY_PAIRS[a])]
                pe.wait_ge(att[a]["early_bank_free"], 2 * KT * i + KT * s + k + 1)
                for f in range(2):
                    ins = mm(ps[:, b + f, :], slots[:, bass.ds(i * (4 * SEQ) + s * SEQ + k * P, P)],
                             slots[:, bass.ds(i * (4 * SEQ) + (2 + s) * SEQ + f * 512, 512)], start=True, stop=True)
                ins.then_inc(att[a]["early_scores_ready"], 1)

            for n in range(2):
                pe.wait_ge(att[0]["qk_loaded"][n], 64)
            with pe.Fori(0, BATCH) as i:
                for s in range(2):
                    n = 2 * i + s
                    pe.wait_ge(S["bv_kept"], FREE + 2 * n)
                    mm(ps[:, 4, :], wcol("pe"), y_t[:, blk(i, s)], start=True, stop=True).then_inc(S["pe_ready"], 1)
                    early_peaks(0, i, s, 0)
                    pe.wait_ge(S["xs_kept"], FREE + n + 1)
                    for m in range(2):
                        pe.wait_ge(S["bq_kept"], FREE + 2 * n)
                        at = W1["qkv"] + m * P
                        mm(ps[:, 5 + m, :].rearrange("p (h t) -> p h t", h=8), w1[:, at:at + P], xs[:, :, 0, :],
                           start=True, stop=True).then_inc(S["bq_ready"], 1)
                        early_peaks(0, i, s, 1 + m)
                    for g in range(2):
                        pe.wait_ge(S["bv_kept"], FREE + 2 * n)
                        at = W1["qkv"] + 2 * P
                        for h in range(4):
                            ins = mm(ps[:, (7, 4)[g], h * D:(h + 1) * D], xs[:, 4 * g + h, :, :].rearrange(
                                "p c t -> p (c t)"), w1[:, at:at + P], start=True, stop=True)
                        ins.then_inc(S["bv_ready"], 1)
                        early_peaks(0, i, s, 3 + g)
                    for k in range(5, KT):
                        early_peaks(0, i, s, k)

            def attention(a):
                A = att[a]
                items = Count()

                def peaks(i, c, k):
                    sl = slot[c % SLOTS]
                    if k == 0:
                        use = i + c // SLOTS
                        pe.wait_ge(A["qk_loaded"][c % SLOTS], 64 * (use + 1))
                        pe.wait_ge(A["rows_zeroed"], SLOTS * i + c + 1)
                    b = 2 * (items.n % 2)
                    pe.wait_ge(A["peak_bank_free"], items.next())
                    h, qt = k // KT, k % KT
                    for f in range(2):
                        at = h * SEQ + f * 512
                        ins = mm(ps[:, b + f, :], sl[:, 0, h * SEQ + qt * P:h * SEQ + (qt + 1) * P],
                                 sl[:, 1, at:at + 512], start=True, stop=True)
                    ins.then_inc(A["peak_scores_ready"], 1)

                def turn_maxima(i, c):
                    b = 2 * (items.n % 2)
                    wait_apart(pe, A["m_split_ready"], SLOTS * i + c + 1)
                    wait_apart(pe, A["peak_bank_free"], items.next())
                    nc.tensor.transpose(ps[0:PARTS * 16, b, 0:P // 2].bitcast(BF16),
                                        m_split[:, c % 2].rearrange("p a k -> p (a k)"), ident_b[:, :]).then_inc(
                        A["peak_scores_ready"], 1)

                def scores(i, c, s, tiles):
                    sl = slot[c % SLOTS]
                    if s == 0 and 0 in tiles:
                        pe.wait_ge(A["m_loaded"][c % SLOTS], 16 * (i + c // SLOTS + 1))
                    for q in tiles:
                        tile = 32 * c + 4 * s + q
                        pe.wait_ge(A["probs_done"], 32 * SLOTS * i + tile + 1 - (2 if q % 2 else 4) + CREDIT)
                        h, half = q // 2, q % 2
                        mm(ps[:, SCORE_BANK[q], :], sl[:, 1, h * SEQ + s * P:h * SEQ + (s + 1) * P],
                           sl[:, 0, h * SEQ + half * 512:h * SEQ + (half + 1) * 512],
                           start=True, stop=True).then_inc(A["scores_ready"], 1)

                def sums(i, c, s):
                    if s == 0:
                        pe.wait_ge(A["va_ready"], SLOTS * i + c + 1)
                        pe.wait_ge(A["out_kept"], FREE + SLOTS * i + c)
                    pe.wait_ge(A["probs_done"], 32 * SLOTS * i + 32 * c + 4 * s + 4 + CREDIT)
                    vals = values(a, c)
                    for q in range(4):
                        h = q // 2
                        ins = mm(ps[32 * q:32 * q + 32, 7, :], vals[:, (h * KT + s) * 32:(h * KT + s + 1) * 32],
                                 probabilities(a, s)[:, q * 512:(q + 1) * 512], start=s == 0, stop=s == KT - 1)
                    ins.then_inc(A["av_steps"], 1)

                def unit(i, c, left):
                    plan = peak_plan(left)
                    for s in range(1, KT + 1):
                        def step(tiles):
                            if s < KT:
                                scores(i, c, s, tiles)
                            elif left:
                                scores(i, c + 1, 0, tiles)

                        def for_maxima(items_):
                            for ahead, k in items_:
                                if k is None:
                                    turn_maxima(i, c + ahead)
                                else:
                                    peaks(i, c + ahead, k)

                        step((0, 1))
                        for_maxima(plan[s][:1])
                        step((2,))
                        if a == 0:
                            for_maxima(plan[s][1:])
                            step((3,))
                            sums(i, c, s - 1)
                        else:
                            sums(i, c, s - 1)
                            step((3,))
                            for_maxima(plan[s][1:])

                turn_maxima(0, 0)
                peaks(0, 2, 0)
                peaks(0, 2, 1)
                scores(0, 0, 0, range(4))
                with pe.Fori(0, UNITS // SLOTS - 1) as i:
                    items.enter(i, 17 * SLOTS)
                    for c in range(SLOTS):
                        unit(i, c, 3)
                    items.leave(UNITS // SLOTS - 1)
                for c in range(SLOTS):
                    unit(UNITS // SLOTS - 1, c, 3 - c)

            def project(a, b, w):
                pe.wait_ge(S["ctx_ready"], BATCH * a + b + 1)
                for s in range(2):
                    n = 2 * (BATCH * a + b) + s
                    if n >= 2:
                        pe.wait_ge(S["wo_kept"], n - 1)
                    for j in range(BT):
                        t0 = (s * BT + j) * P
                        ins = mm(ps[:, n % 2, j * P:(j + 1) * P], ctx_t[:, t0:t0 + P], wcol(w), start=True, stop=True)
                    ins.then_inc(S["wo_ready"], 1)

            pe.wait_ge(att[0]["early_bank_free"], len(EARLY_PAIRS[0]) + 2 * 2 * KT)
            pe.wait_ge(S["bq_kept"], FREE + 2 * BLOCKS)
            pe.wait_ge(S["bv_kept"], FREE + 2 * BLOCKS)
            attention(0)

            for b in range(BATCH):
                project(0, b, "o")
                for s in range(2):
                    n = 2 * b + s
                    pe.wait_ge(S["o_n"], n + 1)
                    if n:
                        pe.wait_ge(S["o_t_kept"], n)
                    turn(2, lambda j: stage[:, s, j * P:(j + 1) * P]).then_inc(S["o_t_psum"], 1)
                    pe.wait_ge(S["o_t_kept"], n + 1)
                    for j in range(BT):
                        at = (n * BT + j) * EXP
                        ins = mm(ps[:, 4, at:at + EXP], stage_t[:, s, j * P:(j + 1) * P], wcol("r", EXP),
                                 start=True, stop=True)
                    ins.then_inc(S["route_ready"], 1)
            pe.wait_ge(S["gates_ready"], 1)
            pe.wait_ge(S["wo_kept"], 2 * BATCH)
            for n in range(BLOCKS):
                if n >= 2:
                    pe.wait_ge(S["gt_kept"], n - 1)
                for j in range(BT):
                    ins = nc.tensor.transpose(ps[0:EXP, n % 2, j * P:(j + 1) * P], gates[:, n * BT + j, :], ident)
                ins.then_inc(S["gt_psum"], 1)
            for n in range(BLOCKS):
                pe.wait_ge(S["gt_kept"], BLOCKS + (n - 1 if n >= 2 else 0))
                for j in range(BT):
                    t0 = (n * BT + j) * P
                    ins = mm(ps[:, 2 + n % 2, j * P:(j + 1) * P], g_t[:, t0:t0 + P], be2[:, :], start=True, stop=True)
                ins.then_inc(S["gt_psum"], 1)

            for n in ("we1", "we2"):
                pe.wait_ge(landed[n], 16 * NDMA[n])
            pe.wait_ge(att[1]["rows_zeroed"], SLOTS)
            for n in range(2):
                pe.wait_ge(att[1]["qk_loaded"][n], 64)
            pe.wait_ge(S["gt_kept"], 2 * BLOCKS)
            pe.wait_ge(S["o_t_kept"], BLOCKS)
            with pe.Fori(0, BATCH) as i:
                for s in range(2):
                    n = 2 * i + s

                    def up(e):
                        for fc in range(FC):
                            pe.wait_ge(S["up_done"], FREE + 4 * EXP * n + (4 * e - 3 + fc if e else 0))
                            at = (e * FC + fc) * P
                            mm(ps[:, fc, :], we1[:, at:at + P], o1_t[:, blk(i, s)], start=True, stop=True).then_inc(
                                S["up_ready"], 1)

                    def down(e):
                        pe.wait_ge(S["up_done"], FREE + 4 * (EXP * n + e + 1))
                        pe.wait_ge(S["down_kept"], FREE + EXP * n + (e - 1 if e >= 2 else 0))
                        h = flat((hid0, hid1)[e % 2])
                        for j in range(BT):
                            for fc in range(FC):
                                at = (e * FC + fc) * D
                                ins = mm(ps[:, 4 + e % 2, j * P:(j + 1) * P], h[:, fc * BLK + j * P:fc * BLK + (j + 1) * P],
                                         we2[:, at:at + D], start=fc == 0, stop=fc == FC - 1)
                        ins.then_inc(S["down_ready"], 1)

                    up(0)
                    for e in range(EXP):
                        if e + 1 < EXP:
                            up(e + 1)
                        early_peaks(1, i, s, e)
                        down(e)

            pe.wait_ge(S["up_done"], FREE + 4 * EXP * BLOCKS)
            pe.wait_ge(S["down_kept"], FREE + EXP * BLOCKS)
            pe.wait_ge(att[1]["early_bank_free"], len(EARLY_PAIRS[1]) + 2 * 2 * KT)
            attention(1)
            for b in range(BATCH):
                project(1, b, "ao")

        @block.scalar
        def _(act):
            link = Chain(act, act_seq, wait_apart)
            fn = nc.scalar.activation

            def root(s, ready, n, eps, done):
                act.wait_ge(S[ready], n)
                fn(sd[:, s, :], mv[:, s, :, 1], ACT.Sqrt, bias=eps).then_inc(S[done], 1)

            act.wait_ge(landed["cols"], 16 * NDMA["cols"])
            act.wait_ge(S["consts"], 4)
            with act.Fori(0, BATCH) as i:
                link.enter(i, 4)
                n = 2 * i
                for s in range(2):
                    root(s, "var_ready", 4 * i + s + 1, eps0, "sd_ready")
                for s in range(2):
                    act.wait_ge(S["xn_t_psum"], n + s + 1)
                    fn(xn_t[:, blk(i, s)], ps[:, s, :], ACT.Copy).then_inc(S["xn_t_kept"], 1)
                    root(s, "var_ready", 4 * i + 2 + s + 1, eps0, "sd_ready")
                for s in range(2):
                    act.wait_ge(S["n1_t_psum"], n + s + 1)
                    fn(stage_t[:, s, :], ps[:, 6 + s, :], ACT.Identity, scale=col("g1"), bias=col("b1")).then_inc(
                        S["n1_t_kept"], 1)
                for s in range(2):
                    at = blk(i, s)
                    act.wait_ge(S["qkv_ready"], n + s + 1)
                    for j in range(BT):
                        for h in range(2):
                            m = 2 * j + h
                            ins = fn(qk2[:, s, m * D:(m + 1) * D], ps[:, 2 + j, h * D:(h + 1) * D], ACT.Square,
                                     accum_out=ss[:, s, m:m + 1])
                    link(ins)
                    fn(tiled(v_tok[:, at]), ps[:, 2:2 + BT, 2 * D:3 * D], ACT.Copy)
                    fn(nrm[:, s, :], ss[:, s, :], ACT.Sqrt).then_inc(S["nrm_ready"], 1)
                    act.wait_ge(S["gp_ready"], n + s + 1)
                    fn(zg[:, at], ps[:, 0, :], ACT.Identity, bias=col("gate_b")).then_inc(S["zg_kept"], 1)
                    fn(zp[:, at], ps[:, 6 + s, :], ACT.Identity, bias=col("p_b")).then_inc(S["zp_kept"], 1)
                    act.wait_ge(S["clock_ready"], n + s + 1)
                    fn(zc[:, at], ps[:, (1, 6)[s], :], ACT.Identity, bias=col("clock_b")).then_inc(S["zc_kept"], 1)
                at = bass.ds(i * SEQ, SEQ)
                act.wait_ge(S["zc_kept"], FREE + n + 2)
                fn(tmp[:, at], zg[:, at], ACT.Abs)
                link.apart(fn(tmp2[:, at], zc[:, at], ACT.Abs))
                fn(tmp[:, at], tmp[:, at], ACT.Exp, scale=-1.0)
                link.apart(fn(tmp2[:, at], tmp2[:, at], ACT.Exp, scale=-1.0))
                fn(tmp[:, at], tmp[:, at], ACT.Ln, bias=1.0)
                fn(tmp2[:, at], tmp2[:, at], ACT.Ln, bias=1.0).then_inc(S["logs_ready"], 1)
                for s in range(2):
                    at = blk(i, s)
                    act.wait_ge(S["rope_t_psum"], n + s + 1)
                    fn(q_t[:, at], ps[:, (1, 7)[s], :], ACT.Copy).then_inc(S["q_kept"], 1)
                    fn(k_t[:, at], ps[:, (0, 6)[s], :], ACT.Copy).then_inc(S["k_kept"], 1)
                link.leave(BATCH)

            for n in ("zg_kept", "zp_kept", "zc_kept"):
                act.wait_ge(S[n], FREE + BLOCKS)

            def silu(n, fc, bank):
                act.wait_ge(S["z_ready"], 4 * n + fc + 1)
                act.wait_ge(S["glu_done"], FREE + 4 * n + (fc - 1 if fc >= 2 else 0))
                fn(sil[:, fc % 2, :], ps[:, bank, :], ACT.Silu, scale=col("s1", fc)).then_inc(S["sil_done"], 1)

            def gelu(layer, n, oc, bank):
                ready, done, free, dst, scales = (
                    (), ("h1_ready", "h1_done", "h2_ready", hid1, "t1"), ("h2_ready", "h2_done", "y_ready", hid2, "t2"))[layer]
                if oc == 0:
                    act.wait_ge(S[free], FREE + (4, 1)[layer - 1] * n)
                act.wait_ge(S[ready], FREE + 4 * n + oc + 1)
                fn(flat(dst)[:, oc * BLK:(oc + 1) * BLK], ps[:, bank, :], ACT.Gelu,
                   scale=col(scales, oc)).then_inc(S[done], 1)

            with act.Fori(0, BATCH) as i:
                at = bass.ds(i * SEQ, SEQ)
                for fc in range(FC):
                    silu(i, fc, fc % 2)
                wait_apart(act, S["pm_ready"], i + 1)
                fn(zp[:, at], zp[:, at], ACT.Exp, bias=pm[:, 0:1]).then_inc(S["p_exp"], 1)
                wait_apart(act, S["decay_ready"], i + 1)
                fn(zg[:, at], tmp[:, at], ACT.Exp).then_inc(S["decay_exp"], 1)
                for oc in range(FC):
                    gelu(1, i, oc, 4 + oc % 2)
                for oc in range(FC):
                    gelu(2, i, oc, 6 + oc % 2)

            with act.Fori(0, BATCH) as i:
                def exps(qt):
                    act.wait_ge(S["peak_ready"], KT * i + qt + 1)
                    act.wait_ge(S["p_t_psum"], FREE + KT * i + (qt - 1 if qt >= 2 else 0))
                    pair = ps[:, 0:2, :].rearrange("p a b -> p (a b)")
                    fn(probs[:, qt % 2, 0:(qt + 1) * P], pair[:, 0:(qt + 1) * P], ACT.Exp, scale=1.0 / math.sqrt(D),
                       bias=nm[:, 2 + qt % 2:3 + qt % 2], accum_out=sm[:, qt % 2:qt % 2 + 1]).then_inc(S["exp_done"], 1)

                def mlp_group(kind, k):
                    if kind == "z":
                        silu(2 + i, k, 5)
                    elif kind == "h1":
                        gelu(1, 2 + i, k, 5 + k % 2)
                    elif kind == "h2":
                        gelu(2, 2 + i, k, 5 + k % 2)

                exps(0)
                for qt in range(KT):
                    if qt + 1 < KT:
                        exps(qt + 1)
                    groups = list(MLP_GROUPS[qt])
                    if groups and groups[0][0] == "z":
                        mlp_group(*groups.pop(0))
                    act.wait_ge(S["p_t_psum"], FREE + KT * i + qt + 1)
                    act.wait_ge(S["av_ready"], FREE + KT * i + qt)
                    fn(probs_t[:, 0:(qt + 1) * P], ps[:, 2:4, :].rearrange("p a b -> p (a b)")[:, 0:(qt + 1) * P],
                       ACT.Copy).then_inc(S["p_t_kept"], 1)
                    for group in groups:
                        mlp_group(*group)

            with act.Fori(0, BATCH) as i:
                for s in range(2):
                    root(s, "m_var", 2 * i + s + 1, eps0, "m_sd")
                for s, bank in enumerate((0, 7)):
                    act.wait_ge(S["m_t_psum"], 2 * i + s + 1)
                    fn(stage_t[:, s, :], ps[:, bank, :], ACT.Identity, scale=col("g2"), bias=col("b2")).then_inc(
                        S["m_t_kept"], 1)
                for s in range(2):
                    n = 2 * i + s
                    act.wait_ge(S["m2_ready"], FREE + 2 * i)
                    for fc in range(FC):
                        act.wait_ge(S["m1_ready"], 4 * n + fc + 1)
                        fn(flat((hid0, hid1)[s])[:, fc * BLK:(fc + 1) * BLK], ps[:, 1 + fc, :], ACT.Gelu,
                           bias=col("mb1", fc)).then_inc(S["m1_done"], 1)

            with act.Fori(0, BATCH) as i:
                for s in range(2):
                    root(s, "l_var", 2 * i + s + 1, eps0, "l_sd")
                for s, bank in enumerate((0, 7)):
                    at = blk(i, s)
                    act.wait_ge(S["l_t_psum"], 2 * i + s + 1)
                    fn(stage_t[:, s, :], ps[:, bank, :], ACT.Copy)
                    fn(x3_t[:, at], ps[:, bank, :], ACT.Copy).then_inc(S["l_t_kept"], 1)
                for s in range(2):
                    n, at = 2 * i + s, blk(i, s)
                    for m, parts in enumerate((q_parts, k_parts)):
                        act.wait_ge(S["lq_ready"], 2 * n + m + 1)
                        fn(parts[:, 0, at], ps[:, 1 + 2 * s + m, :], ACT.Copy).then_inc(S["hi_kept"], 1)
                for s in range(2):
                    act.wait_ge(S["lv_ready"], 2 * i + s + 1)
                    for j in range(BT):
                        dst = v1[:, bass.ds(i * SEQ, SEQ)].rearrange("p (u h k j) -> p u h k j", u=8, h=2, k=KT)
                        ins = fn(dst[:, :, :, 4 * s + j, :], ps[:, 5 + s, j * P:(j + 1) * P].rearrange(
                            "p (u h j) -> p u h j", u=8, h=2), ACT.Copy)
                    ins.then_inc(S["lv_kept"], 1)
            with act.Fori(0, BATCH) as i:
                for s in range(2):
                    n, at = 2 * i + s, blk(i, s)
                    for m, dst in enumerate((q_b, k_b)):
                        act.wait_ge(S["bq_ready"], 2 * n + m + 1)
                        fn(dst[:, at], ps[:, 5 + m, :], ACT.Copy).then_inc(S["bq_kept"], 1)
                    for g in range(2):
                        act.wait_ge(S["bv_ready"], FREE + 2 * n + g + 1)
                        for c in range(2):
                            rng = slice(64 * c, 64 * c + 64)
                            vals = ps[rng, (7, 4)[g], :].rearrange("p (a c j) -> p a c j", c=2, j=HD)[:, :, c, :]
                            dst = v2[rng, bass.ds(i * 1024 + s * 512 + g * 256, 256)]
                            ins = fn(dst.rearrange("p (a j) -> p a j", j=HD), vals, ACT.Copy)
                        ins.then_inc(S["bv_kept"], 1)

            def attention(a):
                A = att[a]

                def exps(i, c, s):
                    act.wait_ge(A["av_steps"], SLOTS * KT * i + KT * c + s - 1 + PCREDIT)
                    for q in range(4):
                        act.wait_ge(A["scores_ready"], 32 * SLOTS * i + 32 * c + 4 * s + q + 1)
                        fn(probabilities(a, s)[:, q * 512:(q + 1) * 512], ps[:, SCORE_BANK[q], :], ACT.Exp,
                           scale=HEAD_SCALE[a]).then_inc(A["probs_done"], 1)

                def keep(i, c):
                    act.wait_ge(A["av_steps"], SLOTS * KT * i + KT * (c + 1) + PCREDIT)
                    act.wait_ge(A["out_stored"][c % 2], FREE + 16 * (SLOTS // 2 * i + c // 2))
                    fn(o_st[c % 2], ps[:, 7, :], ACT.Copy).then_inc(A["out_kept"], 1)

                def unit(i, c, left):
                    for s in range(1, KT):
                        exps(i, c, s)
                    if left:
                        exps(i, c + 1, 0)
                    keep(i, c)

                exps(0, 0, 0)
                with act.Fori(0, UNITS // SLOTS - 1) as i:
                    for c in range(SLOTS):
                        unit(i, c, 3)
                for c in range(SLOTS):
                    unit(UNITS // SLOTS - 1, c, 3 - c)

            act.wait_ge(parts_stored, 16 * PARTS_STORES)
            attention(0)

            for n in range(BLOCKS):
                s = n % 2
                root(s, "o_var", n + 1, eps1, "o_sd")
                act.wait_ge(S["o_t_psum"], n + 1)
                fn(o1_t[:, n * BLK:(n + 1) * BLK], ps[:, 2, :], ACT.Copy)
                fn(stage_t[:, s, :], ps[:, 2, :], ACT.Copy).then_inc(S["o_t_kept"], 1)
            act.wait_ge(S["route_sum"], 1)
            fn(tk[:, 2, :], tk[:, 0, :], ACT.Exp).then_inc(S["route_exp"], 1)
            act.wait_ge(S["route_sum"], 2)
            fn(tk[:, 10, 0:TILES], tk[:, 9, 0:TILES], ACT.Exp).then_inc(S["route_exp"], 1)

            with act.Fori(0, BATCH) as i:
                for s in range(2):
                    n = 2 * i + s
                    for e in range(EXP):
                        act.wait_ge(S["down_ready"], FREE + EXP * n + (e - 1 if e >= 2 else 0))
                        for fc in range(FC):
                            act.wait_ge(S["up_ready"], 4 * EXP * n + 4 * e + fc + 1)
                            fn(flat((hid0, hid1)[e % 2])[:, fc * BLK:(fc + 1) * BLK], ps[:, fc, :], ACT.Gelu,
                               bias=col("be1", e * FC + fc)).then_inc(S["up_done"], 1)
                    root(s, "f_var", n + 1, eps1, "f_sd")

            attention(1)

        @block.gpsimd
        def _(pool):
            g = nc.gpsimd
            for semaphore in free_at_start:
                pool.sem_inc(semaphore, FREE)
            for a in range(2):
                pool.sem_inc(att[a]["early_bank_free"], len(EARLY_PAIRS[a]))
            g.memset(eps0, EPS0).then_inc(S["consts"], 1)
            g.memset(eps1, EPS1).then_inc(S["consts"], 1)
            g.memset(one_col[:, :], 1.0).then_inc(S["consts"], 1)
            pool.wait_ge(landed["cst"], 16 * NDMA["cst"])
            g.tensor_copy(ident_b[:, :], ident).then_inc(S["consts"], 1)

            def attention(a):
                A = att[a]
                pool.sem_inc(A["probs_done"], CREDIT)
                pool.sem_inc(A["peak_bank_free"], PCREDIT)
                pool.sem_inc(A["av_steps"], PCREDIT)
                for n in range(SLOTS):
                    if a == 0 and n == SLOTS - 1:
                        pool.wait_ge(parts_stored, 16 * PARTS_STORES)
                    g.memset(r[5 + n], 0.0).then_inc(pool_seq, 1)
                    pool.wait_ge(pool_seq, (SLOTS + 2) * a + n + 1)
                    g.memset(slot[n][MROW:MROW + PARTS, 1, :], 1.0).then_inc(A["slots_ready"], 1)
                    pool.wait_ge(A["slots_ready"], n + 1)
                for n in range(2):
                    g.memset(values(a, n), 1.0).then_inc(pool_seq, 1)
                pool.wait_ge(pool_seq, (SLOTS + 2) * a + SLOTS + 2)

                def values_of(i, c):
                    src = v1 if a == 0 else v2
                    g.tensor_copy(values(a, c).rearrange("p (m w) -> p m w", w=32)[:, :, 0:HD],
                                  src[:, bass.ds(i * (SLOTS * P) + c * P, P)].rearrange("p (m j) -> p m j", j=HD)).then_inc(
                        A["va_ready"], 1)

                def unit(i, c, left):
                    if left:
                        pool.wait_ge(A["rows_zeroed"], SLOTS * i + c + SLOTS if left > 3 else UNITS)
                        pool.wait_ge(A["av_steps"], SLOTS * KT * i + KT * c + PCREDIT)
                        values_of(i, c + 1)
                    if left > 3:
                        pool.wait_ge(A["va_ready"], SLOTS * i + c + 2)
                        wait_apart(pool, A["av_steps"], SLOTS * KT * i + KT * (c + 1) + PCREDIT)
                        g.memset(slot[c][MROW:MROW + PARTS, 0, :], 0.0).then_inc(A["rows_zeroed"], 1)

                pool.sem_inc(A["rows_zeroed"], SLOTS)
                if a == 0:
                    pool.wait_ge(S["lv_kept"], FREE + BLOCKS)
                values_of(0, 0)
                with pool.Fori(0, UNITS // SLOTS - 1) as i:
                    for c in range(SLOTS):
                        unit(i, c, 4)
                for c in range(SLOTS):
                    unit(UNITS // SLOTS - 1, c, 3 - c)

            pool.wait_ge(S["x2_kept"], FREE + BLOCKS)
            pool.wait_ge(S["y_done"], FREE + BLOCKS)
            attention(0)
            pool.wait_ge(S["ctx_ready"], 1)
            attention(1)

        @block.sync
        def _(sp):
            def load(name, dst, src):
                sp.dma_start(dst, src).then_inc(landed[name], 16)

            xv = t["L0_attn_x"].rearrange("b (n p) d -> p (b n) d", p=P)
            xt3 = x_tok.rearrange("p (n d) -> p n d", d=D)
            for n in range(BLOCKS):
                load("x", xt3[:, n * BT:(n + 1) * BT, :], xv[:, n * BT:(n + 1) * BT, :])
            load("cst", cst[:, :], t["consts"])
            load("cols", cols[:, :], t["cols"])
            for m, name in enumerate(("L0_attn_out_b", "L0_attn_mlp_b2", "L0_ffn_w3_s", "L1_ffn_bo", "L1_ffn_ln1_g",
                                      "L1_ffn_ln1_b", "L1_ffn_ln2_g", "L1_ffn_ln2_b")):
                load("rows", rows[:, m, :], t[name].partition_broadcast(P))
            load("w0", w0[:, :], t["w0"])
            load("wf", wf[:, :], t["wf"])
            load("w1", w1[:, :], t["w1"])
            load("we1", we1[:, :].rearrange("p (e f) -> p e f", e=EXP), t["L1_ffn_We1"].rearrange("e d f -> d e f"))
            load("we2", we2[:, :].rearrange("p (e c d) -> p e c d", e=EXP, c=FC),
                 t["L1_ffn_We2"].rearrange("e (c p) d -> p e c d", p=P))
            load("we2", be2[:, :], t["L1_ffn_be2"])

            with sp.Fori(0, BATCH) as i:
                for s in range(2):
                    for m, (dram, parts, runs) in enumerate(((qs_dram, q_parts, Q_RUNS), (ks_dram, k_parts, K_RUNS))):
                        sp.wait_ge(S["parts_kept"], FREE + 2 * (2 * i + s) + m + 1)
                        for first, count, part in runs:
                            dst = dram[first:first + count, bass.ds(i, 1), :, s * BLK:(s + 1) * BLK].rearrange(
                                "m b p t -> (b p) m t")
                            if m == 0:
                                src = parts[:, part, blk(i, s)].unsqueeze(1).to_broadcast([P, count, BLK])
                            else:
                                src = parts[:, part:part + count, blk(i, s)]
                            sp.dma_start(dst, src).then_inc(parts_stored, 16)

            def attention(a):
                A = att[a]
                if a == 0:
                    heads = [d.rearrange("m b (u h j) t -> (b u) h m j t", u=8, h=2) for d in (qs_dram, ks_dram)]
                    n_rows = len(Q_PARTS) * HD
                else:
                    heads = [d.rearrange("(c j) (u h t) -> u h j c t", c=HEADS, h=2, t=64) for d in (qb_dram, kb_dram)]
                    n_rows = HD

                def fetch(i, c):
                    for m in range(2):
                        for h in range(2):
                            sp.dma_start(slot[c % SLOTS][0:n_rows, m, h * SEQ:(h + 1) * SEQ],
                                         one_of(heads[m], i * SLOTS + c)[h]).then_inc(A["qk_loaded"][c % SLOTS], 16)

                items = Count()

                def maxima(c):
                    sp.wait_ge(A["peak_bank_free"], items.seen() + PCREDIT)
                    sp.dma_start(slot[c % SLOTS][MROW:MROW + PARTS, 0, :].rearrange("p (k q) -> p k q", q=P),
                                 m_t[:, c % 2, :]).then_inc(A["m_loaded"][c % SLOTS], 16)

                def unit(i, c, left):
                    for s in range(1, KT + 1):
                        for ahead, k in peak_plan(min(left, 3))[s]:
                            items.next()
                            if k is None:
                                maxima(c + ahead)
                    sp.wait_ge(A["av_steps"], SLOTS * KT * i + KT * (c + 1) + PCREDIT)
                    if left > 3:
                        fetch(i, c + SLOTS)
                    sp.wait_ge(A["out_kept"], FREE + SLOTS * i + c + 1)
                    sp.dma_start(one_of(o_dram[a], i * SLOTS + c), o_st[c % 2]).then_inc(A["out_stored"][c % 2], 16)

                for c in range(SLOTS):
                    sp.wait_ge(A["slots_ready"], c + 1)
                    fetch(0, c)
                if a == 0:
                    sp.wait_ge(S["bq_kept"], FREE + 2 * BLOCKS)
                    sp.dma_start(qb_dram, q_b).then_inc(b_stored, 16)
                    sp.dma_start(kb_dram, k_b).then_inc(b_stored, 16)
                items.next()
                maxima(0)
                items.next()
                items.next()
                with sp.Fori(0, UNITS // SLOTS - 1) as i:
                    items.enter(i, 17 * SLOTS)
                    for c in range(SLOTS):
                        unit(i, c, 4)
                    items.leave(UNITS // SLOTS - 1)
                for c in range(SLOTS):
                    unit(UNITS // SLOTS - 1, c, 3 - c)
                for n in range(2):
                    sp.wait_ge(A["out_stored"][n], FREE + 16 * UNITS // 2)
                for b in range(BATCH):
                    if b:
                        sp.wait_ge(S["ctx_ready"], BATCH * a + b)
                    src = o_dram[a][b * 8:(b + 1) * 8].rearrange("u (h q m) t -> u h m q t", h=2, q=2)
                    for q in range(2):
                        at = slice(512 * q, 512 * (q + 1))
                        sp.dma_start(o_in[:, at], src[:, :, 0:HD, q]).then_inc(A["out_back"], 16)
                        sp.dma_start(den[:, at], src[:, :, HD:2 * HD, q]).then_inc(A["out_back"], 16)

            sp.wait_ge(parts_stored, 16 * PARTS_STORES)
            attention(0)
            sp.wait_ge(b_stored, 32)
            attention(1)
            ov = out.rearrange("b (n p) d -> p (b n) d", p=P)
            for n in range(BLOCKS):
                sp.wait_ge(S["wo_kept"], 2 * BATCH + n + 1)
                sp.dma_start(ov[:, n * BT:(n + 1) * BT, :], xt3[:, n * BT:(n + 1) * BT, :]).then_inc(stored, 16)
            sp.wait_ge(stored, 16 * BLOCKS)


def laid_out(x):
    n = lambda k: np.asarray(x[k])
    chunks = lambda w: w.reshape(-1, P, w.shape[1]).transpose(1, 0, 2).reshape(P, -1)
    vec = lambda v: v.reshape(-1, P).T
    clock = np.repeat(n("L0_attn_clock_W"), P, axis=1)
    w0 = [n("L0_attn_Wq"), n("L0_attn_Wk"), n("L0_attn_Wv"), n("L0_attn_gate_W"), n("L0_attn_p_W"), clock,
          n("L0_attn_out_W"), n("L0_attn_mlp_W1"), chunks(n("L0_attn_mlp_W2"))]
    wf = [n("L0_ffn_w1_w").T, n("L0_ffn_w2_w").T, chunks(n("L0_ffn_h1_w").T), chunks(n("L0_ffn_h2_w").T),
          chunks(n("L0_ffn_w3_w").T)]
    w1 = [n("L1_attn_pe_w").T, n("L1_attn_qkv_w").T, n("L1_attn_out_w").T, n("L1_ffn_Wq"), n("L1_ffn_Wk"),
          n("L1_ffn_Wv"), n("L1_ffn_Wo"), n("L1_ffn_Wr")]
    cols = [vec(n("L0_attn_gate_b")), vec(n("L0_attn_p_b")), np.repeat(n("L0_attn_clock_b"), P)[:, None]]
    cols += [vec(n("L0_attn_" + k)) for k in ("ln1_g", "ln1_b", "ln2_g", "ln2_b", "mlp_b1")]
    cols += [vec(n("L0_ffn_" + k)) for k in ("w1_s", "w2_s", "h1_s", "h2_s")]
    cols += [vec(n("L1_ffn_be1")), n("L1_attn_conv_w")[:, 0, :, 1]]
    return {"w0": np.concatenate(w0, 1), "wf": np.concatenate(wf, 1), "w1": np.concatenate(w1, 1),
            "cols": np.concatenate(cols, 1)}


def constants():
    half = D // 2
    freqs = np.exp(-np.arange(half, dtype=np.float32) * np.float32(math.log(10000.0) / half)).astype(np.float32)
    th = np.arange(SEQ, dtype=np.float32)[:, None] * freqs[None, :]
    c = np.repeat(np.cos(th.astype(np.float64)), 2, axis=1)
    s = np.stack([-np.sin(th.astype(np.float64)), np.sin(th.astype(np.float64))], -1).reshape(SEQ, D)
    tiles = lambda a: a.reshape(KT, P, D).transpose(1, 0, 2).reshape(P, KT * D)
    above = np.triu(np.ones((P, P)), 1) * -3e38
    rank = np.broadcast_to(np.arange(EXP, 0, -1), (P, EXP))
    return np.concatenate([np.eye(P), above, tiles(c), tiles(s), rank], 1).astype(np.float32)


_PLAIN = ["L0_attn_x", "L0_attn_out_b", "L0_attn_mlp_b2", "L0_ffn_w3_s", "L1_ffn_bo", "L1_ffn_ln1_g", "L1_ffn_ln1_b",
          "L1_ffn_ln2_g", "L1_ffn_ln2_b", "L1_ffn_We1", "L1_ffn_We2", "L1_ffn_be2"]


def kernel(**inputs):
    import concourse.bacc as bacc
    from concourse.bass_utils import run_bass_kernel_spmd

    arrays = {k: np.ascontiguousarray(inputs[k]) for k in _PLAIN}
    arrays |= {k: np.ascontiguousarray(a) for k, a in laid_out(inputs).items()}
    arrays["consts"] = constants()
    nc = bacc.Bacc("TRN2", target_bir_lowering=False, num_devices=1)
    t = {k: nc.dram_tensor("in_" + k, a.shape, mybir.dt.from_np(a.dtype), kind="ExternalInput").ap()
         for k, a in arrays.items()}
    out = nc.dram_tensor("out", (BATCH, SEQ, D), F32, kind="ExternalOutput").ap()
    build(nc, t, out)
    r = run_bass_kernel_spmd(nc, [{"in_" + k: a for k, a in arrays.items()}], core_ids=[0])
    return r.results[0]["out"]
```

```python
from contextlib import ExitStack
import math

import numpy as np
import concourse.bass as bass
from concourse import mybir

ALU = mybir.AluOpType
ACT = mybir.ActivationFunctionType
AX = mybir.AxisListType
F32 = mybir.dt.float32
BF16 = mybir.dt.bfloat16

P = 128
D = 128
BATCH, SEQ = 2, 1024
TOK = BATCH * SEQ
TILES = TOK // P
BT = 4
BLK = BT * P
BLOCKS = TOK // BLK
HID = 512
FC = HID // P
EXP = 8
HEADS, HD = 16, 8
UNITS = BATCH * HEADS // 2
KT = SEQ // P
PARTS = 3
EPS0, EPS1 = 1e-5, 1e-6
MROW = 64
SLOTS = 4
MLP_GROUPS = ((("z", 0), ("z", 1)), (("z", 2), ("z", 3)), (("h1", 0), ("h1", 1)), (("h1", 2), ("h1", 3)),
              (("h2", 0), ("h2", 1)), (("h2", 2), ("h2", 3)), (("y", 0), ("y", 1)), ())
EARLY_PAIRS = ((0, 2), (6,))
FREE = 1
CREDIT = 3
PCREDIT = 2
SCORE_BANK = (4, 5, 6, 5)
N_PRODUCTS = 6
Q_RUNS = ((0, 3, 0), (3, 2, 1), (5, 1, 2))
K_RUNS = ((0, 3, 0), (3, 2, 0), (5, 1, 0))
HEAD_SCALE = (1.0 / math.sqrt(HD), 1.0 / 2.828125)
NDMA = dict(x=BLOCKS, cst=1, cols=9, w0=1, wf=1, w1=1, we1=1, we2=2)

W0 = dict(qkv=0, gate=384, p=512, clock=640, out=768, m1=896, m2=1408)
W0N = 1920
WF = dict(w1=0, w2=512, h1=1024, h2=3072, w3=5120)
WFN = 5632
W1 = dict(pe=0, qkv=128, ao=512, q=640, k=768, v=896, o=1024, r=1152)
W1N = 1160
COLS = ["gate_b", "p_b", "clock_b", "g1", "b1", "g2", "b2"]
ROWS = ["out_b", "mlp_b2", "w3_s", "bo", "l1g", "l1b", "l2g", "l2b"]
C4 = ["mb1", "s1", "s2", "t1", "t2"]
CC = {n: i for i, n in enumerate(COLS)}
for _i, _n in enumerate(C4):
    CC[_n] = len(COLS) + 4 * _i
CC["be1"] = len(COLS) + 4 * len(C4)
CC["conv"] = CC["be1"] + 4 * EXP
CN = CC["conv"] + 3
CST = dict(ident=0, mask=128, cos=256, sin=256 + KT * D, rank=256 + 2 * KT * D)
CSTN = 256 + 2 * KT * D + EXP


class Chain:

    def __init__(self, eng, sem, wait_apart):
        self.eng, self.sem, self.wait_apart, self.n, self.reg = eng, sem, wait_apart, 0, None

    def mark(self, ins):
        ins.then_inc(self.sem, 1)
        self.n += 1

    def wait(self):
        self.eng.wait_ge(self.sem, self.n if self.reg is None else self.reg + self.n)

    def __call__(self, ins):
        self.mark(ins)
        self.wait()

    def apart(self, ins):
        self.mark(ins)
        self.wait_apart(self.eng, self.sem, self.n if self.reg is None else self.reg + self.n)

    def enter(self, i, per):
        self.reg, self.start, self.per = i * per, self.n, per

    def leave(self, rounds):
        assert self.n - self.start == self.per, (self.n - self.start, self.per)
        self.reg, self.n = None, self.start + rounds * self.per


class Count:

    def __init__(self):
        self.n, self.reg = 0, None

    def seen(self):
        return self.n if self.reg is None else self.reg + self.n

    def next(self):
        self.n += 1
        return self.seen()

    def enter(self, i, per):
        self.reg, self.start, self.per = i * per, self.n, per

    def leave(self, rounds):
        assert self.n - self.start == self.per
        self.reg, self.n = None, self.start + rounds * self.per


def peak_plan(left):
    plan = {s: [] for s in range(1, KT + 1)}
    for s in range(1, KT):
        if left >= 2:
            plan[s] += [(2, 2 * s), (2, 2 * s + 1)]
        if s == 2 and left >= 1:
            plan[s].append((1, None))
    if left >= 3:
        plan[KT] += [(3, 0), (3, 1)]
    return plan


def build(nc, t, out):
    ctx = ExitStack()
    with ctx:
        def sb(name, shape, dt=F32):
            return ctx.enter_context(nc.sbuf_tensor(name, shape, dt))

        def sem(name):
            return ctx.enter_context(nc.semaphore(name))

        ps = ctx.enter_context(nc.psum_tensor("ps", [P, 8, 512], F32))
        w0 = sb("w0", [P, W0N])
        wf = sb("wf", [P, WFN])
        w1 = sb("w1", [P, W1N])
        we1 = sb("we1", [P, EXP * HID])
        we2 = sb("we2", [P, EXP * FC * D])
        cols = sb("cols", [P, CN])
        cst = sb("cst", [P, CSTN])
        rows = sb("rows", [P, len(ROWS), D])
        ident = cst[:, 0:P]
        big = sb("big", [P, 11 * TOK])
        r = [big[:, n * TOK:(n + 1) * TOK] for n in range(11)]
        x_tok, xn_tok, xn_t, v_tok, q_t, k_t, zg, zp, zc, tmp, tmp2 = r
        stage = sb("stage", [P, 2, BLK])
        stage1 = sb("stage1", [P, 2, BLK])
        stage_t = sb("stage_t", [P, 2, BLK])
        qk = sb("qk", [P, 2, 2 * BLK])
        qk1 = sb("qk1", [P, 2, 2 * BLK])
        qk2 = sb("qk2", [P, 2, 2 * BLK])
        st = sb("st", [P, 2, BT, 6])
        mv = sb("mv", [P, 2, BT, 2])
        sd = sb("sd", [P, 2, BT])
        rs = sb("rs", [P, 2, BT])
        ss = sb("ss", [P, 2, 2 * BT])
        nrm = sb("nrm", [P, 2, 2 * BT])
        rn = sb("rn", [P, 2, 2 * BT])
        pm = sb("pm", [P, BATCH])
        nm = sb("nm", [P, 4])
        sm = sb("sm", [P, 4])
        gates = sb("gates", [P, TILES, EXP])
        sil, hid0, hid1, hid2 = stage, qk, qk1, qk2
        q_s, k_s = r[6][:, 0:SEQ], r[6][:, SEQ:TOK]
        v_s, ao_t = r[7][:, 0:SEQ], r[7][:, SEQ:TOK]
        probs = r[8].rearrange("p (a t) -> p a t", a=2)
        probs_t = r[9][:, 0:SEQ]
        x3_tok, x3_t, y_t, v1 = r[1], r[2], r[3], r[4]
        q_parts = big[:, 8 * TOK:8 * TOK + 3 * TOK // 2].bitcast(BF16).rearrange("p (a t) -> p a t", a=PARTS)
        k_parts = big[:, 8 * TOK + 3 * TOK // 2:11 * TOK].bitcast(BF16).rearrange("p (a t) -> p a t", a=PARTS)
        q_b, k_b = (qk2[:, n, :].bitcast(BF16) for n in range(2))
        slots = big[:, 5 * TOK:(5 + SLOTS) * TOK].bitcast(BF16)
        slot = [r[5 + n].bitcast(BF16).rearrange("p (a t) -> p a t", a=2) for n in range(SLOTS)]
        pr = [r[9 + n] for n in range(2)]
        o_in, den = r[2][:, 0:SEQ], r[2][:, SEQ:TOK]
        ctx_t = r[3][:, 0:SEQ]
        o_st = [r[3][:, SEQ + n * 512:SEQ + (n + 1) * 512] for n in range(2)]
        va = [wf[:, n * 512:(n + 1) * 512] for n in range(4)]
        v2 = wf[:, 2048:2048 + TOK // 2].bitcast(BF16)
        neg_m = sb("neg_m", [P, 2, 16])
        m_rest = sb("m_rest", [P, 2, 16])
        m_split = sb("m_split", [P, 2, PARTS, 16], BF16)
        m_t = sb("m_t", [PARTS * 16, 2, P], BF16)
        ident_b = sb("ident_b", [P, P], BF16)
        o1_t = r[4]
        g_t = r[2][0:EXP, 0:2 * BLK]
        xs = qk1[:, 0, :].rearrange("p (h c t) -> p h c t", h=8, c=2)
        gb = sb("gb", [P, 2, BT * EXP])
        be2 = sb("be2", [EXP, D])
        one_col = sb("one_col", [P, 1])
        eps0, eps1 = (sb(f"eps{n}", [P, 1])[:, :] for n in range(2))
        tk = wf[:, 3072:3072 + 12 * TILES * EXP].rearrange("p (k m) -> p k m", k=12)
        qs_dram = nc.dram_tensor("qs_dram", (N_PRODUCTS, BATCH, P, SEQ), BF16, kind="Internal").ap()
        ks_dram = nc.dram_tensor("ks_dram", (N_PRODUCTS, BATCH, P, SEQ), BF16, kind="Internal").ap()
        qb_dram = nc.dram_tensor("qb_dram", (P, TOK), BF16, kind="Internal").ap()
        kb_dram = nc.dram_tensor("kb_dram", (P, TOK), BF16, kind="Internal").ap()
        o_dram = [nc.dram_tensor(f"o_dram{n}", (UNITS, P, 512), F32, kind="Internal").ap() for n in range(2)]

        landed = {n: sem("in_" + n) for n in NDMA}
        dve_seq, act_seq, pool_seq = (sem(n + "_seq") for n in ("dve", "act", "pool"))
        stored = sem("stored")
        S = {n: sem(n) for n in (
            "consts var_ready sd_ready xn_ready n1_ready xn_t_psum n1_t_psum n1_t_kept xn_t_kept qkv_ready gp_ready "
            "clock_ready nrm_ready qk_scaled rope_ready rope_t_psum zg_kept zp_kept zc_kept q_kept k_kept "
            "z_ready sil_done glu_done h1_ready h1_done h2_ready h2_done y_ready y_done pm_ready logs_ready "
            "p_exp decay_ready decay_exp "
            "batch_staged s_ready peak_ready exp_done p_ready p_t_psum p_t_kept av_ready av_kept x2_ready x2_kept "
            "m_var m_sd m_n m_t_psum m_t_kept m1_ready m1_done m2_ready m2_kept "
            "l_var l_sd l_n l_t_psum l_t_kept lq_ready hi_kept parts_kept lv_ready lv_kept conv_done pe_ready "
            "xs_kept bq_ready bq_kept bv_ready bv_kept o_var o_sd o_n o_t_psum o_t_kept route_ready "
            "route_exp route_sum gates_ready gt_psum gt_kept up_ready up_done down_ready down_kept f_var f_sd "
            "ctx_ready wo_ready wo_kept bo_added o_kept gb_ready").split()}
        att = [{n: sem(f"{n}{a}") for n in (
            "peak_scores_ready peak_bank_free scores_ready probs_done av_steps out_kept m_split_ready "
            "va_ready rows_zeroed slots_ready out_back early_scores_ready early_bank_free").split()} for a in range(2)]
        for a in range(2):
            att[a]["out_stored"] = [sem(f"out_stored{a}_{n}") for n in range(2)]
            att[a]["qk_loaded"] = [sem(f"qk_loaded{a}_{n}") for n in range(SLOTS)]
            att[a]["m_loaded"] = [sem(f"m_loaded{a}_{n}") for n in range(SLOTS)]
        parts_stored, b_stored = sem("parts_stored"), sem("b_stored")
        PARTS_STORES = BLOCKS * (len(Q_RUNS) + len(K_RUNS))
        free_at_start = [S[n] for n in (
            "k_kept q_kept qk_scaled zg_kept zp_kept zc_kept y_done glu_done h1_done h2_done h1_ready h2_ready y_ready "
            "exp_done p_t_kept p_t_psum av_ready av_kept x2_kept m_t_kept m1_done m2_kept m2_ready l_t_kept parts_kept "
            "lv_kept xs_kept bq_kept bv_kept bv_ready up_done down_kept down_ready").split()]
        for A in att:
            free_at_start += [A["out_kept"], *A["out_stored"]]

        block = ctx.enter_context(nc.Block())

        def wait_apart(eng, semaphore, value):
            if not isinstance(value, int):
                eng.compute_val(value)
                eng.wait_ge(S["consts"], 1)
            eng.wait_ge(semaphore, value)

        def flat(a):
            return a[:, :, :].rearrange("p a b -> p (a b)")

        def tiled(a):
            return a.rearrange("p (j d) -> p j d", d=D)

        def rep(name):
            return rows[:, ROWS.index(name), :].unsqueeze(1).to_broadcast([P, BT, D])

        def values(a, c):
            return va[c % 2] if a == 0 else va[2 + c % 2].bitcast(BF16)[:, 0:512]

        def probabilities(a, s):
            return pr[s % 2] if a == 0 else pr[s % 2].bitcast(BF16)[:, 0:4 * 512]

        def one_of(ap, n):
            return ap[n] if isinstance(n, int) else ap[bass.ds(n, 1)].squeeze(0)

        def blk(i, s):
            return bass.ds(i * (2 * BLK) + s * BLK, BLK)

        def tile_cols(i, s, j):
            return bass.ds(i * (2 * BLK) + (s * BT + j) * P, P)

        def col(name, n=0):
            return cols[:, CC[name] + n:CC[name] + n + 1]

        @block.vector
        def _(dve):
            link = Chain(dve, dve_seq, wait_apart)
            v = nc.vector

            def stats(s, src, ready):
                for j in range(BT):
                    ins = v.bn_stats(st[:, s, j, :], src(j))
                link.apart(ins)
                for j in range(BT):
                    ins = v.bn_aggr(mv[:, s, j, :], st[:, s, j, :])
                ins.then_inc(S[ready], 1)

            def normalise(s, src, dst, sd_ready, n, done):
                dve.wait_ge(S[sd_ready], n)
                link(v.reciprocal(rs[:, s, :], sd[:, s, :]))
                for j in range(BT):
                    ins = v.tensor_scalar(dst(j), src(j), mv[:, s, j, 0:1], rs[:, s, j:j + 1], ALU.subtract, ALU.mult)
                if done is None:
                    link(ins)
                else:
                    ins.then_inc(S[done], 1)

            for n in ("x", "cst", "cols"):
                dve.wait_ge(landed[n], 16 * NDMA[n])
            with dve.Fori(0, BATCH) as i:
                link.enter(i, 2 * 8)
                two = range(2)
                x_of = [lambda j, s=s: x_tok[:, tile_cols(i, s, j)] for s in two]
                xn_of = [lambda j, s=s: stage[:, s, j * P:(j + 1) * P] for s in two]
                n1_of = [lambda j, s=s: stage1[:, s, j * P:(j + 1) * P] for s in two]
                for s in two:
                    stats(s, x_of[s], "var_ready")
                for s in two:
                    normalise(s, x_of[s], xn_of[s], "sd_ready", 4 * i + s + 1, "xn_ready")
                for s in two:
                    dve.wait_ge(S["xn_ready"], 2 * i + s + 1)
                    stats(s, xn_of[s], "var_ready")
                for s in two:
                    normalise(s, xn_of[s], n1_of[s], "sd_ready", 4 * i + 2 + s + 1, "n1_ready")
                for s in two:
                    link.mark(v.tensor_copy(xn_tok[:, blk(i, s)], stage[:, s, :]))
                for s in two:
                    n = 2 * i + s
                    dve.wait_ge(S["nrm_ready"], n + 1)
                    link(v.tensor_scalar(nrm[:, s, :], nrm[:, s, :], 1e-12, None, ALU.max))
                    link(v.reciprocal(rn[:, s, :], nrm[:, s, :]))
                    for j in range(BT):
                        for h in range(2):
                            ins = v.tensor_scalar(qk[:, s, (2 * j + h) * D:(2 * j + h + 1) * D],
                                                  ps[:, 2 + j, h * D:(h + 1) * D],
                                                  rn[:, s, 2 * j + h:2 * j + h + 1], None, ALU.mult)
                    ins.then_inc(S["qk_scaled"], 1)
                    dve.wait_ge(S["qk_scaled"], FREE + n + 1)
                    src = qk[:, s, :].rearrange("p (j h d) -> p j h d", j=BT, h=2)
                    pairs = qk[:, s, :].rearrange("p (j h f e) -> p j h f e", j=BT, h=2, e=2)
                    turned = qk2[:, s, :].rearrange("p (j h f e) -> p j h f e", j=BT, h=2, e=2)
                    a = qk1[:, s, :].rearrange("p (j h d) -> p j h d", j=BT, h=2)
                    cos = cst[:, CST["cos"] + s * BLK:CST["cos"] + (s + 1) * BLK].rearrange("p (j d) -> p j d", j=BT)
                    sin = cst[:, CST["sin"] + s * BLK:CST["sin"] + (s + 1) * BLK].rearrange(
                        "p (j f e) -> p j f e", j=BT, e=2)
                    for h in range(2):
                        v.tensor_tensor(a[:, :, h, :], src[:, :, h, :], cos, ALU.mult)
                        v.tensor_tensor(turned[:, :, h, :, 0], pairs[:, :, h, :, 1], sin[:, :, :, 0], ALU.mult)
                        ins = v.tensor_tensor(turned[:, :, h, :, 1], pairs[:, :, h, :, 0], sin[:, :, :, 1], ALU.mult)
                    link(ins)
                    v.tensor_tensor(qk1[:, s, :], qk1[:, s, :], qk2[:, s, :], ALU.add).then_inc(S["rope_ready"], 1)
                link.leave(BATCH)

            def glu(n, fc, bank):
                dve.wait_ge(S["sil_done"], 4 * n + fc + 1)
                if fc == 0:
                    dve.wait_ge(S["h1_ready"], FREE + 4 * n)
                v.scalar_tensor_tensor(out=flat(hid0)[:, fc * BLK:(fc + 1) * BLK], in0=ps[:, bank, :],
                                       scalar=col("s2", fc), in1=sil[:, fc % 2, :], op0=ALU.mult,
                                       op1=ALU.mult).then_inc(S["glu_done"], 1)

            def add_mlp(n, at, bank):
                dve.wait_ge(S["y_ready"], FREE + n + 1)
                v.tensor_tensor(tiled(stage1[:, 0, :]), tiled(ps[:, bank, :]), rep("w3_s"),
                                ALU.mult).then_inc(S["y_done"], 1)
                dve.wait_ge(S["y_done"], FREE + n + 1)
                link(v.tensor_tensor(x_tok[:, at], x_tok[:, at], stage1[:, 0, :], ALU.add))

            dve.wait_ge(S["zp_kept"], FREE + BLOCKS)
            with dve.Fori(0, BATCH) as i:
                link.enter(i, 14)
                at = bass.ds(i * SEQ, SEQ)
                v.tensor_reduce(pm[:, 0:1], zp[:, at], AX.X, ALU.max, negate=True).then_inc(S["pm_ready"], 1)
                glu(i, 0, 2)
                glu(i, 1, 3)
                dve.wait_ge(S["logs_ready"], BATCH)
                link(v.scalar_tensor_tensor(out=zg[:, at], in0=zg[:, at], scalar=0.0, in1=tmp[:, at],
                                            op0=ALU.max, op1=ALU.add))
                ones = one_col[:, 0:1].to_broadcast([P, SEQ])
                link(v.tensor_tensor_scan(tmp[:, at], ones, zg[:, at], 0.0, ALU.mult, ALU.add))
                glu(i, 2, 2)
                glu(i, 3, 3)
                link(v.tensor_scalar(tmp[:, at], tmp[:, at], -1.0, -60.0, ALU.mult, ALU.max))
                v.tensor_scalar(tmp[:, at], tmp[:, at], 50.0, None, ALU.min).then_inc(S["decay_ready"], 1)
                link(v.scalar_tensor_tensor(out=zc[:, at], in0=zc[:, at], scalar=0.0, in1=tmp2[:, at],
                                            op0=ALU.max, op1=ALU.add))
                dve.wait_ge(S["p_exp"], i + 1)
                link(v.tensor_tensor(zp[:, at], zp[:, at], zc[:, at], ALU.mult))
                link(v.tensor_tensor_scan(tmp2[:, at], ones, zp[:, at], 0.0, ALU.mult, ALU.add))
                link.apart(v.tensor_scalar(tmp2[:, at], tmp2[:, at], 1e-8, None, ALU.add))
                link(v.reciprocal(tmp2[:, at], tmp2[:, at]))
                dve.wait_ge(S["decay_exp"], i + 1)
                link(v.tensor_tensor(tmp2[:, at], zg[:, at], tmp2[:, at], ALU.mult))
                link.apart(v.tensor_scalar(tmp[:, at], zg[:, at], 1e-8, None, ALU.add))
                link(v.reciprocal(tmp[:, at], tmp[:, at]))
                link(v.tensor_tensor(tmp[:, at], zp[:, at], tmp[:, at], ALU.mult))
                v.tensor_tensor(q_t[:, at], q_t[:, at], tmp2[:, at], ALU.mult)
                link(v.tensor_tensor(k_t[:, at], k_t[:, at], tmp[:, at], ALU.mult))
                add_mlp(i, bass.ds(i * BLK, BLK), 4)
                link.leave(BATCH)

            scale = 1.0 / math.sqrt(D)
            with dve.Fori(0, BATCH) as i:
                link.enter(i, 2 * KT + 3)
                all_of = bass.ds(i * SEQ, SEQ)
                v.tensor_copy(q_s, q_t[:, all_of])
                v.tensor_copy(k_s, k_t[:, all_of])
                v.tensor_copy(v_s, v_tok[:, all_of]).then_inc(S["batch_staged"], 1)

                def peak(qt):
                    dve.wait_ge(S["s_ready"], KT * i + qt + 1)
                    pair = ps[:, 0:2, :].rearrange("p a b -> p (a b)")
                    link(v.tensor_reduce(nm[:, qt % 2:qt % 2 + 1], pair[:, 0:(qt + 1) * P], AX.X, ALU.max,
                                         negate=True))
                    v.tensor_scalar(nm[:, 2 + qt % 2:3 + qt % 2], nm[:, qt % 2:qt % 2 + 1], scale, None,
                                    ALU.mult).then_inc(S["peak_ready"], 1)

                def divide(qt):
                    dve.wait_ge(S["exp_done"], FREE + KT * i + qt + 1)
                    link(v.reciprocal(sm[:, 2 + qt % 2:3 + qt % 2], sm[:, qt % 2:qt % 2 + 1]))
                    p = probs[:, qt % 2, 0:(qt + 1) * P]
                    v.tensor_scalar(p, p, sm[:, 2 + qt % 2:3 + qt % 2], None, ALU.mult).then_inc(S["p_ready"], 1)

                def keep(qt):
                    dve.wait_ge(S["av_ready"], FREE + KT * i + qt + 1)
                    v.tensor_copy(ao_t[:, qt * P:(qt + 1) * P],
                                  ps[:, (4, 7)[qt % 2], 0:P]).then_inc(S["av_kept"], 1)

                peak(0)
                for qt in range(KT):
                    divide(qt)
                    if qt + 1 < KT:
                        peak(qt + 1)
                    if qt:
                        keep(qt - 1)
                    for group in MLP_GROUPS[qt]:
                        if group[0] == "z":
                            glu(2 + i, group[1], 6)
                    if qt == KT - 1:
                        add_mlp(2 + i, bass.ds((2 + i) * BLK, BLK), 6)
                keep(KT - 1)
                for s in range(2):
                    at = blk(i, s)
                    dve.wait_ge(S["x2_ready"], 2 * i + s + 1)
                    v.tensor_tensor(xn_tok[:, at], xn_tok[:, at], ps[:, 2 + s, :], ALU.add).then_inc(S["x2_kept"], 1)
                    dve.wait_ge(S["x2_kept"], FREE + 2 * i + s + 1)
                    link(v.tensor_tensor(tiled(xn_tok[:, at]), tiled(xn_tok[:, at]), rep("out_b"), ALU.add))
                link.leave(BATCH)

            def norm_4(i):
                x2_of = [lambda j, s=s: xn_tok[:, tile_cols(i, s, j)] for s in range(2)]
                for s in range(2):
                    stats(s, x2_of[s], "m_var")
                if i:
                    dve.wait_ge(S["m_t_psum"], 2 * i)
                for s in range(2):
                    normalise(s, x2_of[s], lambda j: stage[:, s, j * P:(j + 1) * P], "m_sd", 2 * i + s + 1, "m_n")

            def add_4(i):
                for s in range(2):
                    n, at = 2 * i + s, blk(i, s)
                    dve.wait_ge(S["m2_ready"], FREE + n + 1)
                    v.tensor_tensor(x_tok[:, at], x_tok[:, at], ps[:, 5 + s, :], ALU.add).then_inc(S["m2_kept"], 1)
                    dve.wait_ge(S["m2_kept"], FREE + n + 1)
                    link(v.tensor_tensor(x_tok[:, at], x_tok[:, at], xn_tok[:, at], ALU.add))
                    link(v.tensor_tensor(tiled(x_tok[:, at]), tiled(x_tok[:, at]), rep("mlp_b2"), ALU.add))

            def norm_5(i):
                xl_of = [lambda j, s=s: x_tok[:, tile_cols(i, s, j)] for s in range(2)]
                for s in range(2):
                    stats(s, xl_of[s], "l_var")
                dve.wait_ge(S["l_t_psum"] if i else S["m_t_psum"], 2 if i else BLOCKS)
                for s in range(2):
                    normalise(s, xl_of[s], lambda j: stage[:, s, j * P:(j + 1) * P], "l_sd", 2 * i + s + 1, "l_n")
                for s in range(2):
                    n, at = 2 * i + s, blk(i, s)
                    dve.wait_ge(S["l_n"], n + 1)
                    ins = v.tensor_copy(x3_tok[:, at], stage[:, s, :])
                link(ins)

            def parts_5(i):
                for s in range(2):
                    n, at = 2 * i + s, blk(i, s)
                    for m, parts in enumerate((q_parts, k_parts)):
                        rest = stage1[:, m, :]
                        dve.wait_ge(S["hi_kept"], 2 * n + m + 1)
                        link(v.tensor_tensor(rest, ps[:, 1 + 2 * s + m, :], parts[:, 0, at], ALU.subtract))
                        link(v.tensor_copy(parts[:, 1, at], rest))
                        link(v.tensor_tensor(rest, rest, parts[:, 1, at], ALU.subtract))
                        v.tensor_copy(parts[:, 2, at], rest).then_inc(S["parts_kept"], 1)
                        dve.wait_ge(S["parts_kept"], FREE + 2 * n + m + 1)

            def convolution(i):
                dve.wait_ge(S["l_t_kept"], FREE + 2 * i + 2)
                x3 = lambda a, b: x3_t[:, i * SEQ + a:i * SEQ + b]
                y3 = lambda a, b: y_t[:, i * SEQ + a:i * SEQ + b]
                link(v.tensor_scalar(y3(0, SEQ), x3(0, SEQ), col("conv", 1), None, ALU.mult))
                link(v.scalar_tensor_tensor(out=y3(1, SEQ), in0=x3(0, SEQ - 1), scalar=col("conv", 0),
                                            in1=y3(1, SEQ), op0=ALU.mult, op1=ALU.add))
                v.scalar_tensor_tensor(out=y3(0, SEQ - 1), in0=x3(1, SEQ), scalar=col("conv", 2),
                                       in1=y3(0, SEQ - 1), op0=ALU.mult, op1=ALU.add).then_inc(S["conv_done"], 1)

            norm_4(0)
            norm_4(1)
            add_4(0)
            norm_5(0)
            add_4(1)
            norm_5(1)
            parts_5(0)
            parts_5(1)
            convolution(0)
            convolution(1)

            def split_maxima(a, neg, rest, part):
                link(v.tensor_copy(part(0), neg))
                link(v.tensor_tensor(rest, neg, part(0), ALU.subtract))
                link(v.tensor_copy(part(1), rest))
                link(v.tensor_tensor(rest, rest, part(1), ALU.subtract))
                v.tensor_copy(part(2), rest).then_inc(att[a]["m_split_ready"], 1)

            def early_maxima(a, i, s, k):
                A, b = att[a], EARLY_PAIRS[a][k % len(EARLY_PAIRS[a])]
                dve.wait_ge(A["early_scores_ready"], 17 * i + KT * s + k + 1)
                pair = ps[:, b:b + 2, :].rearrange("p a b -> p (a b)")
                maxima = neg_m[:, :, :].rearrange("p c k -> p (c k)")
                v.tensor_reduce(maxima[:, bass.ds(i * 16 + s * KT + k, 1)], pair, AX.X, ALU.max,
                                negate=True).then_inc(A["early_bank_free"], 1)
                if s and k == KT - 1:
                    dve.wait_ge(A["early_bank_free"], len(EARLY_PAIRS[a]) + 17 * i + 16)
                    parts = m_split[:, :, :, :].rearrange("p c a k -> p (c a k)")
                    split_maxima(a, maxima[:, bass.ds(i * 16, 16)], m_rest[:, 0, :],
                                 lambda n: parts[:, bass.ds(i * (16 * PARTS) + n * 16, 16)])
                    dve.wait_ge(A["early_scores_ready"], 17 * i + 17)
                    v.tensor_copy(m_t[:, :, :].rearrange("p c q -> p (c q)")[:, bass.ds(i * P, P)],
                                  ps[0:PARTS * 16, EARLY_PAIRS[a][0], 0:P // 2].bitcast(BF16)).then_inc(
                        A["early_bank_free"], 1)

            def heads_out(a, b):
                dve.wait_ge(att[a]["out_back"], 64 * (b + 1))
                if a or b:
                    dve.wait_ge(S["wo_ready"], 2 * (BATCH * a + b))
                for q in range(2):
                    at = slice(q * BLK, (q + 1) * BLK)
                    link(v.reciprocal(den[:, at], den[:, at]))
                    if a == 0:
                        v.tensor_tensor(ctx_t[:, at], o_in[:, at], den[:, at], ALU.mult).then_inc(S["ctx_ready"], 1)
                    else:
                        order = lambda x: x[:, at].rearrange("p (c t) -> p c t", c=HEADS // 2)
                        dst = ctx_t.rearrange("p (t c) -> p c t", c=HEADS)[:, q * 8:(q + 1) * 8, :]
                        v.tensor_tensor(dst, order(o_in), order(den), ALU.mult).then_inc(S["ctx_ready"], 1)

            def attention(a):
                A = att[a]
                items = Count()

                def peaks(i, c, k):
                    b = 2 * (items.n % 2)
                    if k == 0:
                        dve.wait_ge(A["m_split_ready"], SLOTS * i + c - 1)
                    dve.wait_ge(A["peak_scores_ready"], items.next())
                    pair = ps[:, b:b + 2, :].rearrange("p a b -> p (a b)")
                    v.tensor_reduce(neg_m[:, c % 2, k:k + 1], pair, AX.X, ALU.max,
                                    negate=True).then_inc(A["peak_bank_free"], 1)

                def turned(c):
                    b = 2 * (items.n % 2)
                    dve.wait_ge(A["peak_scores_ready"], items.next())
                    v.tensor_copy(m_t[:, c % 2, :], ps[0:PARTS * 16, b, 0:P // 2].bitcast(BF16)).then_inc(
                        A["peak_bank_free"], 1)

                def unit(i, c, left):
                    plan = peak_plan(left)
                    for s in range(1, KT + 1):
                        for ahead, k in plan[s]:
                            if k is None:
                                turned(c + ahead)
                            else:
                                peaks(i, c + ahead, k)

                peaks(0, 2, 0)
                peaks(0, 2, 1)
                with dve.Fori(0, UNITS // SLOTS - 1) as i:
                    items.enter(i, 17 * SLOTS)
                    for c in range(SLOTS):
                        unit(i, c, 3)
                    items.leave(UNITS // SLOTS - 1)
                for c in range(SLOTS):
                    if c == 2:
                        heads_out(a, 0)
                    unit(UNITS // SLOTS - 1, c, 3 - c)

            with dve.Fori(0, BATCH) as i:
                link.enter(i, 4)
                for s in range(2):
                    n, at = 2 * i + s, blk(i, s)
                    dve.wait_ge(S["pe_ready"], n + 1)
                    dve.wait_ge(S["conv_done"], BATCH)
                    dve.wait_ge(S["bv_ready"], FREE + 2 * n)
                    for c in range(2):
                        ins = v.tensor_tensor(xs[:, :, c, :], ps[:, 4, :].rearrange("p (h t) -> p h t", h=8),
                                              y_t[:, at].rearrange("p (h t) -> p h t", h=8), ALU.add)
                    ins.then_inc(S["xs_kept"], 1)
                    for k in range(KT):
                        early_maxima(0, i, s, k)
                link.leave(BATCH)

            attention(0)

            dve.wait_ge(S["bo_added"], BLOCKS)
            for b in range(BATCH):
                if b:
                    heads_out(0, b)
                o_of = [lambda j, s=s: x3_tok[:, (2 * b + s) * BLK + j * P:(2 * b + s) * BLK + (j + 1) * P] for s in range(2)]
                for s in range(2):
                    n = 2 * b + s
                    at = slice(n * BLK, (n + 1) * BLK)
                    dve.wait_ge(S["wo_ready"], n + 1)
                    v.tensor_tensor(x3_tok[:, at], x3_tok[:, at], ps[:, s, :], ALU.add).then_inc(S["wo_kept"], 1)
                for s in range(2):
                    dve.wait_ge(S["wo_kept"], 2 * b + s + 1)
                    stats(s, o_of[s], "o_var")
                if b:
                    dve.wait_ge(S["o_kept"], 2 * b)
                for s in range(2):
                    n = 2 * b + s
                    normalise(s, o_of[s], lambda j: stage1[:, s, j * P:(j + 1) * P], "o_sd", n + 1, None)
                    link(v.tensor_tensor(tiled(stage1[:, s, :]), tiled(stage1[:, s, :]), rep("l1g"), ALU.mult))
                    v.tensor_tensor(tiled(stage[:, s, :]), tiled(stage1[:, s, :]), rep("l1b"),
                                    ALU.add).then_inc(S["o_n"], 1)
            n_e = TILES * EXP
            T = lambda k: tk[:, k, :].rearrange("p (a e) -> p a e", e=EXP)
            one = lambda k: tk[:, k, 0:TILES]
            wide = lambda k: one(k).unsqueeze(2).to_broadcast([P, TILES, EXP])
            rank = cst[:, CST["rank"]:CST["rank"] + EXP].unsqueeze(1).to_broadcast([P, TILES, EXP])
            dve.wait_ge(S["route_ready"], BLOCKS)
            link(v.tensor_copy(tk[:, 0, :], ps[:, 3, 0:n_e]))
            link(v.tensor_reduce(one(1), T(0), AX.X, ALU.max))
            v.tensor_tensor(T(0), T(0), wide(1), ALU.subtract).then_inc(S["route_sum"], 1)
            dve.wait_ge(S["route_exp"], 1)
            link(v.tensor_reduce(one(1), T(2), AX.X, ALU.add))
            link(v.reciprocal(one(1), one(1)))
            link(v.tensor_tensor(T(2), T(2), wide(1), ALU.mult))
            for best, chosen in ((3, 4), (5, 6)):
                link(v.tensor_reduce(one(best), T(2), AX.X, ALU.max))
                link(v.tensor_tensor(T(7), T(2), wide(best), ALU.is_equal))
                link(v.tensor_tensor(T(7), T(7), rank, ALU.mult))
                link(v.tensor_reduce(one(8), T(7), AX.X, ALU.max))
                link(v.tensor_tensor(T(chosen), T(7), wide(8), ALU.is_equal))
                link(v.scalar_tensor_tensor(out=T(2), in0=T(chosen), scalar=-2.0, in1=T(2), op0=ALU.mult,
                                            op1=ALU.add))
            v.tensor_tensor(one(9), one(5), one(3), ALU.subtract).then_inc(S["route_sum"], 1)
            dve.wait_ge(S["route_exp"], 2)
            link(v.tensor_scalar(one(11), one(10), 1.0, None, ALU.add))
            link(v.reciprocal(one(11), one(11)))
            link(v.tensor_tensor(one(10), one(10), one(11), ALU.mult))
            link(v.tensor_tensor(T(4), T(4), wide(11), ALU.mult))
            link(v.tensor_tensor(T(6), T(6), wide(10), ALU.mult))
            v.tensor_tensor(gates[:, :, :], T(4), T(6), ALU.add).then_inc(S["gates_ready"], 1)

            dve.wait_ge(S["gates_ready"], 1)
            dve.wait_ge(S["o_kept"], BLOCKS)
            with dve.Fori(0, BATCH) as i:
                link.enter(i, 2 * 6 + 4)
                for s in range(2):
                    n, at = 2 * i + s, blk(i, s)
                    acc = stage1[:, s, :]
                    v.tensor_copy(gb[:, s, :], gates[:, :, :].rearrange("p a e -> p (a e)")[
                        :, bass.ds(i * (2 * BT * EXP) + s * BT * EXP, BT * EXP)]).then_inc(S["gb_ready"], 1)
                    dve.wait_ge(S["gt_psum"], 2 * n + 1)
                    v.tensor_copy(g_t[:, s * BLK:(s + 1) * BLK], ps[0:EXP, 6, :]).then_inc(S["gt_kept"], 1)
                    dve.wait_ge(S["gt_psum"], 2 * n + 2)
                    v.tensor_tensor(acc, x3_tok[:, at], ps[:, 7, :], ALU.add).then_inc(S["gt_kept"], 1)
                    dve.wait_ge(S["gt_kept"], 2 * n + 2)
                    for e in range(EXP):
                        if e:
                            early_maxima(1, i, s, e - 1)
                        dve.wait_ge(S["down_ready"], FREE + EXP * n + e + 1)
                        for j in range(BT):
                            a = acc[:, j * P:(j + 1) * P]
                            ins = v.scalar_tensor_tensor(out=a, in0=ps[:, 4 + e % 2, j * P:(j + 1) * P],
                                                         scalar=gb[:, s, j * EXP + e:j * EXP + e + 1], in1=a,
                                                         op0=ALU.mult, op1=ALU.add)
                        ins.then_inc(S["down_kept"], 1)
                        dve.wait_ge(S["down_kept"], FREE + EXP * n + e + 1)
                    early_maxima(1, i, s, EXP - 1)
                    own = lambda j: acc[:, j * P:(j + 1) * P]
                    stats(s, own, "f_var")
                    normalise(s, own, own, "f_sd", n + 1, None)
                    link(v.tensor_tensor(tiled(acc), tiled(acc), rep("l2g"), ALU.mult))
                    link(v.tensor_tensor(tiled(acc), tiled(acc), rep("l2b"), ALU.add))
                    link(v.tensor_tensor(x_tok[:, at], x_tok[:, at], acc, ALU.add))
                link.leave(BATCH)

            attention(1)
            for b in range(BATCH):
                if b:
                    heads_out(1, b)
                for s in range(2):
                    n = 2 * BATCH + 2 * b + s
                    at = slice((2 * b + s) * BLK, (2 * b + s + 1) * BLK)
                    dve.wait_ge(S["wo_ready"], n + 1)
                    v.tensor_tensor(x_tok[:, at], x_tok[:, at], ps[:, n % 2, :], ALU.add).then_inc(S["wo_kept"], 1)

        @block.tensor
        def _(pe):
            mm = nc.tensor.matmul

            def turn(bank, src, width=BT):
                for j in range(width):
                    ins = nc.tensor.transpose(ps[:, bank, j * P:(j + 1) * P], src(j), ident)
                return ins

            for n in ("cst", "w0"):
                pe.wait_ge(landed[n], 16 * NDMA[n])
            with pe.Fori(0, BATCH) as i:
                n = 2 * i
                for s, (bank, kept) in enumerate(((0, "k_kept"), (1, "q_kept"))):
                    pe.wait_ge(S["xn_ready"], n + s + 1)
                    pe.wait_ge(S[kept], FREE + n)
                    turn(bank, lambda j: stage[:, s, j * P:(j + 1) * P]).then_inc(S["xn_t_psum"], 1)
                for s, (bank, kept) in enumerate(((6, "k_kept"), (7, "q_kept"))):
                    pe.wait_ge(S["n1_ready"], n + s + 1)
                    pe.wait_ge(S[kept], FREE + n)
                    turn(bank, lambda j: stage1[:, s, j * P:(j + 1) * P]).then_inc(S["n1_t_psum"], 1)
                for s in range(2):
                    pe.wait_ge(S["n1_t_kept"], n + s + 1)
                    pe.wait_ge(S["qk_scaled"], FREE + n + s)
                    xt = stage_t[:, s, :]
                    for j in range(BT):
                        ins = mm(ps[:, 2 + j, 0:3 * D], xt[:, j * P:(j + 1) * P], w0[:, 0:3 * D], start=True, stop=True)
                    ins.then_inc(S["qkv_ready"], 1)
                    if s == 0:
                        pe.wait_ge(S["xn_t_kept"], n + 2)
                    else:
                        pe.wait_ge(S["zg_kept"], FREE + n + 1)
                    mm(ps[:, 0, :], w0[:, W0["gate"]:W0["gate"] + P], xt, start=True, stop=True)
                    mm(ps[:, 6 + s, :], w0[:, W0["p"]:W0["p"] + P], xt, start=True, stop=True).then_inc(S["gp_ready"], 1)
                    if s == 1:
                        pe.wait_ge(S["zp_kept"], FREE + n + 1)
                    mm(ps[:, (1, 6)[s], :], w0[:, W0["clock"]:W0["clock"] + P], xt, start=True, stop=True).then_inc(
                        S["clock_ready"], 1)
                for s in range(2):
                    pe.wait_ge(S["rope_ready"], n + s + 1)
                    pe.wait_ge(S["zc_kept"], FREE + n + s + 1)
                    pe.wait_ge(S["zg_kept"], FREE + n + 2)
                    pe.wait_ge(S["zp_kept"], FREE + n + s + 1)
                    turn((1, 7)[s], lambda j: qk1[:, s, 2 * j * D:(2 * j + 1) * D])
                    turn((0, 6)[s], lambda j: qk1[:, s, (2 * j + 1) * D:(2 * j + 2) * D]).then_inc(S["rope_t_psum"], 1)

            pe.wait_ge(landed["wf"], 16 * NDMA["wf"])
            for n in ("k_kept", "q_kept", "qk_scaled", "zg_kept", "zp_kept"):
                pe.wait_ge(S[n], FREE + BLOCKS)
            pe.wait_ge(S["xn_t_kept"], BLOCKS)
            h0, h1, h2 = flat(hid0), flat(hid1), flat(hid2)

            def z(n, at, fc, banks):
                for b, w in zip(banks, ("w1", "w2")):
                    ins = mm(ps[:, b, :], wf[:, WF[w] + fc * P:WF[w] + (fc + 1) * P], xn_t[:, at], start=True, stop=True)
                ins.then_inc(S["z_ready"], 1)

            def hidden(w, src, oc, bank, ready):
                for fc in range(FC):
                    at = WF[w] + fc * HID + oc * P
                    ins = mm(ps[:, bank, :], wf[:, at:at + P], src[:, fc * BLK:(fc + 1) * BLK],
                             start=fc == 0, stop=fc == FC - 1)
                ins.then_inc(S[ready], 1)

            def last(j, bank):
                for fc in range(FC):
                    ins = mm(ps[:, bank, j * P:(j + 1) * P], h2[:, fc * BLK + j * P:fc * BLK + (j + 1) * P],
                             wf[:, WF["w3"] + fc * D:WF["w3"] + (fc + 1) * D], start=fc == 0, stop=fc == FC - 1)
                return ins

            with pe.Fori(0, BATCH) as i:
                for fc in range(FC):
                    pe.wait_ge(S["glu_done"], FREE + 4 * i + (fc - 1 if fc >= 2 else 0))
                    z(i, bass.ds(i * BLK, BLK), fc, (fc % 2, 2 + fc % 2))
                pe.wait_ge(S["glu_done"], FREE + 4 * i + 4)
                pe.wait_ge(S["y_done"], FREE + i)
                for oc in range(FC):
                    pe.wait_ge(S["h1_done"], FREE + 4 * i + (oc - 1 if oc >= 2 else 0))
                    hidden("h1", h0, oc, 4 + oc % 2, "h1_ready")
                pe.wait_ge(S["h1_done"], FREE + 4 * i + 4)
                for oc in range(FC):
                    pe.wait_ge(S["h2_done"], FREE + 4 * i + (oc - 1 if oc >= 2 else 0))
                    hidden("h2", h1, oc, 6 + oc % 2, "h2_ready")
                pe.wait_ge(S["h2_done"], FREE + 4 * i + 4)
                for j in range(BT):
                    ins = last(j, 4)
                ins.then_inc(S["y_ready"], 1)

            pe.wait_ge(S["y_done"], FREE + 2)
            with pe.Fori(0, BATCH) as i:
                n = 2 + i

                def mlp_group(kind, k):
                    if kind == "z":
                        if k == 0:
                            pe.wait_ge(S["y_done"], FREE + n)
                        pe.wait_ge(S["glu_done"], FREE + 4 * n + k)
                        z(n, bass.ds((2 + i) * BLK, BLK), k, (5, 6))
                    elif kind == "h1":
                        pe.wait_ge(S["glu_done"], FREE + 4 * n + 4)
                        if k >= 2:
                            pe.wait_ge(S["h1_done"], FREE + 4 * n + k - 1)
                        hidden("h1", h0, k, 5 + k % 2, "h1_ready")
                    elif kind == "h2":
                        pe.wait_ge(S["h1_done"], FREE + 4 * n + 4)
                        if k >= 2:
                            pe.wait_ge(S["h2_done"], FREE + 4 * n + k - 1)
                        hidden("h2", h1, k, 5 + k % 2, "h2_ready")
                    else:
                        pe.wait_ge(S["h2_done"], FREE + 4 * n + 4)
                        last(2 * k, 6)
                        ins = last(2 * k + 1, 6)
                        if k == 1:
                            ins.then_inc(S["y_ready"], 1)

                pe.wait_ge(S["batch_staged"], i + 1)

                def scores(qt):
                    pe.wait_ge(S["exp_done"], FREE + KT * i + qt)
                    width = (qt + 1) * P
                    q = q_s[:, qt * P:(qt + 1) * P]
                    for c in range((width + 511) // 512):
                        w = min(512, width - 512 * c)
                        mm(ps[:, c, 0:w], q, k_s[:, 512 * c:512 * c + w], start=True, stop=c != qt // 4)
                    m = (qt % 4) * P
                    mm(ps[:, qt // 4, m:m + P], ident, cst[:, CST["mask"]:CST["mask"] + P], start=False,
                       stop=True).then_inc(S["s_ready"], 1)

                scores(0)
                for qt in range(KT):
                    if qt + 1 < KT:
                        scores(qt + 1)
                    groups = MLP_GROUPS[qt]
                    if groups:
                        mlp_group(*groups[0])
                    pe.wait_ge(S["p_ready"], KT * i + qt + 1)
                    pe.wait_ge(S["p_t_kept"], FREE + KT * i + qt)
                    if qt == 0:
                        pe.wait_ge(S["x2_kept"], FREE + 2 * i)
                    for kt in range(qt + 1):
                        ins = nc.tensor.transpose(ps[:, 2 + kt // 4, (kt % 4) * P:(kt % 4 + 1) * P],
                                                  probs[:, qt % 2, kt * P:(kt + 1) * P], ident)
                    ins.then_inc(S["p_t_psum"], 1)
                    if groups:
                        mlp_group(*groups[1])
                    pe.wait_ge(S["p_t_kept"], FREE + KT * i + qt + 1)
                    if qt >= 2:
                        pe.wait_ge(S["av_kept"], FREE + KT * i + qt - 1)
                    for kt in range(qt + 1):
                        ins = mm(ps[:, (4, 7)[qt % 2], 0:P], v_s[:, kt * P:(kt + 1) * P],
                                 probs_t[:, kt * P:(kt + 1) * P], start=kt == 0, stop=kt == qt)
                    ins.then_inc(S["av_ready"], 1)
                pe.wait_ge(S["av_kept"], FREE + KT * i + KT)
                for s in range(2):
                    for j in range(BT):
                        t0 = (s * BT + j) * P
                        ins = mm(ps[:, 2 + s, j * P:(j + 1) * P], ao_t[:, t0:t0 + P], w0[:, W0["out"]:W0["out"] + D],
                                 start=True, stop=True)
                    ins.then_inc(S["x2_ready"], 1)

            pe.wait_ge(S["y_done"], FREE + BLOCKS)
            pe.wait_ge(S["exp_done"], FREE + KT * BATCH)
            pe.wait_ge(S["p_t_kept"], FREE + KT * BATCH)
            def turn_4(i):
                for s, bank in enumerate((0, 7)):
                    pe.wait_ge(S["m_n"], 2 * i + s + 1)
                    pe.wait_ge(S["m_t_kept"], FREE + 2 * i)
                    turn(bank, lambda j: stage[:, s, j * P:(j + 1) * P]).then_inc(S["m_t_psum"], 1)

            def first_4(i):
                for s in range(2):
                    pe.wait_ge(S["m_t_kept"], FREE + 2 * i + s + 1)
                    for fc in range(FC):
                        if i or s:
                            pe.wait_ge(S["m1_done"], FREE + 8 * i + 4 * s - 4 + fc + 1)
                        at = W0["m1"] + fc * P
                        mm(ps[:, 1 + fc, :], w0[:, at:at + P], stage_t[:, s, :], start=True, stop=True).then_inc(
                            S["m1_ready"], 1)

            def second_4(i):
                for s in range(2):
                    pe.wait_ge(S["m1_done"], FREE + 8 * i + 4 * s + 4)
                    pe.wait_ge(S["m2_kept"], FREE + 2 * i)
                    for j in range(BT):
                        for fc in range(FC):
                            at = W0["m2"] + fc * D
                            ins = mm(ps[:, 5 + s, j * P:(j + 1) * P],
                                     (h0, h1)[s][:, fc * BLK + j * P:fc * BLK + (j + 1) * P],
                                     w0[:, at:at + D], start=fc == 0, stop=fc == FC - 1)
                    ins.then_inc(S["m2_ready"], 1)

            turn_4(0)
            first_4(0)
            turn_4(1)
            second_4(0)
            first_4(1)
            second_4(1)

            pe.wait_ge(landed["w1"], 16 * NDMA["w1"])
            pe.wait_ge(S["m_t_kept"], FREE + BLOCKS)
            pe.wait_ge(S["m1_done"], FREE + FC * BLOCKS)
            wcol = lambda name, n=P: w1[:, W1[name]:W1[name] + n]
            for i in range(BATCH):
                for s, bank in enumerate((0, 7)):
                    pe.wait_ge(S["l_n"], 2 * i + s + 1)
                    pe.wait_ge(S["l_t_kept"], FREE + 2 * i)
                    turn(bank, lambda j: stage[:, s, j * P:(j + 1) * P]).then_inc(S["l_t_psum"], 1)
                for s in range(2):
                    n = 2 * i + s
                    pe.wait_ge(S["l_t_kept"], FREE + n + 1)
                    pe.wait_ge(S["parts_kept"], FREE + 4 * i)
                    for m, w in enumerate(("q", "k")):
                        mm(ps[:, 1 + 2 * s + m, :], wcol(w), stage_t[:, s, :], start=True, stop=True).then_inc(
                            S["lq_ready"], 1)
                    pe.wait_ge(S["lv_kept"], FREE + 2 * i)
                    pe.wait_ge(S["m2_kept"], FREE + BLOCKS)
                    for j in range(BT):
                        ins = mm(ps[:, 5 + s, j * P:(j + 1) * P], stage_t[:, s, j * P:(j + 1) * P], wcol("v"),
                                 start=True, stop=True)
                    ins.then_inc(S["lv_ready"], 1)
            pe.wait_ge(S["l_t_kept"], FREE + BLOCKS)
            pe.wait_ge(S["parts_kept"], FREE + 2 * BLOCKS)
            pe.wait_ge(S["lv_kept"], FREE + BLOCKS)

            def early_peaks(a, i, s, k):
                b = EARLY_PAIRS[a][k % len(EARLY_PAIRS[a])]
                first = len(EARLY_PAIRS[a]) if s == k == 0 else 1
                pe.wait_ge(att[a]["early_bank_free"], 17 * i + KT * s + k + first)
                for f in range(2):
                    ins = mm(ps[:, b + f, :], slots[:, bass.ds(i * (4 * SEQ) + s * SEQ + k * P, P)],
                             slots[:, bass.ds(i * (4 * SEQ) + (2 + s) * SEQ + f * 512, 512)], start=True, stop=True)
                ins.then_inc(att[a]["early_scores_ready"], 1)
                if s and k == KT - 1:
                    wait_apart(pe, att[a]["m_split_ready"], i + 1)
                    wait_apart(pe, att[a]["early_bank_free"], 17 * i + 17)
                    nc.tensor.transpose(ps[0:PARTS * 16, EARLY_PAIRS[a][0], 0:P // 2].bitcast(BF16),
                                        m_split[:, 0].rearrange("p a k -> p (a k)"), ident_b[:, :]).then_inc(
                        att[a]["early_scores_ready"], 1)

            with pe.Fori(0, BATCH) as i:
                for s in range(2):
                    n = 2 * i + s
                    pe.wait_ge(S["conv_done"], i + 1)
                    pe.wait_ge(S["bv_kept"], FREE + 2 * n)
                    mm(ps[:, 4, :], wcol("pe"), y_t[:, blk(i, s)], start=True, stop=True).then_inc(S["pe_ready"], 1)
                    for m in range(2):
                        pe.wait_ge(att[0]["qk_loaded"][m], 64)
                        early_peaks(0, i, s, m)
                    pe.wait_ge(S["xs_kept"], FREE + n + 1)
                    for m in range(2):
                        pe.wait_ge(S["bq_kept"], FREE + 2 * n)
                        at = W1["qkv"] + m * P
                        mm(ps[:, 5 + m, :].rearrange("p (h t) -> p h t", h=8), w1[:, at:at + P], xs[:, :, 0, :],
                           start=True, stop=True).then_inc(S["bq_ready"], 1)
                        early_peaks(0, i, s, 2 + m)
                    for g in range(2):
                        pe.wait_ge(S["bv_kept"], FREE + 2 * n)
                        at = W1["qkv"] + 2 * P
                        for h in range(4):
                            ins = mm(ps[:, (7, 4)[g], h * D:(h + 1) * D], xs[:, 4 * g + h, :, :].rearrange(
                                "p c t -> p (c t)"), w1[:, at:at + P], start=True, stop=True)
                        ins.then_inc(S["bv_ready"], 1)
                        early_peaks(0, i, s, 4 + g)
                    for k in range(6, KT):
                        early_peaks(0, i, s, k)

            def attention(a):
                A = att[a]
                items = Count()

                def peaks(i, c, k):
                    sl = slot[c % SLOTS]
                    if k == 0:
                        use = i + c // SLOTS
                        pe.wait_ge(A["qk_loaded"][c % SLOTS], 64 * (use + 1))
                        pe.wait_ge(A["rows_zeroed"], SLOTS * i + c + 1)
                    b = 2 * (items.n % 2)
                    pe.wait_ge(A["peak_bank_free"], items.next())
                    h, qt = k // KT, k % KT
                    for f in range(2):
                        at = h * SEQ + f * 512
                        ins = mm(ps[:, b + f, :], sl[:, 0, h * SEQ + qt * P:h * SEQ + (qt + 1) * P],
                                 sl[:, 1, at:at + 512], start=True, stop=True)
                    ins.then_inc(A["peak_scores_ready"], 1)

                def turn_maxima(i, c):
                    b = 2 * (items.n % 2)
                    wait_apart(pe, A["m_split_ready"], SLOTS * i + c + 1)
                    wait_apart(pe, A["peak_bank_free"], items.next())
                    nc.tensor.transpose(ps[0:PARTS * 16, b, 0:P // 2].bitcast(BF16),
                                        m_split[:, c % 2].rearrange("p a k -> p (a k)"), ident_b[:, :]).then_inc(
                        A["peak_scores_ready"], 1)

                def scores(i, c, s, tiles):
                    sl = slot[c % SLOTS]
                    if s == 0 and 0 in tiles:
                        pe.wait_ge(A["m_loaded"][c % SLOTS], 16 * (i + c // SLOTS + 1))
                    for q in tiles:
                        tile = 32 * c + 4 * s + q
                        pe.wait_ge(A["probs_done"], 32 * SLOTS * i + tile + 1 - (2 if q % 2 else 4) + CREDIT)
                        h, half = q // 2, q % 2
                        mm(ps[:, SCORE_BANK[q], :], sl[:, 1, h * SEQ + s * P:h * SEQ + (s + 1) * P],
                           sl[:, 0, h * SEQ + half * 512:h * SEQ + (half + 1) * 512],
                           start=True, stop=True).then_inc(A["scores_ready"], 1)

                def sums(i, c, s):
                    if s == 0:
                        pe.wait_ge(A["va_ready"], SLOTS * i + c + 1)
                        pe.wait_ge(A["out_kept"], FREE + SLOTS * i + c)
                    pe.wait_ge(A["probs_done"], 32 * SLOTS * i + 32 * c + 4 * s + 4 + CREDIT)
                    vals = values(a, c)
                    for q in range(4):
                        h = q // 2
                        ins = mm(ps[32 * q:32 * q + 32, 7, :], vals[:, (h * KT + s) * 32:(h * KT + s + 1) * 32],
                                 probabilities(a, s)[:, q * 512:(q + 1) * 512], start=s == 0, stop=s == KT - 1)
                    ins.then_inc(A["av_steps"], 1)

                def unit(i, c, left, beside=None):
                    plan = peak_plan(left)
                    for s in range(1, KT + 1):
                        def step(tiles):
                            if s < KT:
                                scores(i, c, s, tiles)
                            elif left:
                                scores(i, c + 1, 0, tiles)

                        def for_maxima(items_):
                            for ahead, k in items_:
                                if k is None:
                                    turn_maxima(i, c + ahead)
                                else:
                                    peaks(i, c + ahead, k)

                        step((0, 1))
                        for_maxima(plan[s][:1])
                        step((2,))
                        if a == 0 and left >= 2:
                            for_maxima(plan[s][1:2])
                            step((3,))
                            sums(i, c, s - 1)
                            for_maxima(plan[s][2:])
                        else:
                            sums(i, c, s - 1)
                            step((3,))
                            for_maxima(plan[s][1:])
                        if beside:
                            beside(s)

                peaks(0, 2, 0)
                peaks(0, 2, 1)
                scores(0, 0, 0, range(4))
                with pe.Fori(0, UNITS // SLOTS - 1) as i:
                    items.enter(i, 17 * SLOTS)
                    for c in range(SLOTS):
                        unit(i, c, 3)
                    items.leave(UNITS // SLOTS - 1)
                for c in range(SLOTS):
                    unit(UNITS // SLOTS - 1, c, 3 - c, lambda s: batch_0[a](c, s, items.seen() + PCREDIT))

            def project(a, b, w):
                for s in range(2):
                    pe.wait_ge(S["ctx_ready"], 2 * (BATCH * a + b) + (2 if a else s + 1))
                    if a == 0 and b:
                        pe.wait_ge(S["o_t_kept"], s + 1)
                    n = 2 * (BATCH * a + b) + s
                    if n >= 2:
                        pe.wait_ge(S["wo_kept"], n - 1)
                    for j in range(BT):
                        t0 = (s * BT + j) * P
                        ins = mm(ps[:, n % 2, j * P:(j + 1) * P], ctx_t[:, t0:t0 + P], wcol(w), start=True, stop=True)
                    ins.then_inc(S["wo_ready"], 1)

            pe.wait_ge(att[0]["early_bank_free"], len(EARLY_PAIRS[0]) + 2 * 17)
            pe.wait_ge(S["bq_kept"], FREE + 2 * BLOCKS)
            pe.wait_ge(S["bv_kept"], FREE + 2 * BLOCKS)
            def route(n):
                s = n % 2
                pe.wait_ge(S["o_n"], n + 1)
                turn(s, lambda j: stage[:, s, j * P:(j + 1) * P]).then_inc(S["o_t_psum"], 1)
                pe.wait_ge(S["o_t_kept"], n + 1)
                for j in range(BT):
                    at = (n * BT + j) * EXP
                    ins = mm(ps[:, 3, at:at + EXP], stage_t[:, s, j * P:(j + 1) * P], wcol("r", EXP),
                             start=True, stop=True)
                ins.then_inc(S["route_ready"], 1)

            def batch_0_of_first(c, s, last_peak):
                if (c, s) == (2, 4):
                    pe.wait_ge(att[0]["peak_bank_free"], last_peak)
                    project(0, 0, "o")
                if c == 3 and s in (2, 4):
                    route((s - 2) // 2)

            def batch_0_of_second(c, s, last_peak):
                if (c, s) == (2, 6):
                    pe.wait_ge(att[1]["peak_bank_free"], last_peak)
                    project(1, 0, "ao")

            batch_0 = (batch_0_of_first, batch_0_of_second)
            attention(0)

            project(0, 1, "o")
            route(2)
            route(3)

            for n in ("we1", "we2"):
                pe.wait_ge(landed[n], 16 * NDMA[n])
            pe.wait_ge(att[1]["rows_zeroed"], SLOTS)
            for n in range(2):
                pe.wait_ge(att[1]["qk_loaded"][n], 64)
            pe.wait_ge(S["o_t_kept"], BLOCKS)
            pe.wait_ge(S["wo_kept"], BLOCKS)
            pe.wait_ge(S["route_sum"], 1)
            with pe.Fori(0, BATCH) as i:
                for s in range(2):
                    n = 2 * i + s

                    def up(e):
                        for fc in range(FC):
                            pe.wait_ge(S["up_done"], FREE + 4 * EXP * n + (4 * e - 3 + fc if e else 0))
                            at = (e * FC + fc) * P
                            mm(ps[:, fc, :], we1[:, at:at + P], o1_t[:, blk(i, s)], start=True, stop=True).then_inc(
                                S["up_ready"], 1)

                    def down(e):
                        pe.wait_ge(S["up_done"], FREE + 4 * (EXP * n + e + 1))
                        pe.wait_ge(S["down_kept"], FREE + EXP * n + (e - 1 if e >= 2 else 0))
                        h = flat((hid0, hid1)[e % 2])
                        for j in range(BT):
                            for fc in range(FC):
                                at = (e * FC + fc) * D
                                ins = mm(ps[:, 4 + e % 2, j * P:(j + 1) * P], h[:, fc * BLK + j * P:fc * BLK + (j + 1) * P],
                                         we2[:, at:at + D], start=fc == 0, stop=fc == FC - 1)
                        ins.then_inc(S["down_ready"], 1)

                    up(0)
                    for e in range(EXP):
                        if e + 1 < EXP:
                            up(e + 1)
                        if e == 0:
                            pe.wait_ge(S["gb_ready"], n + 1)
                            pe.wait_ge(att[1]["early_bank_free"], 17 * i + KT * s + 1)
                            for j in range(BT):
                                ins = nc.tensor.transpose(ps[0:EXP, 6, j * P:(j + 1) * P],
                                                          gb[:, s, j * EXP:(j + 1) * EXP], ident)
                            ins.then_inc(S["gt_psum"], 1)
                        else:
                            if e == 1:
                                pe.wait_ge(S["gt_kept"], 2 * n + 2)
                            early_peaks(1, i, s, e - 1)
                        down(e)
                        if e == 0:
                            pe.wait_ge(S["gt_kept"], 2 * n + 1)
                            for j in range(BT):
                                t0 = s * BLK + j * P
                                ins = mm(ps[:, 7, j * P:(j + 1) * P], g_t[:, t0:t0 + P], be2[:, :], start=True, stop=True)
                            ins.then_inc(S["gt_psum"], 1)
                    early_peaks(1, i, s, EXP - 1)

            pe.wait_ge(S["up_done"], FREE + 4 * EXP * BLOCKS)
            pe.wait_ge(S["down_kept"], FREE + EXP * BLOCKS)
            pe.wait_ge(att[1]["early_bank_free"], len(EARLY_PAIRS[1]) + 2 * 17)
            attention(1)
            project(1, 1, "ao")

        @block.scalar
        def _(act):
            link = Chain(act, act_seq, wait_apart)
            fn = nc.scalar.activation

            def root(s, ready, n, eps, done):
                act.wait_ge(S[ready], n)
                fn(sd[:, s, :], mv[:, s, :, 1], ACT.Sqrt, bias=eps).then_inc(S[done], 1)

            act.wait_ge(landed["cols"], 16 * NDMA["cols"])
            act.wait_ge(S["consts"], 4)
            with act.Fori(0, BATCH) as i:
                link.enter(i, 4)
                n = 2 * i
                for s in range(2):
                    root(s, "var_ready", 4 * i + s + 1, eps0, "sd_ready")
                for s in range(2):
                    act.wait_ge(S["xn_t_psum"], n + s + 1)
                    fn(xn_t[:, blk(i, s)], ps[:, s, :], ACT.Copy).then_inc(S["xn_t_kept"], 1)
                    root(s, "var_ready", 4 * i + 2 + s + 1, eps0, "sd_ready")
                for s in range(2):
                    act.wait_ge(S["n1_t_psum"], n + s + 1)
                    fn(stage_t[:, s, :], ps[:, 6 + s, :], ACT.Identity, scale=col("g1"), bias=col("b1")).then_inc(
                        S["n1_t_kept"], 1)
                for s in range(2):
                    at = blk(i, s)
                    act.wait_ge(S["qkv_ready"], n + s + 1)
                    for j in range(BT):
                        for h in range(2):
                            m = 2 * j + h
                            ins = fn(qk2[:, s, m * D:(m + 1) * D], ps[:, 2 + j, h * D:(h + 1) * D], ACT.Square,
                                     accum_out=ss[:, s, m:m + 1])
                    link(ins)
                    fn(tiled(v_tok[:, at]), ps[:, 2:2 + BT, 2 * D:3 * D], ACT.Copy)
                    fn(nrm[:, s, :], ss[:, s, :], ACT.Sqrt).then_inc(S["nrm_ready"], 1)
                    act.wait_ge(S["gp_ready"], n + s + 1)
                    fn(zg[:, at], ps[:, 0, :], ACT.Identity, bias=col("gate_b")).then_inc(S["zg_kept"], 1)
                    fn(zp[:, at], ps[:, 6 + s, :], ACT.Identity, bias=col("p_b")).then_inc(S["zp_kept"], 1)
                    act.wait_ge(S["clock_ready"], n + s + 1)
                    fn(zc[:, at], ps[:, (1, 6)[s], :], ACT.Identity, bias=col("clock_b")).then_inc(S["zc_kept"], 1)
                at = bass.ds(i * SEQ, SEQ)
                act.wait_ge(S["zc_kept"], FREE + n + 2)
                fn(tmp[:, at], zg[:, at], ACT.Abs)
                link.apart(fn(tmp2[:, at], zc[:, at], ACT.Abs))
                fn(tmp[:, at], tmp[:, at], ACT.Exp, scale=-1.0)
                link.apart(fn(tmp2[:, at], tmp2[:, at], ACT.Exp, scale=-1.0))
                fn(tmp[:, at], tmp[:, at], ACT.Ln, bias=1.0)
                fn(tmp2[:, at], tmp2[:, at], ACT.Ln, bias=1.0).then_inc(S["logs_ready"], 1)
                for s in range(2):
                    at = blk(i, s)
                    act.wait_ge(S["rope_t_psum"], n + s + 1)
                    fn(q_t[:, at], ps[:, (1, 7)[s], :], ACT.Copy).then_inc(S["q_kept"], 1)
                    fn(k_t[:, at], ps[:, (0, 6)[s], :], ACT.Copy).then_inc(S["k_kept"], 1)
                link.leave(BATCH)

            for n in ("zg_kept", "zp_kept", "zc_kept"):
                act.wait_ge(S[n], FREE + BLOCKS)

            def silu(n, fc, bank):
                act.wait_ge(S["z_ready"], 4 * n + fc + 1)
                act.wait_ge(S["glu_done"], FREE + 4 * n + (fc - 1 if fc >= 2 else 0))
                fn(sil[:, fc % 2, :], ps[:, bank, :], ACT.Silu, scale=col("s1", fc)).then_inc(S["sil_done"], 1)

            def gelu(layer, n, oc, bank):
                ready, done, free, dst, scales = (
                    (), ("h1_ready", "h1_done", "h2_ready", hid1, "t1"), ("h2_ready", "h2_done", "y_ready", hid2, "t2"))[layer]
                if oc == 0:
                    act.wait_ge(S[free], FREE + (4, 1)[layer - 1] * n)
                act.wait_ge(S[ready], FREE + 4 * n + oc + 1)
                fn(flat(dst)[:, oc * BLK:(oc + 1) * BLK], ps[:, bank, :], ACT.Gelu,
                   scale=col(scales, oc)).then_inc(S[done], 1)

            with act.Fori(0, BATCH) as i:
                at = bass.ds(i * SEQ, SEQ)
                for fc in range(FC):
                    silu(i, fc, fc % 2)
                wait_apart(act, S["pm_ready"], i + 1)
                fn(zp[:, at], zp[:, at], ACT.Exp, bias=pm[:, 0:1]).then_inc(S["p_exp"], 1)
                wait_apart(act, S["decay_ready"], i + 1)
                fn(zg[:, at], tmp[:, at], ACT.Exp).then_inc(S["decay_exp"], 1)
                for oc in range(FC):
                    gelu(1, i, oc, 4 + oc % 2)
                for oc in range(FC):
                    gelu(2, i, oc, 6 + oc % 2)

            with act.Fori(0, BATCH) as i:
                def exps(qt):
                    act.wait_ge(S["peak_ready"], KT * i + qt + 1)
                    act.wait_ge(S["p_t_psum"], FREE + KT * i + (qt - 1 if qt >= 2 else 0))
                    pair = ps[:, 0:2, :].rearrange("p a b -> p (a b)")
                    fn(probs[:, qt % 2, 0:(qt + 1) * P], pair[:, 0:(qt + 1) * P], ACT.Exp, scale=1.0 / math.sqrt(D),
                       bias=nm[:, 2 + qt % 2:3 + qt % 2], accum_out=sm[:, qt % 2:qt % 2 + 1]).then_inc(S["exp_done"], 1)

                def mlp_group(kind, k):
                    if kind == "z":
                        silu(2 + i, k, 5)
                    elif kind == "h1":
                        gelu(1, 2 + i, k, 5 + k % 2)
                    elif kind == "h2":
                        gelu(2, 2 + i, k, 5 + k % 2)

                exps(0)
                for qt in range(KT):
                    if qt + 1 < KT:
                        exps(qt + 1)
                    groups = list(MLP_GROUPS[qt])
                    if groups and groups[0][0] == "z":
                        mlp_group(*groups.pop(0))
                    act.wait_ge(S["p_t_psum"], FREE + KT * i + qt + 1)
                    act.wait_ge(S["av_ready"], FREE + KT * i + qt)
                    fn(probs_t[:, 0:(qt + 1) * P], ps[:, 2:4, :].rearrange("p a b -> p (a b)")[:, 0:(qt + 1) * P],
                       ACT.Copy).then_inc(S["p_t_kept"], 1)
                    for group in groups:
                        mlp_group(*group)

            def roots_4(i):
                for s in range(2):
                    root(s, "m_var", 2 * i + s + 1, eps0, "m_sd")

            def turned_4(i):
                if i:
                    act.wait_ge(S["m1_ready"], 8 * i)
                for s, bank in enumerate((0, 7)):
                    act.wait_ge(S["m_t_psum"], 2 * i + s + 1)
                    fn(stage_t[:, s, :], ps[:, bank, :], ACT.Identity, scale=col("g2"), bias=col("b2")).then_inc(
                        S["m_t_kept"], 1)

            def gelu_4(i):
                for s in range(2):
                    n = 2 * i + s
                    act.wait_ge(S["m2_ready"], FREE + 2 * i)
                    for fc in range(FC):
                        act.wait_ge(S["m1_ready"], 4 * n + fc + 1)
                        fn(flat((hid0, hid1)[s])[:, fc * BLK:(fc + 1) * BLK], ps[:, 1 + fc, :], ACT.Gelu,
                           bias=col("mb1", fc)).then_inc(S["m1_done"], 1)

            roots_4(0)
            turned_4(0)
            roots_4(1)
            gelu_4(0)
            turned_4(1)
            gelu_4(1)

            for i in range(BATCH):
                for s in range(2):
                    root(s, "l_var", 2 * i + s + 1, eps0, "l_sd")
                for s, bank in enumerate((0, 7)):
                    at = blk(i, s)
                    act.wait_ge(S["l_t_psum"], 2 * i + s + 1)
                    fn(stage_t[:, s, :], ps[:, bank, :], ACT.Copy)
                    fn(x3_t[:, at], ps[:, bank, :], ACT.Copy).then_inc(S["l_t_kept"], 1)
                for s in range(2):
                    n, at = 2 * i + s, blk(i, s)
                    for m, parts in enumerate((q_parts, k_parts)):
                        act.wait_ge(S["lq_ready"], 2 * n + m + 1)
                        fn(parts[:, 0, at], ps[:, 1 + 2 * s + m, :], ACT.Copy).then_inc(S["hi_kept"], 1)
                for s in range(2):
                    act.wait_ge(S["lv_ready"], 2 * i + s + 1)
                    for j in range(BT):
                        dst = v1[:, bass.ds(i * SEQ, SEQ)].rearrange("p (u h k j) -> p u h k j", u=8, h=2, k=KT)
                        ins = fn(dst[:, :, :, 4 * s + j, :], ps[:, 5 + s, j * P:(j + 1) * P].rearrange(
                            "p (u h j) -> p u h j", u=8, h=2), ACT.Copy)
                    ins.then_inc(S["lv_kept"], 1)
            with act.Fori(0, BATCH) as i:
                for s in range(2):
                    n, at = 2 * i + s, blk(i, s)
                    for m, dst in enumerate((q_b, k_b)):
                        act.wait_ge(S["bq_ready"], 2 * n + m + 1)
                        fn(dst[:, at], ps[:, 5 + m, :], ACT.Copy).then_inc(S["bq_kept"], 1)
                    for g in range(2):
                        act.wait_ge(S["bv_ready"], FREE + 2 * n + g + 1)
                        for c in range(2):
                            rng = slice(64 * c, 64 * c + 64)
                            vals = ps[rng, (7, 4)[g], :].rearrange("p (a c j) -> p a c j", c=2, j=HD)[:, :, c, :]
                            dst = v2[rng, bass.ds(i * 1024 + s * 512 + g * 256, 256)]
                            ins = fn(dst.rearrange("p (a j) -> p a j", j=HD), vals, ACT.Copy)
                        ins.then_inc(S["bv_kept"], 1)

            def attention(a):
                A = att[a]

                def exps(i, c, s):
                    act.wait_ge(A["av_steps"], SLOTS * KT * i + KT * c + s - 1 + PCREDIT)
                    for q in range(4):
                        act.wait_ge(A["scores_ready"], 32 * SLOTS * i + 32 * c + 4 * s + q + 1)
                        fn(probabilities(a, s)[:, q * 512:(q + 1) * 512], ps[:, SCORE_BANK[q], :], ACT.Exp,
                           scale=HEAD_SCALE[a]).then_inc(A["probs_done"], 1)

                def keep(i, c):
                    act.wait_ge(A["av_steps"], SLOTS * KT * i + KT * (c + 1) + PCREDIT)
                    act.wait_ge(A["out_stored"][c % 2], FREE + 16 * (SLOTS // 2 * i + c // 2))
                    fn(o_st[c % 2], ps[:, 7, :], ACT.Copy).then_inc(A["out_kept"], 1)

                def unit(i, c, left, beside=None):
                    for s in range(1, KT):
                        exps(i, c, s)
                        if beside:
                            beside(s)
                    if left:
                        exps(i, c + 1, 0)
                    keep(i, c)

                exps(0, 0, 0)
                with act.Fori(0, UNITS // SLOTS - 1) as i:
                    for c in range(SLOTS):
                        unit(i, c, 3)
                for c in range(SLOTS):
                    unit(UNITS // SLOTS - 1, c, 3 - c, (lambda s: batch_0(c, s)) if a == 0 else None)

            def roots(b):
                for s in range(2):
                    root(s, "o_var", 2 * b + s + 1, eps1, "o_sd")

            def keep_out1(n):
                s, at = n % 2, slice(n * BLK, (n + 1) * BLK)
                act.wait_ge(S["o_t_psum"], n + 1)
                fn(stage_t[:, s, :], ps[:, s, :], ACT.Copy)
                fn(o1_t[:, at], ps[:, s, :], ACT.Copy).then_inc(S["o_t_kept"], 1)
                fn(x3_tok[:, at], stage[:, s, :], ACT.Copy).then_inc(S["o_kept"], 1)

            def batch_0(c, s):
                if (c, s) == (2, 7):
                    roots(0)
                if c == 3 and s in (2, 4):
                    keep_out1((s - 2) // 2)

            act.wait_ge(parts_stored, 16 * PARTS_STORES)
            attention(0)

            roots(1)
            keep_out1(2)
            keep_out1(3)
            act.wait_ge(S["route_sum"], 1)
            fn(tk[:, 2, :], tk[:, 0, :], ACT.Exp).then_inc(S["route_exp"], 1)
            act.wait_ge(S["route_sum"], 2)
            fn(tk[:, 10, 0:TILES], tk[:, 9, 0:TILES], ACT.Exp).then_inc(S["route_exp"], 1)

            with act.Fori(0, BATCH) as i:
                for s in range(2):
                    n = 2 * i + s
                    for e in range(EXP):
                        act.wait_ge(S["down_ready"], FREE + EXP * n + (e - 1 if e >= 2 else 0))
                        for fc in range(FC):
                            act.wait_ge(S["up_ready"], 4 * EXP * n + 4 * e + fc + 1)
                            fn(flat((hid0, hid1)[e % 2])[:, fc * BLK:(fc + 1) * BLK], ps[:, fc, :], ACT.Gelu,
                               bias=col("be1", e * FC + fc)).then_inc(S["up_done"], 1)
                    root(s, "f_var", n + 1, eps1, "f_sd")

            attention(1)

        @block.gpsimd
        def _(pool):
            g = nc.gpsimd
            link = Chain(pool, pool_seq, wait_apart)
            for semaphore in free_at_start:
                pool.sem_inc(semaphore, FREE)
            for a in range(2):
                pool.sem_inc(att[a]["early_bank_free"], len(EARLY_PAIRS[a]))
            g.memset(eps0, EPS0).then_inc(S["consts"], 1)
            g.memset(eps1, EPS1).then_inc(S["consts"], 1)
            g.memset(one_col[:, :], 1.0).then_inc(S["consts"], 1)
            pool.wait_ge(landed["cst"], 16 * NDMA["cst"])
            g.tensor_copy(ident_b[:, :], ident).then_inc(S["consts"], 1)

            def attention(a):
                A = att[a]
                pool.sem_inc(A["probs_done"], CREDIT)
                pool.sem_inc(A["peak_bank_free"], PCREDIT)
                pool.sem_inc(A["av_steps"], PCREDIT)
                for n in range(SLOTS):
                    if a == 0 and n == SLOTS - 1:
                        pool.wait_ge(parts_stored, 16 * PARTS_STORES)
                    link(g.memset(r[5 + n], 0.0))
                    g.memset(slot[n][MROW:MROW + PARTS, 1, :], 1.0).then_inc(A["slots_ready"], 1)
                    pool.wait_ge(A["slots_ready"], n + 1)
                for n in range(2):
                    link.mark(g.memset(values(a, n), 1.0))
                link.wait()

                def values_of(i, c):
                    src = v1 if a == 0 else v2
                    g.tensor_copy(values(a, c).rearrange("p (m w) -> p m w", w=32)[:, :, 0:HD],
                                  src[:, bass.ds(i * (SLOTS * P) + c * P, P)].rearrange("p (m j) -> p m j", j=HD)).then_inc(
                        A["va_ready"], 1)

                def unit(i, c, left):
                    if left:
                        pool.wait_ge(A["rows_zeroed"], SLOTS * i + c + SLOTS if left > 3 else UNITS)
                        pool.wait_ge(A["av_steps"], SLOTS * KT * i + KT * c + PCREDIT)
                        values_of(i, c + 1)
                    if left >= 2:
                        pool.wait_ge(A["va_ready"], SLOTS * i + c + 2)
                        wait_apart(pool, A["peak_bank_free"], 17 * SLOTS * i + 17 * c + 17 + PCREDIT)
                        neg, rest, parts = neg_m[:, c % 2, :], m_rest[:, c % 2, :], m_split[:, c % 2]
                        link.apart(g.tensor_copy(parts[:, 0, :], neg))
                        link.apart(g.tensor_tensor(rest, neg, parts[:, 0, :], ALU.subtract))
                        link.apart(g.tensor_copy(parts[:, 1, :], rest))
                        link.apart(g.tensor_tensor(rest, rest, parts[:, 1, :], ALU.subtract))
                        g.tensor_copy(parts[:, 2, :], rest).then_inc(A["m_split_ready"], 1)
                        wait_apart(pool, A["m_split_ready"], SLOTS * i + c + 3)
                    if left > 3:
                        wait_apart(pool, A["av_steps"], SLOTS * KT * i + KT * (c + 1) + PCREDIT)
                        g.memset(slot[c][MROW:MROW + PARTS, 0, :], 0.0).then_inc(A["rows_zeroed"], 1)

                pool.sem_inc(A["rows_zeroed"], SLOTS)
                if a == 0:
                    pool.wait_ge(S["lv_kept"], FREE + BLOCKS)
                values_of(0, 0)
                if a == 0:
                    pool.wait_ge(S["conv_done"], BATCH)
                    for n in range(BLOCKS):
                        x3 = tiled(x3_tok[:, n * BLK:(n + 1) * BLK])
                        g.tensor_tensor(x3, x3, rep("bo"), ALU.add).then_inc(S["bo_added"], 1)
                    pool.wait_ge(S["bo_added"], BLOCKS)
                with pool.Fori(0, UNITS // SLOTS - 1) as i:
                    link.enter(i, 4 * SLOTS)
                    for c in range(SLOTS):
                        unit(i, c, 4)
                    link.leave(UNITS // SLOTS - 1)
                for c in range(SLOTS):
                    unit(UNITS // SLOTS - 1, c, 3 - c)

            pool.wait_ge(S["x2_kept"], FREE + BLOCKS)
            pool.wait_ge(S["y_done"], FREE + BLOCKS)
            attention(0)
            pool.wait_ge(att[0]["av_steps"], KT * UNITS + PCREDIT)
            attention(1)

        @block.sync
        def _(sp):
            def load(name, dst, src):
                sp.dma_start(dst, src).then_inc(landed[name], 16)

            xv = t["L0_attn_x"].rearrange("b (n p) d -> p (b n) d", p=P)
            xt3 = x_tok.rearrange("p (n d) -> p n d", d=D)
            for n in range(BLOCKS):
                load("x", xt3[:, n * BT:(n + 1) * BT, :], xv[:, n * BT:(n + 1) * BT, :])
            load("cst", cst[:, :], t["consts"])
            load("cols", cols[:, :], t["cols"])
            for m, name in enumerate(("L0_attn_out_b", "L0_attn_mlp_b2", "L0_ffn_w3_s", "L1_ffn_bo", "L1_ffn_ln1_g",
                                      "L1_ffn_ln1_b", "L1_ffn_ln2_g", "L1_ffn_ln2_b")):
                load("cols", rows[:, m, :], t[name].partition_broadcast(P))
            load("w0", w0[:, :], t["w0"])
            load("wf", wf[:, :], t["wf"])
            load("w1", w1[:, :], t["w1"])
            load("we1", we1[:, :].rearrange("p (e f) -> p e f", e=EXP), t["L1_ffn_We1"].rearrange("e d f -> d e f"))
            load("we2", we2[:, :].rearrange("p (e c d) -> p e c d", e=EXP, c=FC),
                 t["L1_ffn_We2"].rearrange("e (c p) d -> p e c d", p=P))
            load("we2", be2[:, :], t["L1_ffn_be2"])

            with sp.Fori(0, BATCH) as i:
                for s in range(2):
                    for m, (dram, parts, runs) in enumerate(((qs_dram, q_parts, Q_RUNS), (ks_dram, k_parts, K_RUNS))):
                        sp.wait_ge(S["parts_kept"], FREE + 2 * (2 * i + s) + m + 1)
                        for first, count, part in runs:
                            dst = dram[first:first + count, bass.ds(i, 1), :, s * BLK:(s + 1) * BLK].rearrange(
                                "m b p t -> (b p) m t")
                            if m == 0:
                                src = parts[:, part, blk(i, s)].unsqueeze(1).to_broadcast([P, count, BLK])
                            else:
                                src = parts[:, part:part + count, blk(i, s)]
                            sp.dma_start(dst, src).then_inc(parts_stored, 16)

            def attention(a):
                A = att[a]
                if a == 0:
                    heads = [d.rearrange("m b (u h j) t -> (b u) h m j t", u=8, h=2) for d in (qs_dram, ks_dram)]
                    n_rows = N_PRODUCTS * HD
                else:
                    heads = [d.rearrange("(c j) (u h t) -> u h j c t", c=HEADS, h=2, t=64) for d in (qb_dram, kb_dram)]
                    n_rows = HD

                def fetch(i, c):
                    for m in range(2):
                        for h in range(2):
                            sp.dma_start(slot[c % SLOTS][0:n_rows, m, h * SEQ:(h + 1) * SEQ],
                                         one_of(heads[m], i * SLOTS + c)[h]).then_inc(A["qk_loaded"][c % SLOTS], 16)

                def bring_back(b):
                    src = o_dram[a][b * 8:(b + 1) * 8].rearrange("u (h q m) t -> u h m q t", h=2, q=2)
                    for q in range(2):
                        at = slice(512 * q, 512 * (q + 1))
                        sp.dma_start(o_in[:, at], src[:, :, 0:HD, q]).then_inc(A["out_back"], 16)
                        sp.dma_start(den[:, at], src[:, :, HD:2 * HD, q]).then_inc(A["out_back"], 16)

                items = Count()

                def maxima(c, early=False):
                    if early:
                        sp.wait_ge(A["early_bank_free"], len(EARLY_PAIRS[a]) + 17)
                    else:
                        sp.wait_ge(A["peak_bank_free"], items.seen() + PCREDIT)
                    sp.dma_start(slot[c % SLOTS][MROW:MROW + PARTS, 0, :].rearrange("p (k q) -> p k q", q=P),
                                 m_t[:, c % 2, :]).then_inc(A["m_loaded"][c % SLOTS], 16)

                def unit(i, c, left):
                    for s in range(1, KT + 1):
                        for ahead, k in peak_plan(min(left, 3))[s]:
                            items.next()
                            if k is None:
                                maxima(c + ahead)
                    sp.wait_ge(A["av_steps"], SLOTS * KT * i + KT * (c + 1) + PCREDIT)
                    if left > 3:
                        fetch(i, c + SLOTS)
                    if left == 3:
                        for n in range(2):
                            sp.wait_ge(A["out_stored"][n], FREE + 16 * (UNITS - SLOTS) // 2)
                        bring_back(0)
                    sp.wait_ge(A["out_kept"], FREE + SLOTS * i + c + 1)
                    sp.dma_start(one_of(o_dram[a], i * SLOTS + c), o_st[c % 2]).then_inc(A["out_stored"][c % 2], 16)

                for c in range(SLOTS):
                    sp.wait_ge(A["slots_ready"], c + 1)
                    fetch(0, c)
                maxima(0, early=True)
                if a == 0:
                    sp.wait_ge(S["bq_kept"], FREE + 2 * BLOCKS)
                    sp.dma_start(qb_dram, q_b).then_inc(b_stored, 16)
                    sp.dma_start(kb_dram, k_b).then_inc(b_stored, 16)
                items.next()
                items.next()
                with sp.Fori(0, UNITS // SLOTS - 1) as i:
                    items.enter(i, 17 * SLOTS)
                    for c in range(SLOTS):
                        unit(i, c, 4)
                    items.leave(UNITS // SLOTS - 1)
                for c in range(SLOTS):
                    unit(UNITS // SLOTS - 1, c, 3 - c)
                for n in range(2):
                    sp.wait_ge(A["out_stored"][n], FREE + 16 * UNITS // 2)
                sp.wait_ge(S["ctx_ready"], 2 * (BATCH * a + 1))
                bring_back(1)

            sp.wait_ge(parts_stored, 16 * PARTS_STORES)
            attention(0)
            sp.wait_ge(b_stored, 32)
            attention(1)
            ov = out.rearrange("b (n p) d -> p (b n) d", p=P)
            for n in range(BLOCKS):
                sp.wait_ge(S["wo_kept"], 2 * BATCH + n + 1)
                sp.dma_start(ov[:, n * BT:(n + 1) * BT, :], xt3[:, n * BT:(n + 1) * BT, :]).then_inc(stored, 16)
            sp.wait_ge(stored, 16 * BLOCKS)


def laid_out(x):
    n = lambda k: np.asarray(x[k])
    chunks = lambda w: w.reshape(-1, P, w.shape[1]).transpose(1, 0, 2).reshape(P, -1)
    vec = lambda v: v.reshape(-1, P).T
    clock = np.repeat(n("L0_attn_clock_W"), P, axis=1)
    w0 = [n("L0_attn_Wq"), n("L0_attn_Wk"), n("L0_attn_Wv"), n("L0_attn_gate_W"), n("L0_attn_p_W"), clock,
          n("L0_attn_out_W"), n("L0_attn_mlp_W1"), chunks(n("L0_attn_mlp_W2"))]
    wf = [n("L0_ffn_w1_w").T, n("L0_ffn_w2_w").T, chunks(n("L0_ffn_h1_w").T), chunks(n("L0_ffn_h2_w").T),
          chunks(n("L0_ffn_w3_w").T)]
    w1 = [n("L1_attn_pe_w").T, n("L1_attn_qkv_w").T, n("L1_attn_out_w").T, n("L1_ffn_Wq"), n("L1_ffn_Wk"),
          n("L1_ffn_Wv"), n("L1_ffn_Wo"), n("L1_ffn_Wr")]
    cols = [vec(n("L0_attn_gate_b")), vec(n("L0_attn_p_b")), np.repeat(n("L0_attn_clock_b"), P)[:, None]]
    cols += [vec(n("L0_attn_" + k)) for k in ("ln1_g", "ln1_b", "ln2_g", "ln2_b", "mlp_b1")]
    cols += [vec(n("L0_ffn_" + k)) for k in ("w1_s", "w2_s", "h1_s", "h2_s")]
    cols += [vec(n("L1_ffn_be1")), n("L1_attn_conv_w")[:, 0, :, 1]]
    return {"w0": np.concatenate(w0, 1), "wf": np.concatenate(wf, 1), "w1": np.concatenate(w1, 1),
            "cols": np.concatenate(cols, 1)}


def constants():
    half = D // 2
    freqs = np.exp(-np.arange(half, dtype=np.float32) * np.float32(math.log(10000.0) / half)).astype(np.float32)
    th = np.arange(SEQ, dtype=np.float32)[:, None] * freqs[None, :]
    c = np.repeat(np.cos(th.astype(np.float64)), 2, axis=1)
    s = np.stack([-np.sin(th.astype(np.float64)), np.sin(th.astype(np.float64))], -1).reshape(SEQ, D)
    tiles = lambda a: a.reshape(KT, P, D).transpose(1, 0, 2).reshape(P, KT * D)
    above = np.triu(np.ones((P, P)), 1) * -3e38
    rank = np.broadcast_to(np.arange(EXP, 0, -1), (P, EXP))
    return np.concatenate([np.eye(P), above, tiles(c), tiles(s), rank], 1).astype(np.float32)


_PLAIN = ["L0_attn_x", "L0_attn_out_b", "L0_attn_mlp_b2", "L0_ffn_w3_s", "L1_ffn_bo", "L1_ffn_ln1_g", "L1_ffn_ln1_b",
          "L1_ffn_ln2_g", "L1_ffn_ln2_b", "L1_ffn_We1", "L1_ffn_We2", "L1_ffn_be2"]


def kernel(**inputs):
    import concourse.bacc as bacc
    from concourse.bass_utils import run_bass_kernel_spmd

    arrays = {k: np.ascontiguousarray(inputs[k]) for k in _PLAIN}
    arrays |= {k: np.ascontiguousarray(a) for k, a in laid_out(inputs).items()}
    arrays["consts"] = constants()
    nc = bacc.Bacc("TRN2", target_bir_lowering=False, num_devices=1)
    t = {k: nc.dram_tensor("in_" + k, a.shape, mybir.dt.from_np(a.dtype), kind="ExternalInput").ap()
         for k, a in arrays.items()}
    out = nc.dram_tensor("out", (BATCH, SEQ, D), F32, kind="ExternalOutput").ap()
    build(nc, t, out)
    r = run_bass_kernel_spmd(nc, [{"in_" + k: a for k, a in arrays.items()}], core_ids=[0])
    return r.results[0]["out"]
```
